# Optimizing a Trainium2 kernel written in Bass

```python
import numpy as np
import jax
import jax.numpy as jnp

def _softmax(x, axis=-1):
    return jax.nn.softmax(x, axis=axis)

def _gelu(x):
    return jax.nn.gelu(x, approximate=True)

def _silu(x):
    return jax.nn.silu(x)

def _sigmoid(x):
    return jax.nn.sigmoid(x)

def _layernorm(x, axis=-1, eps=1e-05):
    m = jnp.mean(x, axis=axis, keepdims=True)
    v = jnp.var(x, axis=axis, keepdims=True)
    return (x - m) / jnp.sqrt(v + eps)

def _scatter_add(tgt, idx, src, axis=0):
    return tgt.at[idx].add(src)

def _segment_sum(src, seg, n):
    return jax.ops.segment_sum(src, seg, n)
kernel_name = 'mk_vit_tower_cls_d1_tok_img2048_r4_b93541'

def setup_inputs(seed: int=0):
    np.random.seed(seed)
    _w = jnp.asarray

    def _rec_inputs():
        import jax
        import jax.numpy as jnp
        _rk = jax.random.key(seed)
        x = -0.0043416 + 0.998921 * jax.random.normal(jax.random.fold_in(_rk, 1), (64, 64, 64, 2), jnp.float32)
        cls_tok = 0.02 * jax.random.normal(jax.random.fold_in(_rk, 5), (1, 1, 512), jnp.float32)
        return (x, cls_tok)
    x, cls_tok = _rec_inputs()

    def _L0_tok_setup():
        import jax, jax.numpy as jnp
        import numpy as np
        H, N, CH = (64, 64, 1)

        def _r2c(x):
            return x[..., 0] + 1j * x[..., 1]

        def _bilinear(dt, Ac, Bc):
            n = Ac.shape[-1]
            I = jnp.eye(n, dtype=Ac.dtype)
            half = (dt.astype(Ac.real.dtype) / 2)[:, None]
            A_back = I - half * Ac
            A_fwd = I + half * Ac
            dB = dt.astype(Ac.dtype) * jnp.linalg.solve(A_back, Bc[..., None])[..., 0]
            dA = jnp.linalg.solve(A_back, A_fwd)
            return (dA, dB)

        def _krylov(L, dA, dB):
            x = dB[..., None]
            A_ = dA
            while x.shape[-1] < L:
                x = jnp.concatenate([x, jnp.einsum('hnm,hml->hnl', A_, x)], axis=-1)
                A_ = A_ @ A_
            return x[..., :L]
        key = jax.random.key(seed)
        kA, kB, kC, kdt = jax.random.split(key, 4)
        M = jax.random.normal(kA, (H, N, N, 2), dtype=jnp.float32) / np.float32(np.sqrt(N))
        Mc = _r2c(M)
        Ac = 0.5 * (Mc - jnp.conjugate(jnp.swapaxes(Mc, -1, -2))) - 0.5 * jnp.eye(N, dtype=Mc.dtype)
        A = jnp.stack([Ac.real, Ac.imag], axis=-1)
        B = jax.random.normal(kB, (H, N, 2), dtype=jnp.float32)
        C = jax.random.normal(kC, (CH, H, N, 2), dtype=jnp.float32)
        log_dt = jax.random.uniform(kdt, (H, 1), dtype=jnp.float32, minval=np.float32(np.log(0.001)), maxval=np.float32(np.log(0.1)))
        return {'A': A, 'B': B, 'C': C, 'log_dt': log_dt, 'L': 512}
    _L0_tok_all = _L0_tok_setup()
    _L0_tok_in = {k: v for k, v in _L0_tok_all.items() if k in ('A', 'B', 'log_dt')}
    del _L0_tok_all

    def _L0_attn_setup():
        import jax, jax.numpy as jnp
        import numpy as np
        B, S, D, H = (4, 512, 512, 16)
        DK = D // H
        key = jax.random.key(seed)
        ks = jax.random.split(key, 9)

        def xavier(k, shape):
            fan_in, fan_out = (shape[1], shape[0])
            limit = (6.0 / (fan_in + fan_out)) ** 0.5
            return jax.random.uniform(k, shape, jnp.float32, -limit, limit)
        return {'x': jax.random.normal(ks[0], (B, S, D), jnp.float32), 'Wq': xavier(ks[1], (D, D)), 'bq': jnp.zeros((D,), jnp.float32), 'Wk': xavier(ks[2], (D, D)), 'bk': jnp.zeros((D,), jnp.float32), 'Wv': xavier(ks[3], (D, D)), 'bv': jnp.zeros((D,), jnp.float32), 'Wo': xavier(ks[4], (D, D)), 'bo': jnp.zeros((D,), jnp.float32)}
    _L0_attn_all = _L0_attn_setup()
    _L0_attn_in = {k: v for k, v in _L0_attn_all.items() if k in ('Wq', 'bq', 'Wk', 'bk', 'Wv', 'bv', 'Wo', 'bo')}
    del _L0_attn_all

    def _L0_ffn_setup():
        import jax, jax.numpy as jnp
        import numpy as np
        B, S, H, F, E, R, K = (2, 256, 512, 1792, 8, 32, 2)

        def _gather_slot(a_all, e):
            return jnp.take_along_axis(a_all, e[:, None, None], axis=1)[:, 0]
        key = jax.random.key(seed)
        ks = jax.random.split(key, 12)
        sc = 0.02
        n = lambda k, shape, s: jax.random.normal(k, shape, dtype=jnp.float32) * s
        return {'hidden_states': n(ks[0], (B, S, H), 1.0), 'Wg': n(ks[1], (E, H), sc), 'W1': n(ks[2], (F, H), sc), 'W2': n(ks[3], (H, F), sc), 'W3': n(ks[4], (F, H), sc), 'A1': n(ks[5], (E, R, H), sc), 'B1': n(ks[6], (E, F, R), sc), 'A2': n(ks[7], (E, R, F), sc), 'B2': n(ks[8], (E, H, R), sc), 'A3': n(ks[9], (E, R, H), sc), 'B3': n(ks[10], (E, F, R), sc)}
    _L0_ffn_all = _L0_ffn_setup()
    _L0_ffn_in = {k: v for k, v in _L0_ffn_all.items() if k in ('Wg', 'W1', 'W2', 'W3', 'A1', 'B1', 'A2', 'B2', 'A3', 'B3')}
    del _L0_ffn_all
    return {'x': x, 'cls_tok': cls_tok, 'L0_tok_A': _L0_tok_in['A'], 'L0_tok_B': _L0_tok_in['B'], 'L0_tok_log_dt': _L0_tok_in['log_dt'], 'L0_attn_Wq': _L0_attn_in['Wq'], 'L0_attn_bq': _L0_attn_in['bq'], 'L0_attn_Wk': _L0_attn_in['Wk'], 'L0_attn_bk': _L0_attn_in['bk'], 'L0_attn_Wv': _L0_attn_in['Wv'], 'L0_attn_bv': _L0_attn_in['bv'], 'L0_attn_Wo': _L0_attn_in['Wo'], 'L0_attn_bo': _L0_attn_in['bo'], 'L0_ffn_Wg': _L0_ffn_in['Wg'], 'L0_ffn_W1': _L0_ffn_in['W1'], 'L0_ffn_W2': _L0_ffn_in['W2'], 'L0_ffn_W3': _L0_ffn_in['W3'], 'L0_ffn_A1': _L0_ffn_in['A1'], 'L0_ffn_B1': _L0_ffn_in['B1'], 'L0_ffn_A2': _L0_ffn_in['A2'], 'L0_ffn_B2': _L0_ffn_in['B2'], 'L0_ffn_A3': _L0_ffn_in['A3'], 'L0_ffn_B3': _L0_ffn_in['B3']}

def reference(x, cls_tok, L0_tok_A, L0_tok_B, L0_tok_log_dt, L0_attn_Wq, L0_attn_bq, L0_attn_Wk, L0_attn_bk, L0_attn_Wv, L0_attn_bv, L0_attn_Wo, L0_attn_bo, L0_ffn_Wg, L0_ffn_W1, L0_ffn_W2, L0_ffn_W3, L0_ffn_A1, L0_ffn_B1, L0_ffn_A2, L0_ffn_B2, L0_ffn_A3, L0_ffn_B3):
    import jax
    import jax.numpy as jnp

    def _L0_tok_ref(A, B, C, log_dt, L):
        import jax, jax.numpy as jnp
        import numpy as np
        H, N, CH = (64, 64, 1)

        def _r2c(x):
            return x[..., 0] + 1j * x[..., 1]

        def _bilinear(dt, Ac, Bc):
            n = Ac.shape[-1]
            I = jnp.eye(n, dtype=Ac.dtype)
            half = (dt.astype(Ac.real.dtype) / 2)[:, None]
            A_back = I - half * Ac
            A_fwd = I + half * Ac
            dB = dt.astype(Ac.dtype) * jnp.linalg.solve(A_back, Bc[..., None])[..., 0]
            dA = jnp.linalg.solve(A_back, A_fwd)
            return (dA, dB)

        def _krylov(L, dA, dB):
            x = dB[..., None]
            A_ = dA
            while x.shape[-1] < L:
                x = jnp.concatenate([x, jnp.einsum('hnm,hml->hnl', A_, x)], axis=-1)
                A_ = A_ @ A_
            return x[..., :L]
        Ac, Bc, Cc = (_r2c(A), _r2c(B), _r2c(C))
        dt = jnp.exp(log_dt)
        dA, dB = _bilinear(dt, Ac, Bc)
        x = _krylov(L, dA, dB)
        k = jnp.einsum('chn,hnl->chl', Cc, x).real.astype(jnp.float32)
        return k

    def _L0_attn_ref(x, Wq, bq, Wk, bk, Wv, bv, Wo, bo):
        import jax, jax.numpy as jnp
        import numpy as np
        B, S, D, H = (4, 512, 512, 16)
        DK = D // H
        b, s, d = x.shape
        scale = DK ** 0.5

        def proj(W, bias):
            y = jnp.einsum('bsd,ed->bse', x, W) + bias
            return y.reshape(b, s, H, DK).transpose(0, 2, 1, 3)
        Q, K, V = (proj(Wq, bq), proj(Wk, bk), proj(Wv, bv))
        scores = jnp.einsum('bhqd,bhkd->bhqk', Q, K) / scale
        causal = jnp.triu(jnp.ones((s, s), dtype=bool), k=1)
        scores = jnp.where(causal[None, None], -jnp.inf, scores)
        attn = jax.nn.softmax(scores, axis=-1)
        ctx = jnp.einsum('bhqk,bhkd->bhqd', attn, V)
        ctx = ctx.transpose(0, 2, 1, 3).reshape(b, s, d)
        out = jnp.einsum('bsd,ed->bse', ctx, Wo) + bo
        return out

    def _L0_ffn_ref(hidden_states, Wg, W1, W2, W3, A1, B1, A2, B2, A3, B3):
        import jax, jax.numpy as jnp
        import numpy as np
        B, S, H, F, E, R, K = (2, 256, 512, 1792, 8, 32, 2)

        def _gather_slot(a_all, e):
            return jnp.take_along_axis(a_all, e[:, None, None], axis=1)[:, 0]
        b, s, h = hidden_states.shape
        x = hidden_states.reshape(-1, h)
        nE = Wg.shape[0]
        logits = x @ Wg.T
        probs = jax.nn.softmax(logits.astype(jnp.float32), axis=-1)
        rw, sel = jax.lax.top_k(probs, K)
        rw = (rw / rw.sum(axis=-1, keepdims=True)).astype(x.dtype)
        base1 = x @ W1.T
        base3 = x @ W3.T
        a1_all = jnp.einsum('th,erh->ter', x, A1)
        a3_all = jnp.einsum('th,erh->ter', x, A3)
        out = jnp.zeros_like(x)
        for k in range(K):
            e = sel[:, k]
            mask = jax.nn.one_hot(e, nE, dtype=x.dtype)
            a1 = _gather_slot(a1_all, e)
            a3 = _gather_slot(a3_all, e)
            lora1 = jnp.einsum('ter,efr->tf', mask[:, :, None] * a1[:, None, :], B1)
            lora3 = jnp.einsum('ter,efr->tf', mask[:, :, None] * a3[:, None, :], B3)
            x1 = base1 + lora1
            x3 = base3 + lora3
            x2 = jax.nn.silu(x1) * x3
            down = x2 @ W2.T
            a2_all = jnp.einsum('tf,erf->ter', x2, A2)
            a2 = _gather_slot(a2_all, e)
            lora2 = jnp.einsum('ter,ehr->th', mask[:, :, None] * a2[:, None, :], B2)
            out = out + (down + lora2) * rw[:, k:k + 1]
        return out.reshape(b, s, h)
    h = _L0_tok_ref(L0_tok_A, L0_tok_B, x, L0_tok_log_dt, 512)
    h = jnp.concatenate([jnp.broadcast_to(cls_tok, (h.shape[0], 1, h.shape[2])), h], axis=1)
    h = h + _L0_attn_ref(_layernorm(h, axis=-1), L0_attn_Wq, L0_attn_bq, L0_attn_Wk, L0_attn_bk, L0_attn_Wv, L0_attn_bv, L0_attn_Wo, L0_attn_bo)
    h = h + _L0_ffn_ref(_layernorm(h, axis=-1), L0_ffn_Wg, L0_ffn_W1, L0_ffn_W2, L0_ffn_W3, L0_ffn_A1, L0_ffn_B1, L0_ffn_A2, L0_ffn_B2, L0_ffn_A3, L0_ffn_B3)
    return h

_drawn_inputs = setup_inputs


def setup_inputs(seed=0):
    import zlib

    import numpy as np

    out = dict(_drawn_inputs(seed))
    spreads = {'L0_attn_bq': (0.0, 0.1),
     'L0_attn_bk': (0.0, 0.8),
     'L0_attn_bv': (0.0, 0.1),
     'L0_attn_bo': (0.0, 0.1)}
    factors = {'L0_ffn_A1': 3.625,
     'L0_ffn_B1': 3.597,
     'L0_ffn_A2': 3.623,
     'L0_ffn_B2': 3.647,
     'L0_ffn_A3': 3.539,
     'L0_ffn_B3': 3.531}
    for name, (base, spread) in spreads.items():
        noise = np.random.default_rng([zlib.crc32(name.encode()), seed]).standard_normal(out[name].shape)
        drawn = base * np.exp(spread * noise) if base else spread * noise
        out[name] = jnp.asarray(drawn.astype(out[name].dtype))
    for name, factor in factors.items():
        out[name] = (out[name] * factor).astype(out[name].dtype)
    return out
```

```python
from contextlib import ExitStack

import concourse.bass as bass
from concourse import mybir

F32 = mybir.dt.float32
F16 = mybir.dt.float16
BF16 = mybir.dt.bfloat16
ACT = mybir.ActivationFunctionType
ALU = mybir.AluOpType
AX = mybir.AxisListType
P = 128
W_SCALE = 64.0
W_UNSCALE = 1.0 / W_SCALE


def tokenizer_phase(nc, spectra, kry_b, readout, log_dt, cls_rows, consts, tokens):
    eye32_d, eye16_d, two_eye_d, half_eye_d, ones16_d, ones32_d = consts
    H = spectra.shape[1]
    CHANNELS = readout.shape[2]
    L = tokens.shape[2]
    CHAINS, CH = 4, 4
    SET = CHAINS * CH
    SETS = H // SET
    COARSE = 7
    EXACT = 2
    LEVELS = L.bit_length() - 1

    with ExitStack() as ctx:
        def sb(name, shape, dt):
            return ctx.enter_context(nc.sbuf_tensor(name, shape, dt))

        def sem(name):
            return ctx.enter_context(nc.semaphore(name))

        raw = sb("raw", [P, SET, P], F32)
        minus_back = sb("minus_back", [P, SET, P], F32)
        minus_back16 = sb("minus_back16", [P, SET, P], F16)
        inv16 = sb("inv16", [P, SET, P], F16)
        corr16 = sb("corr16", [P, SET, P], F16)
        inv32 = sb("inv32", [P, SET, P], F32)
        corr32 = sb("corr32", [P, SET, P], F32)
        power = sb("power", [P, SET, P], F32)
        power_t = sb("power_t", [P, 2, SET, P], F32)
        krylov = sb("krylov", [P, SET, L], F32)
        read_t = sb("read_t", [P, SET, CHANNELS], F32)
        rows = sb("rows", [CHANNELS, SET, L], F32)
        half_dt = sb("half_dt", [P, H], F32)
        drive = sb("drive", [P, H], F32)
        row_sum = sb("row_sum", [P, SET], F32)
        col_max = sb("col_max", [P, SET], F32)
        row_max = sb("row_max", [SET, 1], F32)
        row_diag = sb("row_diag", [SET, SET], F32)
        alpha = sb("alpha", [P, SET], F32)
        eye32 = sb("eye32", [P, P], F32)
        eye16 = sb("eye16", [P, P], F16)
        two_eye = sb("two_eye", [P, CH * P], F16)
        half_eye = sb("half_eye", [P, CH * P], F16)
        ones16 = sb("ones16", [P, P], F16)
        ones32 = sb("ones32", [P, P], F32)
        ps = ctx.enter_context(nc.psum_tensor("ps_tok", [P, 8, 512], F32))

        s_const = sem("a_const")
        s_dt = sem("a_dt")
        s_raw = sem("a_raw_loaded")
        s_read = sem("a_readout_loaded")
        s_stored = sem("a_rows_stored")
        s_cls = sem("a_cls_stored")
        s_dve = sem("a_dve_chain")
        s_rawfree = sem("a_raw_consumed")
        s_back = sem("a_back_ready")
        s_abs = sem("a_abs_ready")
        s_norm = sem("a_norms")
        s_diag = sem("a_diag")
        s_bcast = sem("a_bcast")
        s_start = sem("a_start_ready")
        s_neg = sem("a_readout_signed")
        s_pe = sem("a_products")
        s_act = sem("a_act_copied")
        s_vec = sem("a_dve_copied")

        rounds = []
        for n in range(COARSE):
            rounds += [("corr16", n), ("inv16", n)]
        for n in range(EXACT):
            rounds += [("corr32", n), ("inv32", n)]
        rounds += [("transpose", -1), ("seed", 0)]
        for k in range(LEVELS - 1):
            rounds.append(("square", k))
            if k < LEVELS - 2:
                rounds.append(("transpose_back", k))
        rounds += [("last_double", LEVELS - 1), ("read", 0), ("read", 1)]
        R = len(rounds)

        def bank(g, n):
            return ps[:, 2 * g + n, :]

        def bank4(g, n, m=P):
            return ps[:, 2 * g + n, 0:CH * m].rearrange("p (h m) -> p h m", m=m)

        def chain(t, g):
            return t[:, CH * g:CH * g + CH, :]

        def copies(kind, k, g):
            if kind == "corr16":
                return [(chain(corr16, g), bank4(g, 0), 1.0)]
            if kind == "inv16":
                return [(chain(inv32 if k == COARSE - 1 else inv16, g), bank4(g, 1), 1.0)]
            if kind == "corr32":
                return [(chain(corr32, g), bank4(g, 0), 1.0)]
            if kind == "inv32":
                if k == EXACT - 1:
                    return [(chain(power, g), bank4(g, 1), 2.0)]
                return [(chain(inv32, g), bank4(g, 1), 1.0)]
            if kind == "transpose":
                return [(chain(power_t[:, 0], g), bank4(g, 0), 1.0)]
            if kind == "seed":
                return [(krylov[:, CH * g:CH * g + CH, 0:1], bank4(g, 1, 1), 1.0)]
            if kind == "square":
                n = 1 << k
                return [(chain(power_t[:, (k + 1) % 2], g), bank4(g, 0), 1.0),
                        (krylov[:, CH * g:CH * g + CH, n:2 * n], bank4(g, 1, n), 1.0)]
            if kind == "transpose_back":
                return [(chain(power, g), bank4(g, 1), 1.0)]
            if kind == "last_double":
                n = 1 << k
                return [(krylov[:, CH * g + 2 * m:CH * g + 2 * m + 2, n:2 * n],
                         bank(g, m).rearrange("p (h l) -> p h l", h=2), 1.0) for m in range(2)]
            return [(rows[:, CH * g + 2 * k + m, :], bank(g, m)[0:CHANNELS], 1.0) for m in range(2)]

        with nc.Block() as block:

            @block.sync
            def _(sp):
                for dst, src in ((eye32, eye32_d), (eye16, eye16_d), (two_eye, two_eye_d),
                                 (half_eye, half_eye_d), (ones16, ones16_d), (ones32, ones32_d)):
                    sp.dma_start(dst[:], src).then_inc(s_const, 16)
                sp.dma_start(half_dt[:], log_dt).then_inc(s_dt, 16)
                sp.dma_start(drive[:], kry_b).then_inc(s_dt, 16)
                sp.dma_start(raw[:], spectra[:, 0:SET, :]).then_inc(s_raw, 16)
                sp.dma_start(read_t[:], readout[:, 0:SET, :]).then_inc(s_read, 16)
                sp.dma_start(tokens[:, 0, :], cls_rows).then_inc(s_cls, 16)

                def store(i):
                    sp.wait_ge(s_act, (i + 1) * 2 * R)
                    sp.wait_ge(s_vec, (i + 1) * 2 * R)
                    sp.dma_start(tokens[:, bass.ds(i * SET + 1, SET), :], rows[:]).then_inc(s_stored, 16)

                with sp.Fori(0, SETS - 1) as i:
                    sp.wait_ge(s_rawfree, i + 1)
                    sp.dma_start(raw[:], spectra[:, bass.ds((i + 1) * SET, SET), :]).then_inc(s_raw, 16)
                    store(i)
                    sp.dma_start(read_t[:], readout[:, bass.ds((i + 1) * SET, SET), :]).then_inc(s_read, 16)
                store(SETS - 1)
                sp.wait_ge(s_stored, 16 * SETS)
                sp.wait_ge(s_cls, 16)

            @block.scalar
            def _(act):
                def copy(out, src, scale):
                    return nc.scalar.activation(out, src, ACT.Copy, scale=scale)

                act.wait_ge(s_dt, 32)
                nc.scalar.activation(half_dt[:], half_dt[:], ACT.Exp).then_inc(s_dt, 1)

                def one_set(i, first):
                    act.wait_ge(s_back, i + 1)
                    nc.scalar.activation(corr16[:], minus_back[:], ACT.Abs)
                    nc.scalar.activation(minus_back16[:], minus_back[:], ACT.Copy).then_inc(s_abs, 1)
                    for s, (kind, k) in enumerate(rounds):
                        for g in (0, 2):
                            act.wait_ge(s_pe, i * (4 * R) + (4 * s + g + 1))
                            if kind == "read" and k == 0 and not first:
                                act.wait_ge(s_stored, i * 16)
                            for out, src, scale in copies(kind, k, g):
                                last = copy(out, src, scale)
                            last.then_inc(s_act, 1)

                one_set(0, True)
                with act.Fori(1, SETS) as i:
                    one_set(i, False)

            @block.vector
            def _(dve):
                def copy(out, src, scale):
                    if scale == 1.0:
                        return nc.vector.tensor_copy(out, src)
                    return nc.vector.tensor_scalar(out, src, scale, None, ALU.mult)

                dve.wait_ge(s_const, 16 * 6)
                dve.wait_ge(s_dt, 33)
                nc.vector.tensor_scalar(half_dt[:], half_dt[:], 0.5, None, ALU.mult).then_inc(s_dve, 1)
                dve.wait_ge(s_dve, 1)
                nc.vector.tensor_tensor(drive[:], drive[:], half_dt[:], ALU.mult).then_inc(s_dve, 1)
                dve.wait_ge(s_dve, 2)
                LINKS = 5

                def one_set(i, first):
                    count = [0]

                    def link(ins):
                        count[0] += 1
                        ins.then_inc(s_dve, 1)
                        dve.wait_ge(s_dve, i * LINKS + (count[0] + 2))

                    dve.wait_ge(s_raw, (i + 1) * 16)
                    dt_set = half_dt[:, bass.ds(i * SET, SET)]
                    nc.vector.tensor_tensor(minus_back[:], raw[:], dt_set.unsqueeze(2).broadcast_to([P, SET, P]),
                                            ALU.mult).then_inc(s_rawfree, 1)
                    dve.wait_ge(s_rawfree, i + 1)
                    link(nc.vector.tensor_scalar(minus_back[64:P, :, 0:64], minus_back[64:P, :, 0:64], -1.0, None,
                                                 ALU.mult))
                    nc.vector.tensor_tensor(minus_back[:], minus_back[:],
                                            eye32[:].unsqueeze(1).broadcast_to([P, SET, P]),
                                            ALU.subtract).then_inc(s_back, 1)
                    dve.wait_ge(s_back, i + 1)
                    nc.vector.tensor_reduce(row_sum[:], minus_back[:], AX.X, ALU.add,
                                            apply_absolute_value=True).then_inc(s_norm, 1)
                    dve.wait_ge(s_read, (i + 1) * 16)
                    nc.vector.tensor_scalar(read_t[64:P], read_t[64:P], -1.0, None, ALU.mult).then_inc(s_neg, 1)
                    dve.wait_ge(s_diag, 2 * i + 1)
                    nc.vector.tensor_reduce(col_max[:], ps[:, 0:8:2, :].rearrange("p b (h m) -> p b h m", m=P),
                                            AX.X, ALU.max)
                    link(nc.vector.tensor_reduce(row_max[:], ps[0:SET, 1, 0:P], AX.X, ALU.max))
                    nc.vector.tensor_scalar(row_diag[:], eye32[0:SET, 0:SET], row_max[:, 0:1], None,
                                            ALU.mult).then_inc(s_bcast, 1)
                    dve.wait_ge(s_diag, 2 * i + 2)
                    link(nc.vector.tensor_tensor(alpha[:], col_max[:], ps[:, 3, 0:SET], ALU.mult))
                    link(nc.vector.reciprocal(alpha[:], alpha[:]))
                    link(nc.vector.tensor_scalar(alpha[:], alpha[:], -1.0, None, ALU.mult))
                    nc.vector.tensor_tensor(inv16[:], minus_back[:],
                                            alpha[:].unsqueeze(2).broadcast_to([P, SET, P]),
                                            ALU.mult).then_inc(s_start, 1)
                    for s, (kind, k) in enumerate(rounds):
                        for g in (1, 3):
                            dve.wait_ge(s_pe, i * (4 * R) + (4 * s + g + 1))
                            if kind == "read" and k == 0 and not first:
                                dve.wait_ge(s_stored, i * 16)
                            for out, src, scale in copies(kind, k, g):
                                last = copy(out, src, scale)
                            last.then_inc(s_vec, 1)
                    assert count[0] == LINKS

                one_set(0, True)
                with dve.Fori(1, SETS) as i:
                    one_set(i, False)

            @block.tensor
            def _(pe):
                mm = nc.tensor.matmul
                pe.wait_ge(s_const, 16 * 6)

                def one_set(i, first):
                    pe.wait_ge(s_abs, i + 1)
                    pe.wait_ge(s_norm, i + 1)
                    if not first:
                        pe.wait_ge(s_act, i * (2 * R))
                        pe.wait_ge(s_vec, i * (2 * R))
                    for g in range(CHAINS):
                        mm(bank(g, 0), ones16[:], chain(corr16, g), start=True, stop=True)
                    nc.tensor.transpose(ps[0:SET, 1, 0:P], row_sum[:], eye32[:]).then_inc(s_diag, 1)
                    pe.wait_ge(s_bcast, i + 1)
                    mm(ps[:, 3, 0:SET], ones32[0:SET, :], row_diag[:], start=True, stop=True).then_inc(s_diag, 1)
                    pe.wait_ge(s_start, i + 1)
                    pe.wait_ge(s_neg, i + 1)
                    for s, (kind, k) in enumerate(rounds):
                        for g in range(CHAINS):
                            if s:
                                pe.wait_ge(s_vec if g % 2 else s_act, i * (2 * R) + (2 * (s - 1) + g // 2 + 1))
                            hs = range(CH * g, CH * g + CH)
                            if kind in ("corr16", "corr32"):
                                x, b = (inv16, minus_back16) if kind == "corr16" else (inv32, minus_back)
                                mm(bank(g, 0), eye16[:], two_eye[:], start=True, stop=False)
                                for j, h in enumerate(hs):
                                    last = mm(bank4(g, 0)[:, j], x[:, h], b[:, h], start=False, stop=j == CH - 1)
                            elif kind in ("inv16", "inv32"):
                                x, c = (inv16, corr16) if kind == "inv16" else (inv32, corr32)
                                final = kind == "inv32" and k == EXACT - 1
                                if final:
                                    mm(bank(g, 1), eye16[:], half_eye[:], start=True, stop=False)
                                for j, h in enumerate(hs):
                                    last = mm(bank4(g, 1)[:, j], c[:, h], x[:, h], start=not final, stop=not final or j == CH - 1)
                            elif kind == "transpose":
                                for j, h in enumerate(hs):
                                    last = nc.tensor.transpose(bank4(g, 0)[:, j], power[:, h], eye32[:])
                            elif kind == "transpose_back":
                                for j, h in enumerate(hs):
                                    last = nc.tensor.transpose(bank4(g, 1)[:, j], power_t[:, (k + 1) % 2, h],
                                                               eye32[:])
                            elif kind == "seed":
                                b = drive[:, bass.ds(i * SET + CH * g, CH)]
                                mm(bank(g, 1)[:, 0:CH], eye32[:], b, start=True, stop=False)
                                for j, h in enumerate(hs):
                                    last = mm(bank(g, 1)[:, j:j + 1], power_t[:, 0, h],
                                              drive[:, bass.ds(i * SET + h, 1)], start=False, stop=j == CH - 1)
                            elif kind == "square":
                                n = 1 << k
                                for j, h in enumerate(hs):
                                    mm(bank4(g, 0)[:, j], power[:, h], power_t[:, k % 2, h], start=True, stop=True)
                                for j, h in enumerate(hs):
                                    last = mm(bank4(g, 1, n)[:, j], power_t[:, k % 2, h], krylov[:, h, 0:n],
                                              start=True, stop=True)
                            elif kind == "last_double":
                                n = 1 << k
                                for j, h in enumerate(hs):
                                    last = mm(bank(g, j // 2)[:, (j % 2) * n:(j % 2 + 1) * n], power_t[:, k % 2, h],
                                              krylov[:, h, 0:n], start=True, stop=True)
                            else:
                                for m in range(2):
                                    h = CH * g + 2 * k + m
                                    last = mm(bank(g, m)[0:CHANNELS], read_t[:, h], krylov[:, h, :], start=True,
                                              stop=True)
                            last.then_inc(s_pe, 1)

                one_set(0, True)
                with pe.Fori(1, SETS) as i:
                    one_set(i, False)


def attention_phase(nc, weights, biases, consts, tokens, mixed):
    eye32_d, eye_bf_d, causal_d = consts
    IMAGES, S, D = tokens.shape
    HEADS, DK = 16, 32
    QB = 4
    QUADS = IMAGES // QB
    T = QB * S
    KT = D // P
    G = P // DK
    HB = HEADS // 2
    V1 = DK + 1
    EPS = 1e-5

    with ExitStack() as ctx:
        def sb(name, shape, dt):
            return ctx.enter_context(nc.sbuf_tensor(name, shape, dt))

        def sem(name):
            return ctx.enter_context(nc.semaphore(name))

        w_hi = sb("w_hi", [P, 4, KT, D], F16)
        w_lo = sb("w_lo", [P, 4, KT, D], F16)
        stage = sb("stage", [P, 2, KT, D], F32)
        bias = sb("bias", [P, 4, KT], F32)
        eye32 = sb("b_eye32", [P, P], F32)
        eye_bf = sb("b_eye_bf", [S, S], BF16)
        causal = sb("causal", [S, KT * S], BF16)
        rows = sb("b_rows", [S, QB, D], F32)
        normed = sb("b_normed", [S, QB, D], F32)
        stats = sb("b_stats", [S, QB, 6], F32)
        mean = sb("b_mean", [S, QB], F32)
        gap = sb("b_gap", [S, QB], F32)
        spread = sb("b_spread", [S, QB], F32)
        var_eps = sb("b_var_eps", [S, QB], F32)
        rstd = sb("b_rstd", [S, QB], F32)
        minus_half = sb("b_minus_half", [S, QB], F32)
        x_hi = sb("b_x_hi", [P, KT, T], F16)
        x_lo = sb("b_x_lo", [P, KT, T], F16)
        q_t = sb("q_t", [P, 2, KT, T], F32)
        k_t = sb("k_t", [P, 2, KT, T], F32)
        v_t = sb("v_t", [P, KT, T], F32)
        v_rows = sb("v_rows", [S, 2, QB, HEADS, V1], F32)
        top = sb("top", [S, G, KT], F32)
        probs = sb("probs", [S, G, KT, S], F32)
        probs_t = sb("probs_t", [S, G, KT, S], F32)
        recip = sb("recip", [S, HEADS], F32)
        context = sb("context", [S, QB, HEADS, DK], F32)
        c_hi = sb("c_hi", [P, KT, T], F16)
        c_lo = sb("c_lo", [P, KT, T], F16)
        o_t = sb("o_t", [P, KT, T], F32)
        resid = sb("resid", [S, QB, D], F32)
        ps = ctx.enter_context(nc.psum_tensor("ps_attn", [P, 8, 512], F32))
        SCORES, CTX, WORK = 0, 4, 6

        s_const = sem("b_const")
        s_w = [sem(f"b_weight_loaded{n}") for n in range(2)]
        s_whi = sem("b_weight_high")
        s_wlo = sem("b_weight_low")
        s_rows = sem("b_rows_loaded")
        s_resid = sem("b_resid_loaded")
        s_stored = sem("b_mixed_stored")
        s_stats = sem("b_stats")
        s_var = sem("b_variance")
        s_rstd = sem("b_rstd")
        s_normed = sem("b_normed")
        s_ones = sem("b_ones")
        s_moments = sem("b_moments")
        s_top = sem("b_maxima")
        s_recip = sem("b_recips")
        s_scores = sem("b_scores")
        s_shift = sem("b_shifted")
        s_exp = sem("b_exponentials")
        s_pt = sem("b_probs_turned")
        s_pt_act = sem("b_probs_t_act")
        s_pt_dve = sem("b_probs_t_dve")
        s_ctx = sem("b_contexts")
        s_norm = sem("b_contexts_normed")
        KINDS = {"xt": "AD", "ct": "AD", "q": "A", "k": "A", "v": "A", "vt": "D", "wo": "A", "ot": "D"}
        s_unit = {k: sem(f"b_{k}_products") for k in KINDS}
        s_copy = {(k, e): sem(f"b_{k}_copied_{e}") for k, es in KINDS.items() for e in es}

        def count(n, j, per):
            return n * per + (j + 1)

        def slot(name, q, prev, nxt):
            kind, of = {"A0": ("xt", 1), "B0": ("ct", -1), "A1": ("q", 1), "B1": ("wo", -1),
                        "A2": ("k", 1), "B2": ("ot", -1), "A3": ("v", 1), "B3": ("vt", 1)}[name]
            if (of == 1 and not nxt) or (of == -1 and not prev):
                return []
            return [(kind, q + of, j) for j in range(4)]

        def work(j):
            return ps[:, WORK + j % 2, :]

        def run_quads(eng, prologue, quad, epilogue):
            prologue()
            quad(0, 0, False, True, True)
            with eng.Fori(0, (QUADS - 4) // 2) as i:
                quad(i * 2 + 1, 1, True, True, True)
                quad(i * 2 + 2, 0, True, True, True)
            quad(QUADS - 3, 1, True, True, True)
            quad(QUADS - 2, 0, True, True, False)
            quad(QUADS - 1, 1, True, False, False)
            epilogue()

        with nc.Block() as block:

            @block.sync
            def _(sp):
                for n in range(4):
                    if n >= 2:
                        sp.wait_ge(s_whi, n - 1)
                        sp.wait_ge(s_wlo, n - 1)
                    sp.dma_start(stage[:, n % 2], weights[n]).then_inc(s_w[n % 2], 16)
                    if n == 0:
                        sp.dma_start(eye32[:], eye32_d).then_inc(s_const, 16)
                        sp.dma_start(eye_bf[:], eye_bf_d).then_inc(s_const, 16)
                        sp.dma_start(causal[:], causal_d).then_inc(s_const, 16)
                        sp.dma_start(bias[:], biases).then_inc(s_const, 16)
                        sp.dma_start(rows[:], tokens[0:QB].rearrange("b s d -> s b d")).then_inc(s_rows, 16)

                def store(n):
                    sp.wait_ge(s_copy["ot", "D"], count(n, 3, 4))
                    sp.dma_start(mixed[bass.ds(n * QB, QB)].rearrange("b s d -> s b d"), resid[:]).then_inc(s_stored, 16)

                def load_resid(n):
                    sp.dma_start(resid[:], tokens[bass.ds(n * QB, QB)].rearrange("b s d -> s b d")).then_inc(s_resid, 16)

                def load_rows(n):
                    sp.wait_ge(s_normed, count(n - 1, 3, 4))
                    sp.dma_start(rows[:], tokens[bass.ds(n * QB, QB)].rearrange("b s d -> s b d")).then_inc(s_rows, 16)

                load_resid(0)
                load_rows(1)
                load_rows(2)
                with sp.Fori(0, QUADS - 3) as n:
                    load_rows(n + 3)
                    store(n)
                    sp.wait_ge(s_stored, n * 16 + 16)
                    load_resid(n + 1)
                for n in range(QUADS - 3, QUADS):
                    store(n)
                    sp.wait_ge(s_stored, n * 16 + 16)
                    if n + 1 < QUADS:
                        load_resid(n + 1)

            @block.gpsimd
            def _(pool):
                nc.gpsimd.memset(minus_half[:], -0.5).then_inc(s_ones, 1)
                nc.gpsimd.memset(v_rows[:, :, :, :, DK:V1], 1.0).then_inc(s_ones, 1)
                pool.wait_ge(s_ones, 1)

                def one(n):
                    pool.wait_ge(s_var, n + 1)
                    nc.gpsimd.tensor_tensor(rstd[:], var_eps[:], minus_half[:], ALU.pow).then_inc(s_rstd, 1)

                one(0)
                with pool.Fori(1, QUADS) as n:
                    one(n)

            @block.scalar
            def _(act):
                def copy_unit(kind, n, par, j):
                    act.wait_ge(s_unit[kind], count(n, j, 4))
                    src = work(j)
                    if kind in ("xt", "ct"):
                        dst = x_hi if kind == "xt" else c_hi
                        ins = nc.scalar.activation(dst[:, j], src[:, 0:T], ACT.Copy)
                    elif kind in ("q", "k", "v"):
                        w = "qkv".index(kind)
                        dst = v_t[:, j] if kind == "v" else (q_t if kind == "q" else k_t)[:, par, j]
                        ins = nc.scalar.activation(dst, src[:, 0:T], ACT.Identity, bias=bias[:, w, j:j + 1],
                                                   scale=W_UNSCALE)
                    else:
                        ins = nc.scalar.activation(o_t[:, j], src[:, 0:T], ACT.Identity, bias=bias[:, 3, j:j + 1],
                                                   scale=W_UNSCALE)
                    ins.then_inc(s_copy[kind, "A"], 1)

                def fill(name, q, par, prev, nxt):
                    for kind, n, j in slot(name, q, prev, nxt):
                        if "A" in KINDS[kind]:
                            copy_unit(kind, n, 1 - par, j)

                def prologue():
                    for n in range(4):
                        act.wait_ge(s_w[n % 2], 16 * (n // 2 + 1))
                        nc.scalar.activation(w_hi[:, n], stage[:, n % 2], ACT.Copy, scale=W_SCALE).then_inc(s_whi, 1)
                    act.wait_ge(s_const, 64)
                    for name in ("A0", "A1", "A2", "A3"):
                        fill(name, -1, 1, False, True)

                def quad(q, par, prev, nxt, nxt2):
                    for b in range(QB):
                        act.wait_ge(s_shift, count(q, b, QB))
                        nc.scalar.activation(probs[:], probs[:], ACT.Exp, scale=DK ** -0.5).then_inc(s_exp, 1)
                        fill(f"A{b}", q, par, prev, nxt)
                        act.wait_ge(s_pt, count(q, b, QB))
                        nc.scalar.activation(probs_t[:, 0:2], ps[0:S, SCORES:SCORES + 2, 0:KT * S]
                                             .rearrange("p g (t k) -> p g t k", t=KT), ACT.Copy).then_inc(s_pt_act, 1)
                        fill(f"B{b}", q, par, prev, nxt)

                def epilogue():
                    for name in ("B0", "B1", "B2"):
                        fill(name, QUADS, 0, True, False)

                run_quads(act, prologue, quad, epilogue)

            @block.vector
            def _(dve):
                def copy_unit(kind, n, par, j):
                    dve.wait_ge(s_unit[kind], count(n, j, 4))
                    src = work(j)
                    if kind in ("xt", "ct"):
                        hi, lo = (x_hi, x_lo) if kind == "xt" else (c_hi, c_lo)
                        dve.wait_ge(s_copy[kind, "A"], count(n, j, 4))
                        ins = nc.vector.tensor_tensor(lo[:, j], src[:, 0:T], hi[:, j], ALU.subtract)
                    elif kind == "vt":
                        ins = nc.vector.tensor_copy(v_rows[:, par, j, :, 0:DK],
                                                    src[0:S].rearrange("p (h d) -> p h d", d=DK))
                    else:
                        if j == 0:
                            dve.wait_ge(s_resid, n * 16 + 16)
                        ins = nc.vector.tensor_tensor(resid[:, j], src[0:S], resid[:, j], ALU.add)
                    ins.then_inc(s_copy[kind, "D"], 1)

                def fill(name, q, par, prev, nxt):
                    for kind, n, j in slot(name, q, prev, nxt):
                        if "D" in KINDS[kind]:
                            copy_unit(kind, n, 1 - par, j)

                def ln_stats(n, bs):
                    if bs[0] == 0:
                        dve.wait_ge(s_rows, n * 16 + 16)
                    for b in bs:
                        nc.vector.bn_stats(stats[:, b], rows[:, b]).then_inc(s_stats, 1)
                    if bs[-1] < QB - 1:
                        return
                    dve.wait_ge(s_stats, count(n, 3, 4))
                    tt = nc.vector.tensor_tensor
                    tt(mean[:], stats[:, :, 1], stats[:, :, 4], ALU.add)
                    tt(gap[:], stats[:, :, 1], stats[:, :, 4], ALU.subtract)
                    tt(spread[:], stats[:, :, 2], stats[:, :, 5], ALU.add).then_inc(s_moments, 1)
                    dve.wait_ge(s_moments, n * 2 + 1)
                    nc.vector.tensor_scalar(mean[:], mean[:], 0.5, None, ALU.mult)
                    tt(gap[:], gap[:], gap[:], ALU.mult)
                    nc.vector.tensor_scalar(spread[:], spread[:], 1.0 / D, EPS, ALU.mult,
                                            ALU.add).then_inc(s_moments, 1)
                    dve.wait_ge(s_moments, n * 2 + 2)
                    nc.vector.scalar_tensor_tensor(var_eps[:], gap[:], 0.25, spread[:], ALU.mult,
                                                   ALU.add).then_inc(s_var, 1)

                def ln_rows(n, bs):
                    if bs[0] == 0:
                        dve.wait_ge(s_rstd, n + 1)
                    for b in bs:
                        nc.vector.tensor_scalar(normed[:, b], rows[:, b], mean[:, b:b + 1], rstd[:, b:b + 1],
                                                ALU.subtract, ALU.mult).then_inc(s_normed, 1)

                def prologue():
                    dve.wait_ge(s_ones, 2)
                    for n in range(4):
                        dve.wait_ge(s_w[n % 2], 16 * (n // 2 + 1))
                        dve.wait_ge(s_whi, n + 1)
                        nc.vector.scalar_tensor_tensor(w_lo[:, n], stage[:, n % 2], W_SCALE, w_hi[:, n],
                                                       ALU.mult, ALU.subtract).then_inc(s_wlo, 1)
                    ln_stats(0, (0, 1))
                    ln_stats(0, (2, 3))
                    ln_rows(0, (0, 1, 2, 3))
                    fill("A0", -1, 1, False, True)
                    ln_stats(1, (0, 1))
                    ln_stats(1, (2, 3))
                    ln_rows(1, (0, 1, 2, 3))
                    fill("B3", -1, 1, False, True)

                def quad(q, par, prev, nxt, nxt2):
                    for b in range(QB):
                        dve.wait_ge(s_scores, count(q, b, QB))
                        scores = ps[0:S, SCORES:SCORES + G, 0:KT * S].rearrange("p g (t k) -> p g t k", t=KT)
                        nc.vector.tensor_reduce(top[:], scores, AX.X, ALU.max).then_inc(s_top, 1)
                        dve.wait_ge(s_top, count(q, b, QB))
                        nc.vector.tensor_tensor(probs[:], scores, top[:].unsqueeze(3).broadcast_to([S, G, KT, S]),
                                                ALU.subtract).then_inc(s_shift, 1)
                        fill(f"A{b}", q, par, prev, nxt)
                        dve.wait_ge(s_pt, count(q, b, QB))
                        nc.vector.tensor_copy(probs_t[:, 2:4], ps[0:S, SCORES + 2:SCORES + 4, 0:KT * S]
                                              .rearrange("p g (t k) -> p g t k", t=KT)).then_inc(s_pt_dve, 1)
                        fill(f"B{b}", q, par, prev, nxt)
                        if nxt2:
                            if b < 2:
                                ln_stats(q + 2, (2 * b, 2 * b + 1))
                            else:
                                ln_rows(q + 2, (2 * b - 4, 2 * b - 3))
                        dve.wait_ge(s_ctx, count(q, b, QB))
                        sums = ps[0:S, CTX:CTX + 2, 0:HB * V1].rearrange("p m (h d) -> p m h d", d=V1)
                        nc.vector.reciprocal(recip[:].rearrange("p (m h) -> p m h", m=2),
                                             sums[:, :, :, DK]).then_inc(s_recip, 1)
                        dve.wait_ge(s_recip, count(q, b, QB))
                        nc.vector.tensor_tensor(context[:, b].rearrange("p (m h) d -> p m h d", m=2),
                                                sums[:, :, :, 0:DK],
                                                recip[:].rearrange("p (m h) -> p m h", m=2).unsqueeze(3)
                                                .broadcast_to([S, 2, HB, DK]), ALU.mult).then_inc(s_norm, 1)

                def epilogue():
                    for name in ("B0", "B2"):
                        fill(name, QUADS, 0, True, False)

                run_quads(dve, prologue, quad, epilogue)

            @block.tensor
            def _(pe):
                mm = nc.tensor.matmul
                recent = [None, None]

                def unit(kind, n, j):
                    before = recent[j % 2]
                    if before is not None:
                        for e in KINDS[before[0]]:
                            pe.wait_ge(s_copy[before[0], e], count(before[1], before[2], 4))
                    recent[j % 2] = (kind, n, j)
                    out = work(j)
                    if kind == "xt":
                        if j == 0:
                            pe.wait_ge(s_normed, count(n, 3, 4))
                        for b in range(QB):
                            last = nc.tensor.transpose(out[:, b * S:(b + 1) * S], normed[:, b, j * P:(j + 1) * P],
                                                       eye32[0:S, 0:S])
                    elif kind == "ct":
                        if j == 0:
                            pe.wait_ge(s_norm, count(n, 3, 4))
                        for b in range(QB):
                            flat = context[:, b].rearrange("p h d -> p (h d)")
                            last = nc.tensor.transpose(out[:, b * S:(b + 1) * S], flat[:, j * P:(j + 1) * P],
                                                       eye32[0:S, 0:S])
                    elif kind in ("q", "k", "v", "wo"):
                        w = ("q", "k", "v", "wo").index(kind)
                        hi, lo = (c_hi, c_lo) if kind == "wo" else (x_hi, x_lo)
                        src = "ct" if kind == "wo" else "xt"
                        if j == 0:
                            pe.wait_ge(s_copy[src, "A"], count(n, 3, 4))
                            pe.wait_ge(s_copy[src, "D"], count(n, 3, 4))
                        for k in range(KT):
                            for m, (a, x) in enumerate(((w_hi, hi), (w_hi, lo), (w_lo, hi))):
                                last = mm(out[:, 0:T], a[:, w, k, j * P:(j + 1) * P], x[:, k],
                                          start=k == 0 and m == 0, stop=k == KT - 1 and m == 2)
                    elif kind == "vt":
                        if j == 0:
                            pe.wait_ge(s_copy["v", "A"], count(n, 3, 4))
                        for t in range(KT):
                            last = nc.tensor.transpose(out[0:S, t * P:(t + 1) * P], v_t[:, t, j * S:(j + 1) * S],
                                                       eye32[:])
                    else:
                        if j == 0:
                            pe.wait_ge(s_copy["wo", "A"], count(n, 3, 4))
                        for t in range(KT):
                            last = nc.tensor.transpose(out[0:S, t * P:(t + 1) * P], o_t[:, t, j * S:(j + 1) * S],
                                                       eye32[:])
                    last.then_inc(s_unit[kind], 1)

                def fill(name, q, par, prev, nxt):
                    for kind, n, j in slot(name, q, prev, nxt):
                        unit(kind, n, j)

                def prologue():
                    pe.wait_ge(s_const, 64)
                    fill("A0", -1, 1, False, True)
                    pe.wait_ge(s_whi, 4)
                    pe.wait_ge(s_wlo, 4)
                    for name in ("A1", "A2", "A3", "B3"):
                        fill(name, -1, 1, False, True)

                def quad(q, par, prev, nxt, nxt2):
                    recent[:] = [("vt", q, 2), ("vt", q, 3)]
                    pe.wait_ge(s_copy["k", "A"], count(q, 3, 4))
                    for b in range(QB):
                        if prev or b:
                            pe.wait_ge(s_pt_act, count(q, b - 1, QB))
                            pe.wait_ge(s_pt_dve, count(q, b - 1, QB))
                        cols = slice(b * S, (b + 1) * S)
                        for g in range(G):
                            mm(ps[0:S, SCORES + g, 0:KT * S], eye_bf[:], causal[:], start=True, stop=False)
                        for t in range(KT):
                            for g in range(G):
                                rows_g = slice(g * DK, (g + 1) * DK)
                                last = mm(ps[0:S, SCORES + g, t * S:(t + 1) * S], q_t[rows_g, par, t, cols],
                                          k_t[rows_g, par, t, cols], start=False, stop=t == KT - 1)
                        last.then_inc(s_scores, 1)
                        fill(f"A{b}", q, par, prev, nxt)
                        pe.wait_ge(s_exp, count(q, b, QB))
                        for g in range(G):
                            for t in range(KT):
                                last = nc.tensor.transpose(ps[0:S, SCORES + g, t * S:(t + 1) * S], probs[:, g, t],
                                                           eye32[0:S, 0:S])
                        last.then_inc(s_pt, 1)
                        fill(f"B{b}", q, par, prev, nxt)
                        pe.wait_ge(s_pt_act, count(q, b, QB))
                        pe.wait_ge(s_pt_dve, count(q, b, QB))
                        if b == 0:
                            pe.wait_ge(s_copy["vt", "D"], count(q, 3, 4))
                        if prev or b:
                            pe.wait_ge(s_norm, count(q, b - 1, QB))
                        for h in range(HEADS):
                            out = ps[0:S, CTX + h // HB, (h % HB) * V1:(h % HB + 1) * V1]
                            last = mm(out, probs_t[:, h % G, h // G], v_rows[:, par, b, h], start=True, stop=True)
                        last.then_inc(s_ctx, 1)

                def epilogue():
                    for name in ("B0", "B1", "B2"):
                        fill(name, QUADS, 0, True, False)

                run_quads(pe, prologue, quad, epilogue)


def expert_phase(nc, weights, consts, mixed, out):
    eye32_d, iota_d, select_d = consts
    TOKENS, D = mixed.shape
    E, R = 8, 32
    ER = E * R
    F = 1792
    KT, FT, ET = D // P, F // P, ER // P
    PAIRS = FT // 2
    T = 208
    BLOCKS = TOKENS // T
    TR = 104
    TT = T // TR
    EPS = 1e-5
    BIG = 3e38

    HEAD = 2 * KT * ER + KT * E
    PAIR = 2 * KT * 2 * P + 2 * ET * 2 * P + 2 * ER
    W2_AT = HEAD + PAIRS * PAIR
    B2_AT = W2_AT + FT * D
    WIDTH = B2_AT + ET * D
    PC = PAIR // 4
    CHUNKS = [(0, HEAD // 2), (HEAD // 2, HEAD // 2)] + [(HEAD + PC * c, PC) for c in range(4 * PAIRS)] \
        + [(W2_AT + PC * c, PC) for c in range(8)] + [(B2_AT, ET * D)]
    STAGE = max(w for _, w in CHUNKS)
    assert W2_AT + 8 * PC == B2_AT and weights.shape[1] == WIDTH

    with ExitStack() as ctx:
        def sb(name, shape, dt):
            return ctx.enter_context(nc.sbuf_tensor(name, shape, dt))

        def sem(name):
            return ctx.enter_context(nc.semaphore(name))

        w_hi = sb("f_w_hi", [P, WIDTH], F16)
        w_lo = sb("f_w_lo", [P, WIDTH], F16)
        stage = sb("f_stage", [P, 2, STAGE], F32)
        eye32 = sb("f_eye32", [P, P], F32)
        iota = sb("f_iota", [TR, TT, E], F32)
        select = sb("f_select", [32, 8, P], F16)
        rows = sb("f_rows", [TR, TT, D], F32)
        resid = sb("f_resid", [TR, TT, D], F32)
        stats = sb("f_stats", [TR, TT, 6], F32)
        mean = sb("f_mean", [TR, TT], F32)
        gap = sb("f_gap", [TR, TT], F32)
        spread = sb("f_spread", [TR, TT], F32)
        var_eps = sb("f_var_eps", [TR, TT], F32)
        rstd = sb("f_rstd", [TR, TT], F32)
        minus_half = sb("f_minus_half", [TR, TT], F32)
        euler = sb("f_euler", [TR, TT], F32)
        logits = sb("f_logits", [TR, TT, E], F32)
        logits2 = sb("f_logits2", [TR, TT, E], F32)
        rank = sb("f_rank", [TR, TT, E], F32)
        best = sb("f_best", [TR, TT], F32)
        best2 = sb("f_best2", [TR, TT], F32)
        first_at = sb("f_first_at", [TR, TT], F32)
        drop = sb("f_drop", [TR, TT], F32)
        odds = sb("f_odds", [TR, TT], F32)
        total = sb("f_total", [TR, TT], F32)
        route = sb("f_route", [TR, TT, 32], F32)
        route_hi = sb("f_route_hi", [32, T], F16)
        route_lo = sb("f_route_lo", [32, T], F16)
        x_hi = sb("f_x_hi", [P, KT, T], F16)
        x_lo = sb("f_x_lo", [P, KT, T], F16)
        a_hi = sb("f_a_hi", [P, ET, T], F16)
        a_lo = sb("f_a_lo", [P, ET, T], F16)
        am_hi = sb("f_am_hi", [P, 2, 2, ET, T], F16)
        am_lo = sb("f_am_lo", [P, 2, 2, ET, T], F16)
        mask = sb("f_mask", [P, 3, ET, T], F16)
        weight = sb("f_weight", [P, 2, T], F32)
        gate = sb("f_gate", [P, 2, T], F32)
        y0 = sb("f_y0", [P, 4, T], F32)
        y1 = sb("f_y1", [P, 2, T], F32)
        y_hi = sb("f_y_hi", [P, 2, 2, 2, T], F16)
        y_lo = sb("f_y_lo", [P, 2, 2, 2, T], F16)
        sum_hi = sb("f_sum_hi", [P, FT, T], F16)
        sum_lo = sb("f_sum_lo", [P, FT, T], F16)
        m_32 = sb("f_m_32", [P, ET, T], F32)
        m_hi = sb("f_m_hi", [P, ET, T], F16)
        m_lo = sb("f_m_lo", [P, ET, T], F16)
        o_t = y0
        ps = ctx.enter_context(nc.psum_tensor("ps_ffn", [P, 8, 512], F32))

        def bank(n):
            return ps[:, n, 0:2 * T].rearrange("p (a t) -> p a t", a=2)

        A2, DOWN = 4, 6

        def w1(m, p, k, j):
            return HEAD + p * PAIR + (m * KT + k) * 2 * P + j * P

        def b1(m, p, k, j):
            return HEAD + p * PAIR + 2 * KT * 2 * P + (m * ET + k) * 2 * P + j * P

        def a2(p, j, t):
            return HEAD + p * PAIR + 2 * (KT + ET) * 2 * P + j * ER + t * P

        def a1(m, k, t):
            return (m * KT + k) * ER + t * P

        names = ("const", "whi", "wlo", "rows", "resid", "stored", "stats", "moments", "var", "rstd", "normed",
                 "ones", "xt", "xhi", "xlo", "logits", "router", "drop", "odds", "route", "rt", "rhi", "rlo",
                 "expand", "exp_act", "low", "ahi", "alo", "am", "first", "second", "silu", "scaled", "y", "yhi",
                 "ylo", "sum", "shi", "slo", "acc0", "acc1", "masked", "mhi", "mlo", "down", "ot", "turned", "added")
        S = {n: sem("f_" + n) for n in names}
        s_wload = [sem(f"f_weights_loaded{n}") for n in range(2)]

        def at(n, per, j):
            return n * per + (j + 1)

        def turn(slot, p):
            if slot == 0:
                return max(2 * p - 1, 0)
            return min(2 * p + 2, 2 * PAIRS - 1)

        def pair_chunks(p):
            return range(2 + 4 * p, 6 + 4 * p)

        rest_chunks = range(2 + 4 * PAIRS, len(CHUNKS))

        def block_chunks(p):
            if p + 2 < PAIRS:
                return pair_chunks(p + 2)
            return rest_chunks[:len(rest_chunks) // 2] if p + 2 == PAIRS else rest_chunks[len(rest_chunks) // 2:]

        def run_blocks(eng, prologue, body, epilogue):
            prologue()
            body(0, True, True)
            with eng.Fori(1, BLOCKS - 1) as n:
                body(n, False, True)
            body(BLOCKS - 1, False, False)
            epilogue()

        def token_rows(dram, n):
            return dram[bass.ds(n * T, T)].rearrange("(a p) d -> p a d", p=TR)

        with nc.Block() as block:

            @block.sync
            def _(sp):
                sp.dma_start(rows[:], token_rows(mixed, 0)).then_inc(S["rows"], 16)
                for dst, src in ((eye32, eye32_d), (iota, iota_d), (select, select_d)):
                    sp.dma_start(dst[:], src).then_inc(S["const"], 16)
                sp.dma_start(resid[:], token_rows(mixed, 0)).then_inc(S["resid"], 16)
                for c, (start, width) in enumerate(CHUNKS):
                    if c >= 2:
                        sp.wait_ge(S["whi"], c - 1)
                        sp.wait_ge(S["wlo"], c - 1)
                    sp.dma_start(stage[:, c % 2, 0:width], weights[:, start:start + width]).then_inc(s_wload[c % 2], 16)
                    if c == 6:
                        sp.wait_ge(S["xt"], 2)
                        sp.dma_start(rows[:], token_rows(mixed, 1)).then_inc(S["rows"], 16)

                def store(n):
                    sp.wait_ge(S["added"], at(n, 2, 1))
                    sp.dma_start(token_rows(out, n), resid[:]).then_inc(S["stored"], 16)
                    sp.wait_ge(S["stored"], n * 16 + 16)

                with sp.Fori(0, BLOCKS - 2) as n:
                    sp.wait_ge(S["xt"], at(n + 1, 2, 1))
                    sp.dma_start(rows[:], token_rows(mixed, n + 2)).then_inc(S["rows"], 16)
                    store(n)
                    sp.dma_start(resid[:], token_rows(mixed, n + 1)).then_inc(S["resid"], 16)
                store(BLOCKS - 2)
                sp.dma_start(resid[:], token_rows(mixed, BLOCKS - 1)).then_inc(S["resid"], 16)
                store(BLOCKS - 1)

            @block.gpsimd
            def _(pool):
                nc.gpsimd.memset(minus_half[:], -0.5)
                nc.gpsimd.memset(euler[:], 2.718281828459045)
                nc.gpsimd.memset(route[:], 0.0).then_inc(S["ones"], 1)
                pool.wait_ge(S["ones"], 1)

                def one(n):
                    pool.wait_ge(S["var"], n + 1)
                    nc.gpsimd.tensor_tensor(rstd[:], var_eps[:], minus_half[:], ALU.pow).then_inc(S["rstd"], 1)
                    pool.wait_ge(S["drop"], n + 1)
                    nc.gpsimd.tensor_tensor(odds[:], euler[:], drop[:], ALU.pow).then_inc(S["odds"], 1)

                one(0)
                with pool.Fori(1, BLOCKS) as n:
                    one(n)

            @block.scalar
            def _(act):
                cp = nc.scalar.activation

                def split(c):
                    start, width = CHUNKS[c]
                    act.wait_ge(s_wload[c % 2], 16 * (c // 2 + 1))
                    cp(w_hi[:, start:start + width], stage[:, c % 2, 0:width], ACT.Copy,
                       scale=W_SCALE).then_inc(S["whi"], 1)

                def route_copy(n):
                    act.wait_ge(S["rt"], at(n, 1, 0))
                    cp(route_hi[:], ps[0:32, 1, 0:T], ACT.Copy).then_inc(S["rhi"], 1)
                    act.wait_ge(S["expand"], at(n, 4, 1))
                    for m in range(2):
                        last = cp(mask[:, m], bank(m), ACT.Copy)
                    last.then_inc(S["exp_act"], 1)
                    act.wait_ge(S["expand"], at(n, 4, 3))
                    cp(mask[:, 2], bank(4), ACT.Copy)
                    cp(weight[:], bank(5), ACT.Copy).then_inc(S["exp_act"], 1)

                def read_out(slot, n, p, first):
                    par = p % 2
                    k = turn(slot, p)
                    act.wait_ge(S["second" if slot else "first"], at(n, PAIRS, p))
                    cp(gate[:], bank(2 * par), ACT.Silu, scale=W_UNSCALE).then_inc(S["silu"], 1)
                    act.wait_ge(S["y"], at(n, 2 * PAIRS, k))
                    src = y1[:] if slot else y0[:, 2 * par:2 * par + 2]
                    cp(y_hi[:, par, slot], src, ACT.Copy).then_inc(S["yhi"], 1)
                    if slot:
                        act.wait_ge(S["sum"], at(n, PAIRS, p))
                        cp(sum_hi[:, 2 * p:2 * p + 2], y1[:], ACT.Copy).then_inc(S["shi"], 1)

                def prologue():
                    split(0)
                    split(1)
                    prep_all(0)
                    for c in [*pair_chunks(0), *pair_chunks(1)]:
                        split(c)

                def prep_all(n):
                    for u in range(2):
                        act.wait_ge(S["xt"], at(n, 2, u))
                        cp(x_hi[:, 2 * u:2 * u + 2], bank(2 + u), ACT.Copy).then_inc(S["xhi"], 1)
                    route_copy(n)
                    for m in range(2):
                        act.wait_ge(S["low"], at(n, 2, m))
                        if m:
                            act.wait_ge(S["am"], at(n, 2, 0))
                        cp(a_hi[:], bank(2 + m), ACT.Copy, scale=W_UNSCALE).then_inc(S["ahi"], 1)

                def body(n, first, nxt):
                    read_out(0, n, 0, first)
                    for p in range(PAIRS):
                        if first:
                            for c in block_chunks(p):
                                split(c)
                        if p + 1 < PAIRS:
                            read_out(0, n, p + 1, first)
                        read_out(1, n, p, first)
                    if nxt:
                        for u in range(2):
                            act.wait_ge(S["xt"], at(n + 1, 2, u))
                            cp(x_hi[:, 2 * u:2 * u + 2], bank(2 + u), ACT.Copy).then_inc(S["xhi"], 1)
                    act.wait_ge(S["masked"], at(n, 3, 2))
                    cp(m_hi[:], m_32[:], ACT.Copy).then_inc(S["mhi"], 1)
                    if nxt:
                        route_copy(n + 1)
                        for m in range(2):
                            act.wait_ge(S["low"], at(n + 1, 2, m))
                            if m:
                                act.wait_ge(S["am"], at(n + 1, 2, 0))
                            cp(a_hi[:], bank(2 + m), ACT.Copy, scale=W_UNSCALE).then_inc(S["ahi"], 1)
                    for u in range(2):
                        act.wait_ge(S["down"], at(n, 2, u))
                        cp(o_t[:, 2 * u:2 * u + 2], bank(DOWN + u), ACT.Copy, scale=W_UNSCALE).then_inc(S["ot"], 1)

                run_blocks(act, prologue, body, lambda: None)

            @block.vector
            def _(dve):
                tt, ts, stt = nc.vector.tensor_tensor, nc.vector.tensor_scalar, nc.vector.scalar_tensor_tensor
                ROUTER = 13

                def spread_e(small):
                    return small.unsqueeze(2).broadcast_to([TR, TT, E])

                def split(c):
                    start, width = CHUNKS[c]
                    dve.wait_ge(S["whi"], c + 1)
                    stt(w_lo[:, start:start + width], stage[:, c % 2, 0:width], W_SCALE,
                        w_hi[:, start:start + width], ALU.mult, ALU.subtract).then_inc(S["wlo"], 1)

                def ln_stats(n):
                    dve.wait_ge(S["rows"], n * 16 + 16)
                    for b in range(TT):
                        nc.vector.bn_stats(stats[:, b], rows[:, b]).then_inc(S["stats"], 1)
                    dve.wait_ge(S["stats"], at(n, TT, TT - 1))
                    tt(mean[:], stats[:, :, 1], stats[:, :, 4], ALU.add)
                    tt(gap[:], stats[:, :, 1], stats[:, :, 4], ALU.subtract)
                    tt(spread[:], stats[:, :, 2], stats[:, :, 5], ALU.add).then_inc(S["moments"], 1)
                    dve.wait_ge(S["moments"], n * 2 + 1)
                    ts(mean[:], mean[:], 0.5, None, ALU.mult)
                    tt(gap[:], gap[:], gap[:], ALU.mult)
                    ts(spread[:], spread[:], 1.0 / D, EPS, ALU.mult, ALU.add).then_inc(S["moments"], 1)
                    dve.wait_ge(S["moments"], n * 2 + 2)
                    stt(var_eps[:], gap[:], 0.25, spread[:], ALU.mult, ALU.add).then_inc(S["var"], 1)

                def ln_rows(n):
                    dve.wait_ge(S["rstd"], n + 1)
                    for b in range(TT):
                        last = ts(rows[:, b], rows[:, b], mean[:, b:b + 1], rstd[:, b:b + 1],
                                  ALU.subtract, ALU.mult)
                    last.then_inc(S["normed"], 1)

                def x_low(n):
                    for u in range(2):
                        dve.wait_ge(S["xhi"], at(n, 2, u))
                        tt(x_lo[:, 2 * u:2 * u + 2], bank(2 + u), x_hi[:, 2 * u:2 * u + 2],
                           ALU.subtract).then_inc(S["xlo"], 1)

                def router(n):
                    count = [0]

                    def link(ins):
                        count[0] += 1
                        ins.then_inc(S["router"], 1)
                        dve.wait_ge(S["router"], at(n, ROUTER, count[0] - 1))

                    dve.wait_ge(S["logits"], n + 1)
                    link(ts(logits[:], ps[0:TR, 0, 0:TT * E].rearrange("p (a e) -> p a e", e=E), W_UNSCALE, None,
                            ALU.mult))
                    link(nc.vector.tensor_reduce(best[:], logits[:], AX.X, ALU.max))
                    link(tt(rank[:], logits[:], spread_e(best[:]), ALU.is_lt))
                    link(stt(rank[:], rank[:], float(E), iota[:], ALU.mult, ALU.add))
                    link(nc.vector.tensor_reduce(first_at[:], rank[:], AX.X, ALU.min))
                    link(tt(route[:, :, 0:E], iota[:], spread_e(first_at[:]), ALU.is_equal))
                    link(stt(logits2[:], route[:, :, 0:E], -BIG, logits[:], ALU.mult, ALU.add))
                    link(nc.vector.tensor_reduce(best2[:], logits2[:], AX.X, ALU.max))
                    tt(drop[:], best2[:], best[:], ALU.subtract).then_inc(S["drop"], 1)
                    link(tt(rank[:], logits2[:], spread_e(best2[:]), ALU.is_lt))
                    link(stt(rank[:], rank[:], float(E), iota[:], ALU.mult, ALU.add))
                    link(nc.vector.tensor_reduce(first_at[:], rank[:], AX.X, ALU.min))
                    tt(route[:, :, E:2 * E], iota[:], spread_e(first_at[:]), ALU.is_equal)
                    dve.wait_ge(S["odds"], n + 1)
                    link(ts(total[:], odds[:], 1.0, None, ALU.add))
                    link(nc.vector.reciprocal(route[:, :, 2 * E], total[:]))
                    tt(route[:, :, 2 * E + 1], odds[:], route[:, :, 2 * E], ALU.mult).then_inc(S["route"], 1)
                    assert count[0] == ROUTER

                def route_low(n):
                    dve.wait_ge(S["rhi"], n + 1)
                    tt(route_lo[:], ps[0:32, 1, 0:T], route_hi[:], ALU.subtract).then_inc(S["rlo"], 1)

                def mask_low_rank(n):
                    dve.wait_ge(S["exp_act"], at(n, 2, 1))
                    for m in range(2):
                        dve.wait_ge(S["ahi"], at(n, 2, m))
                        stt(a_lo[:], bank(2 + m), W_UNSCALE, a_hi[:], ALU.mult, ALU.subtract).then_inc(S["alo"], 1)
                        dve.wait_ge(S["alo"], at(n, 2, m))
                        for slot in range(2):
                            tt(am_hi[:, slot, m], a_hi[:], mask[:, 2 * slot], ALU.mult)
                            last = tt(am_lo[:, slot, m], a_lo[:], mask[:, 2 * slot], ALU.mult)
                        last.then_inc(S["am"], 1)

                def read_out(slot, n, p, first):
                    par = p % 2
                    k = turn(slot, p)
                    dve.wait_ge(S["silu"], at(n, 2 * PAIRS, k))
                    tt(gate[:], gate[:], weight[:, slot].unsqueeze(1).broadcast_to([P, 2, T]),
                       ALU.mult).then_inc(S["scaled"], 1)
                    dve.wait_ge(S["scaled"], at(n, 2 * PAIRS, k))
                    dst = y1[:] if slot else y0[:, 2 * par:2 * par + 2]
                    if slot == 0 and p < 2 and not first:
                        dve.wait_ge(S["turned"], at(n - 1, 2, 1))
                    stt(dst, bank(2 * par + 1), W_UNSCALE, gate[:], ALU.mult, ALU.mult).then_inc(S["y"], 1)
                    dve.wait_ge(S["yhi"], at(n, 2 * PAIRS, k))
                    tt(y_lo[:, par, slot], dst, y_hi[:, par, slot], ALU.subtract).then_inc(S["ylo"], 1)
                    if slot:
                        tt(y1[:], y1[:], y0[:, 2 * par:2 * par + 2], ALU.add).then_inc(S["sum"], 1)
                        dve.wait_ge(S["shi"], at(n, PAIRS, p))
                        tt(sum_lo[:, 2 * p:2 * p + 2], y1[:], sum_hi[:, 2 * p:2 * p + 2],
                           ALU.subtract).then_inc(S["slo"], 1)

                def masked(n):
                    dve.wait_ge(S["acc1"], n + 1)
                    stt(m_32[:], bank(A2), W_UNSCALE, mask[:, 0], ALU.mult, ALU.mult)
                    stt(gate[:], bank(A2 + 1), W_UNSCALE, mask[:, 1], ALU.mult, ALU.mult).then_inc(S["masked"], 2)
                    dve.wait_ge(S["masked"], at(n, 3, 1))
                    tt(m_32[:], m_32[:], gate[:], ALU.add).then_inc(S["masked"], 1)
                    dve.wait_ge(S["mhi"], n + 1)
                    tt(m_lo[:], m_32[:], m_hi[:], ALU.subtract).then_inc(S["mlo"], 1)

                def add_rows(n):
                    dve.wait_ge(S["resid"], n * 16 + 16)
                    for u in range(TT):
                        dve.wait_ge(S["turned"], at(n, 2, u))
                        tt(resid[:, u], ps[0:TR, DOWN + u, :], resid[:, u], ALU.add).then_inc(S["added"], 1)

                def prologue():
                    dve.wait_ge(S["const"], 48)
                    dve.wait_ge(S["ones"], 1)
                    ln_stats(0)
                    ln_rows(0)
                    split(0)
                    split(1)
                    x_low(0)
                    router(0)
                    route_low(0)
                    mask_low_rank(0)
                    for c in [*pair_chunks(0), *pair_chunks(1)]:
                        split(c)

                def body(n, first, nxt):
                    read_out(0, n, 0, first)
                    if not first:
                        add_rows(n - 1)
                    for p in range(PAIRS):
                        if first:
                            for c in block_chunks(p):
                                split(c)
                        if p + 1 < PAIRS:
                            read_out(0, n, p + 1, first)
                        read_out(1, n, p, first)
                        if nxt and p == 1:
                            ln_stats(n + 1)
                        if nxt and p == 3:
                            ln_rows(n + 1)
                    if nxt:
                        x_low(n + 1)
                    masked(n)
                    if nxt:
                        router(n + 1)
                        route_low(n + 1)
                        mask_low_rank(n + 1)

                run_blocks(dve, prologue, body, lambda: add_rows(BLOCKS - 1))

            @block.tensor
            def _(pe):
                mm = nc.tensor.matmul

                def weight_pair(at_col):
                    return w_hi[:, at_col:at_col + P], w_lo[:, at_col:at_col + P]

                def triple(out_ap, col, x, xl, start, stop, skip=False):
                    hi, lo = weight_pair(col)
                    mm(out_ap, hi, x, start=start, stop=False, skip_group_check=skip)
                    mm(out_ap, hi, xl, start=False, stop=False, skip_group_check=skip)
                    return mm(out_ap, lo, x, start=False, stop=stop, skip_group_check=skip)

                def base(n, p, first):
                    par = p % 2
                    if first:
                        pe.wait_ge(S["wlo"], 2 + 4 * (p + 1))
                    if p >= 2:
                        pe.wait_ge(S["y"], at(n, 2 * PAIRS, turn(1, p - 2)))
                    for m in range(2):
                        for j in range(2):
                            for k in range(KT):
                                last = triple(bank(2 * par + m)[:, j], w1(m, p, k, j), x_hi[:, k], x_lo[:, k],
                                              j == 0 and k == 0, False)
                            for k in range(ET):
                                last = triple(bank(2 * par + m)[:, j], b1(m, p, k, j), am_hi[:, 0, m, k],
                                              am_lo[:, 0, m, k], False, j == 1 and k == ET - 1)
                    last.then_inc(S["first"], 1)

                def delta(n, p):
                    par = p % 2
                    pe.wait_ge(S["y"], at(n, 2 * PAIRS, turn(0, p)))
                    for m in range(2):
                        for j in range(2):
                            for k in range(ET):
                                last = triple(bank(2 * par + m)[:, j], b1(m, p, k, j), am_hi[:, 1, m, k],
                                              am_lo[:, 1, m, k], False, False, skip=True)
                    last.then_inc(S["second"], 1)

                def down_low(n, p, slot):
                    par = p % 2
                    pe.wait_ge(S["ylo"], at(n, 2 * PAIRS, turn(slot, p)))
                    for t in range(ET):
                        for j in range(2):
                            last = triple(bank(A2 + slot)[:, t], a2(p, j, t), y_hi[:, par, slot, j],
                                          y_lo[:, par, slot, j], p == 0 and t == 0 and j == 0,
                                          p == PAIRS - 1 and t == ET - 1 and j == 1)
                    if p == PAIRS - 1:
                        last.then_inc(S[f"acc{slot}"], 1)

                def down(h, fs):
                    for f in fs:
                        triple(bank(DOWN + h // 2)[:, h % 2], W2_AT + f * D + h * P, sum_hi[:, f], sum_lo[:, f],
                               f == 0 and h % 2 == 0, False)

                def turn_rows(n):
                    pe.wait_ge(S["normed"], n + 1)
                    for u in range(2):
                        for k in (2 * u, 2 * u + 1):
                            for b in range(TT):
                                last = nc.tensor.transpose(bank(2 + u)[:, k % 2, b * TR:(b + 1) * TR],
                                                           rows[:, b, k * P:(k + 1) * P], eye32[0:TR, 0:TR])
                        last.then_inc(S["xt"], 1)

                def logit(n):
                    pe.wait_ge(S["xlo"], at(n, 2, 1))
                    for b in range(TT):
                        for k in range(KT):
                            c = 2 * KT * ER + k * E
                            xs = slice(b * TR, (b + 1) * TR)
                            o = ps[0:TR, 0, b * E:(b + 1) * E]
                            mm(o, x_hi[:, k, xs], w_hi[:, c:c + E], start=k == 0, stop=False)
                            mm(o, x_hi[:, k, xs], w_lo[:, c:c + E], start=False, stop=False)
                            last = mm(o, x_lo[:, k, xs], w_hi[:, c:c + E], start=False, stop=k == KT - 1)
                    last.then_inc(S["logits"], 1)

                def low_rank(n):
                    for m in range(2):
                        for t in range(ET):
                            for k in range(KT):
                                last = triple(bank(2 + m)[:, t], a1(m, k, t), x_hi[:, k], x_lo[:, k],
                                              t == 0 and k == 0, t == ET - 1 and k == KT - 1)
                        last.then_inc(S["low"], 1)

                def turn_route(n):
                    pe.wait_ge(S["route"], n + 1)
                    for b in range(TT):
                        last = nc.tensor.transpose(ps[0:32, 1, b * TR:(b + 1) * TR], route[:, b],
                                                   eye32[0:TR, 0:TR])
                    last.then_inc(S["rt"], 1)

                def expand(n):
                    pe.wait_ge(S["rlo"], n + 1)
                    for m, b in enumerate((0, 1, 4, 5)):
                        for t in range(2):
                            o = bank(b)[:, t]
                            s = select[:, 2 * m + t]
                            if m < 3:
                                last = mm(o, s, route_hi[:], start=t == 0, stop=t == 1)
                            else:
                                mm(o, s, route_hi[:], start=t == 0, stop=False)
                                last = mm(o, s, route_lo[:], start=False, stop=t == 1)
                        last.then_inc(S["expand"], 1)

                def turn_out(n):
                    for u in range(TT):
                        pe.wait_ge(S["ot"], at(n, 2, 1))
                        for k in range(KT):
                            last = nc.tensor.transpose(ps[0:TR, DOWN + u, k * P:(k + 1) * P],
                                                       o_t[:, k, u * TR:(u + 1) * TR], eye32[:])
                        last.then_inc(S["turned"], 1)

                def prologue():
                    pe.wait_ge(S["const"], 48)
                    turn_rows(0)
                    pe.wait_ge(S["wlo"], 2)
                    logit(0)
                    low_rank(0)
                    turn_route(0)
                    expand(0)

                def body(n, first, nxt):
                    pe.wait_ge(S["am"], at(n, 2, 1))
                    base(n, 0, first)
                    if not first:
                        turn_out(n - 1)
                    for p in range(PAIRS):
                        if p + 1 < PAIRS:
                            base(n, p + 1, first)
                        delta(n, p)
                        down_low(n, p, 0)
                        if p:
                            down_low(n, p - 1, 1)
                    if nxt:
                        pe.wait_ge(S["y"], at(n, 2 * PAIRS, turn(1, PAIRS - 2)))
                        turn_rows(n + 1)
                    if first:
                        pe.wait_ge(S["wlo"], len(CHUNKS))
                    if not first:
                        pe.wait_ge(S["added"], at(n - 1, 2, 1))
                    pe.wait_ge(S["slo"], at(n, PAIRS, PAIRS - 2))
                    down(0, range(0, FT - 2))
                    down(1, range(0, FT - 2))
                    pe.wait_ge(S["ylo"], at(n, 2 * PAIRS, turn(1, PAIRS - 1)))
                    down_low(n, PAIRS - 1, 1)
                    pe.wait_ge(S["slo"], at(n, PAIRS, PAIRS - 1))
                    if nxt:
                        logit(n + 1)
                        low_rank(n + 1)
                    down(0, range(FT - 2, FT))
                    down(1, range(FT - 2, FT))
                    down(2, range(0, FT // 2))
                    if nxt:
                        turn_route(n + 1)
                    down(2, range(FT // 2, FT))
                    if nxt:
                        expand(n + 1)
                    down(3, range(0, FT))
                    pe.wait_ge(S["mlo"], n + 1)
                    for h in range(KT):
                        for t in range(ET):
                            last = triple(bank(DOWN + h // 2)[:, h % 2], B2_AT + t * D + h * P, m_hi[:, t], m_lo[:, t],
                                          False, h % 2 == 1 and t == ET - 1)
                        if h % 2:
                            last.then_inc(S["down"], 1)

                run_blocks(pe, prologue, body, lambda: turn_out(BLOCKS - 1))


def build(nc, spectra, kry_b, readout, log_dt, cls_rows, eye32, eye16, two_eye, half_eye, ones16, ones32,
          w_attn, b_attn, eye_bf, causal,
          w_ffn, iota, select, out):
    tokens = nc.dram_tensor("tokens", (64, 65, 512), F32, kind="Internal").ap()
    tokenizer_phase(nc, spectra, kry_b, readout, log_dt, cls_rows,
                    (eye32, eye16, two_eye, half_eye, ones16, ones32), tokens)
    mixed = nc.dram_tensor("mixed", (64, 65, 512), F32, kind="Internal").ap()
    attention_phase(nc, w_attn, b_attn, (eye32, eye_bf, causal), tokens, mixed)
    expert_phase(nc, w_ffn, (eye32, iota, select), mixed.rearrange("b s d -> (b s) d"),
                 out.rearrange("b s d -> (b s) d"))


def kernel(**inputs):
    import ml_dtypes
    import numpy as np
    import concourse.bacc as bacc
    from concourse.bass_utils import run_bass_kernel_spmd as run
    a = {k: np.asarray(v) for k, v in inputs.items()}
    A = a["L0_tok_A"]
    re, im = A[..., 0].transpose(2, 0, 1), A[..., 1].transpose(2, 0, 1)
    at = [a["L0_attn_W" + n] for n in "qkvo"]
    ab = [a["L0_attn_b" + n] for n in "qkvo"]
    mask = np.where(np.arange(65)[None, :] > np.arange(65)[:, None], -1e30, 0.0).astype(ml_dtypes.bfloat16)

    def tiles(w):
        return w.reshape(-1, 128, w.shape[1]).transpose(1, 0, 2)

    f = {n: a["L0_ffn_" + n] for n in ("Wg", "W1", "W2", "W3", "A1", "A2", "A3", "B1", "B2", "B3")}
    low = {n: tiles(f[n].reshape(256, -1).T) for n in ("A1", "A2", "A3")}
    high = {n: tiles(f[n].transpose(0, 2, 1).reshape(256, -1)) for n in ("B1", "B2", "B3")}
    up = {n: tiles(f[n].T) for n in ("W1", "W2", "W3", "Wg")}
    cols = [low["A1"], low["A3"], up["Wg"]]
    for p in range(7):
        part = slice(256 * p, 256 * p + 256)
        cols += [up["W1"][:, :, part], up["W3"][:, :, part], high["B1"][:, :, part], high["B3"][:, :, part],
                 low["A2"][:, 2 * p:2 * p + 2]]
    cols += [up["W2"], high["B2"]]
    select = np.zeros((32, 8, 128), np.float16)
    for t in range(2):
        for p in range(128):
            e = 4 * t + p // 32
            select[e, t, p] = 1
            select[8 + e, 2 + t, p] = 1
            select[8 + e, 4 + t, p] = 1
            select[e, 4 + t, p] = -1
            select[16 + t, 6 + t, p] = 1
    arrays = {
        "spectra": np.concatenate([np.concatenate([re, im], 2), np.concatenate([im, re], 2)], 0),
        "kry_b": a["L0_tok_B"].transpose(2, 1, 0).reshape(128, 64),
        "readout": a["x"].transpose(3, 2, 1, 0).reshape(128, 64, 64),
        "log_dt": np.broadcast_to(a["L0_tok_log_dt"].reshape(1, 64), (128, 64)),
        "cls_rows": np.broadcast_to(a["cls_tok"].reshape(1, 512), (64, 512)),
        "eye32": np.eye(128, dtype=np.float32),
        "eye16": np.eye(128, dtype=np.float16),
        "two_eye": np.tile(2 * np.eye(128, dtype=np.float16), (1, 4)),
        "half_eye": np.tile(-0.5 * np.eye(128, dtype=np.float16), (1, 4)),
        "ones16": np.ones((128, 128), np.float16),
        "ones32": np.ones((128, 128), np.float32),
        "w_attn": np.stack([w.T.reshape(4, 128, 512).transpose(1, 0, 2) for w in at]),
        "b_attn": np.stack([b.reshape(4, 128).T for b in ab], 1),
        "eye_bf": np.eye(65).astype(ml_dtypes.bfloat16),
        "causal": np.tile(mask, (1, 4)),
        "w_ffn": np.concatenate([c.reshape(128, -1) for c in cols], 1),
        "iota": np.broadcast_to(np.arange(8, dtype=np.float32), (104, 2, 8)),
        "select": select,
    }
    nc = bacc.Bacc("TRN2", target_bir_lowering=False, num_devices=1)
    feeds, aps = {}, []
    for name, v in arrays.items():
        v = np.ascontiguousarray(v)
        feeds["in_" + name] = v
        aps.append(nc.dram_tensor("in_" + name, v.shape, mybir.dt.from_np(v.dtype), kind="ExternalInput").ap())
    aps.append(nc.dram_tensor("out", (64, 65, 512), F32, kind="ExternalOutput").ap())
    build(nc, *aps)
    return run(nc, [feeds], core_ids=[0]).results[0]["out"]
```

```python
from contextlib import ExitStack

import concourse.bass as bass
from concourse import mybir

F32 = mybir.dt.float32
F16 = mybir.dt.float16
BF16 = mybir.dt.bfloat16
ACT = mybir.ActivationFunctionType
ALU = mybir.AluOpType
AX = mybir.AxisListType
P = 128
W_SCALE = 64.0
W_UNSCALE = 1.0 / W_SCALE


def tokenizer_phase(nc, arena, attn_w, attn_pair, spectra, kry_b, readout, log_dt, cls_rows, consts, tokens):
    eye32_d, eye16_d, two_eye_d, half_eye_d, ones16_d, ones32_d = consts
    H = spectra.shape[1]
    CHANNELS = readout.shape[2]
    L = tokens.shape[2]
    CHAINS, CH = 4, 4
    SET = CHAINS * CH
    SETS = H // SET
    COARSE = 5
    EXACT = 2
    LEVELS = L.bit_length() - 1

    with ExitStack() as ctx:
        def sb(name, shape, dt):
            return ctx.enter_context(nc.sbuf_tensor(name, shape, dt))

        def sem(name):
            return ctx.enter_context(nc.semaphore(name))

        raw = sb("raw", [P, SET, P], F32)
        minus_back = sb("minus_back", [P, SET, P], F32)
        minus_back16 = sb("minus_back16", [P, SET, P], F16)
        inv16 = sb("inv16", [P, SET, P], F16)
        corr16 = sb("corr16", [P, SET, P], F16)
        inv32 = sb("inv32", [P, SET, P], F32)
        corr32 = sb("corr32", [P, SET, P], F32)
        wide = sb("wide", [P, SET, P + L], F32)
        power, krylov = wide[:, :, 0:P], wide[:, :, P:P + L]
        power_t = arena[:, 0:SET * P].rearrange("p (h m) -> p h m", m=P)
        read_t = sb("read_t", [P, SET, CHANNELS], F32)
        rows = arena[0:CHANNELS, SET * P:SET * (P + L)].rearrange("p (h l) -> p h l", l=L)
        attn_stage = sb("attn_stage", [P, 4, 512], F32)
        attn_hi, attn_lo = attn_pair
        half_dt = sb("half_dt", [P, H], F32)
        drive = sb("drive", [P, H], F32)
        row_sum = sb("row_sum", [P, SET], F32)
        col_max = sb("col_max", [P, SET], F32)
        row_max = sb("row_max", [SET, 1], F32)
        row_diag = sb("row_diag", [SET, SET], F32)
        alpha = sb("alpha", [P, SET], F32)
        eye32 = sb("eye32", [P, P], F32)
        eye16 = sb("eye16", [P, P], F16)
        two_eye = sb("two_eye", [P, CH * P], F16)
        half_eye = sb("half_eye", [P, CH * P], F16)
        ones16 = sb("ones16", [P, P], F16)
        ones32 = sb("ones32", [P, P], F32)
        ps = ctx.enter_context(nc.psum_tensor("ps_tok", [P, 8, 512], F32))

        s_const = sem("a_const")
        s_dt = sem("a_dt")
        s_raw = sem("a_raw_loaded")
        s_read = sem("a_readout_loaded")
        s_stored = sem("a_rows_stored")
        s_cls = sem("a_cls_stored")
        s_dve = sem("a_dve_chain")
        s_rawfree = sem("a_raw_consumed")
        s_back = sem("a_back_ready")
        s_abs = sem("a_abs_ready")
        s_norm = sem("a_norms")
        s_diag = sem("a_diag")
        s_bcast = sem("a_bcast")
        s_start = sem("a_start_ready")
        s_neg = sem("a_readout_signed")
        s_pe = sem("a_products")
        s_act = sem("a_act_copied")
        s_vec = sem("a_dve_copied")
        s_attn = sem("a_attn_weight_loaded")
        s_ahi = sem("a_attn_high")
        s_alo = sem("a_attn_low")

        rounds = []
        for n in range(COARSE):
            rounds += [("corr16", n), ("inv16", n)]
        for n in range(EXACT):
            rounds += [("corr32", n), ("inv32", n)]
        rounds += [("transpose", -1), ("seed", 0)]
        for k in range(LEVELS - 1):
            rounds += [("square", k), ("transpose", k)]
        rounds += [("last_double", LEVELS - 1), ("read", 0), ("read", 1)]
        R = len(rounds)
        SPLITS = (3, 4, 5, 6)

        def bank(g, n):
            return ps[:, 2 * g + n, :]

        def bank4(g, n, m=P):
            return ps[:, 2 * g + n, 0:CH * m].rearrange("p (h m) -> p h m", m=m)

        def pairs(g, lo, hi):
            return ps[:, 2 * g:2 * g + 2, :].rearrange("p b (h m) -> p b h m", h=2)[:, :, :, lo:hi]

        def chain2(t, g):
            return chain(t, g).rearrange("p (b h) m -> p b h m", b=2)

        def chain(t, g):
            return t[:, CH * g:CH * g + CH, :]

        def copies(kind, k, g):
            if kind == "corr16":
                return [(chain(corr16, g), bank4(g, 0), 1.0)]
            if kind == "inv16":
                return [(chain(inv32 if k == COARSE - 1 else inv16, g), bank4(g, 1), 1.0)]
            if kind == "corr32":
                return [(chain(corr32, g), bank4(g, 0), 1.0)]
            if kind == "inv32":
                if k == EXACT - 1:
                    return [(chain(power, g), bank4(g, 1), 2.0)]
                return [(chain(inv32, g), bank4(g, 1), 1.0)]
            if kind == "transpose":
                return [(chain(power_t, g), bank4(g, 0), 1.0)]
            if kind == "seed":
                return [(krylov[:, CH * g:CH * g + CH, 0:1], bank4(g, 1, 1), 1.0)]
            if kind == "square":
                n = 1 << k
                return [(chain2(power, g), pairs(g, 0, P), 1.0),
                        (chain2(krylov[:, :, n:2 * n], g), pairs(g, P, P + n), 1.0)]
            if kind == "last_double":
                n = 1 << k
                return [(krylov[:, CH * g + 2 * m:CH * g + 2 * m + 2, n:2 * n],
                         bank(g, m).rearrange("p (h l) -> p h l", h=2), 1.0) for m in range(2)]
            return [(rows[:, CH * g + 2 * k + m, :], bank(g, m)[0:CHANNELS], 1.0) for m in range(2)]

        with nc.Block() as block:

            @block.sync
            def _(sp):
                for dst, src in ((eye32, eye32_d), (eye16, eye16_d), (two_eye, two_eye_d),
                                 (half_eye, half_eye_d), (ones16, ones16_d), (ones32, ones32_d)):
                    sp.dma_start(dst[:], src).then_inc(s_const, 16)
                sp.dma_start(half_dt[:], log_dt).then_inc(s_dt, 16)
                sp.dma_start(drive[:], kry_b).then_inc(s_dt, 16)
                sp.dma_start(raw[:], spectra[:, 0:SET, :]).then_inc(s_raw, 16)
                sp.dma_start(read_t[:], readout[:, 0:SET, :]).then_inc(s_read, 16)
                sp.dma_start(tokens[:, 0, :], cls_rows).then_inc(s_cls, 16)

                sp.dma_start(attn_stage[:], attn_w[0]).then_inc(s_attn, 16)

                def store(i):
                    sp.wait_ge(s_act, (i + 1) * 2 * R)
                    sp.wait_ge(s_vec, (i + 1) * 2 * R)
                    sp.dma_start(tokens[:, bass.ds(i * SET + 1, SET), :], rows).then_inc(s_stored, 16)

                with sp.Fori(0, SETS - 1) as i:
                    sp.wait_ge(s_rawfree, i + 1)
                    sp.dma_start(raw[:], spectra[:, bass.ds((i + 1) * SET, SET), :]).then_inc(s_raw, 16)
                    sp.wait_ge(s_ahi, i * 4 + 4)
                    sp.wait_ge(s_alo, i * 4 + 4)
                    sp.dma_start(attn_stage[:], attn_w[bass.ds(i + 1, 1)].rearrange("a p k d -> p (a k) d")).then_inc(s_attn, 16)
                    store(i)
                    sp.dma_start(read_t[:], readout[:, bass.ds((i + 1) * SET, SET), :]).then_inc(s_read, 16)
                store(SETS - 1)
                sp.wait_ge(s_stored, 16 * SETS)
                sp.wait_ge(s_cls, 16)

            @block.scalar
            def _(act):
                def copy(out, src, scale):
                    return nc.scalar.activation(out, src, ACT.Copy, scale=scale)

                act.wait_ge(s_dt, 32)
                nc.scalar.activation(half_dt[:], half_dt[:], ACT.Exp).then_inc(s_dt, 1)

                def one_set(i, first):
                    act.wait_ge(s_back, i + 1)
                    nc.scalar.activation(corr16[:], minus_back[:], ACT.Abs)
                    nc.scalar.activation(minus_back16[:], minus_back[:], ACT.Copy).then_inc(s_abs, 1)
                    for s, (kind, k) in enumerate(rounds):
                        for g in (0, 2):
                            act.wait_ge(s_pe, i * (4 * R) + (4 * s + g + 1))
                            if kind == "read" and k == 0 and not first:
                                act.wait_ge(s_stored, i * 16)
                            for out, src, scale in copies(kind, k, g):
                                last = copy(out, src, scale)
                            last.then_inc(s_act, 1)
                        if kind == "square" and k in SPLITS:
                            r = SPLITS.index(k)
                            if r == 0:
                                act.wait_ge(s_attn, i * 16 + 16)
                            nc.scalar.activation(attn_hi[:, bass.ds(i, 1), r], attn_stage[:, r:r + 1], ACT.Copy,
                                                 scale=W_SCALE).then_inc(s_ahi, 1)

                one_set(0, True)
                with act.Fori(1, SETS) as i:
                    one_set(i, False)

            @block.vector
            def _(dve):
                def copy(out, src, scale):
                    if scale == 1.0:
                        return nc.vector.tensor_copy(out, src)
                    return nc.vector.tensor_scalar(out, src, scale, None, ALU.mult)

                dve.wait_ge(s_const, 16 * 6)
                dve.wait_ge(s_dt, 33)
                nc.vector.tensor_scalar(half_dt[:], half_dt[:], 0.5, None, ALU.mult).then_inc(s_dve, 1)
                dve.wait_ge(s_dve, 1)
                nc.vector.tensor_tensor(drive[:], drive[:], half_dt[:], ALU.mult).then_inc(s_dve, 1)
                dve.wait_ge(s_dve, 2)
                LINKS = 5

                def one_set(i, first):
                    count = [0]

                    def link(ins):
                        count[0] += 1
                        ins.then_inc(s_dve, 1)
                        dve.wait_ge(s_dve, i * LINKS + (count[0] + 2))

                    dve.wait_ge(s_raw, (i + 1) * 16)
                    dt_set = half_dt[:, bass.ds(i * SET, SET)]
                    nc.vector.tensor_tensor(minus_back[:], raw[:], dt_set.unsqueeze(2).broadcast_to([P, SET, P]),
                                            ALU.mult).then_inc(s_rawfree, 1)
                    dve.wait_ge(s_rawfree, i + 1)
                    link(nc.vector.tensor_scalar(minus_back[64:P, :, 0:64], minus_back[64:P, :, 0:64], -1.0, None,
                                                 ALU.mult))
                    nc.vector.tensor_tensor(minus_back[:], minus_back[:],
                                            eye32[:].unsqueeze(1).broadcast_to([P, SET, P]),
                                            ALU.subtract).then_inc(s_back, 1)
                    dve.wait_ge(s_back, i + 1)
                    nc.vector.tensor_reduce(row_sum[:], minus_back[:], AX.X, ALU.add,
                                            apply_absolute_value=True).then_inc(s_norm, 1)
                    dve.wait_ge(s_read, (i + 1) * 16)
                    nc.vector.tensor_scalar(read_t[64:P], read_t[64:P], -1.0, None, ALU.mult).then_inc(s_neg, 1)
                    dve.wait_ge(s_diag, 2 * i + 1)
                    nc.vector.tensor_reduce(col_max[:], ps[:, 0:8:2, :].rearrange("p b (h m) -> p b h m", m=P),
                                            AX.X, ALU.max)
                    link(nc.vector.tensor_reduce(row_max[:], ps[0:SET, 1, 0:P], AX.X, ALU.max))
                    nc.vector.tensor_scalar(row_diag[:], eye32[0:SET, 0:SET], row_max[:, 0:1], None,
                                            ALU.mult).then_inc(s_bcast, 1)
                    dve.wait_ge(s_diag, 2 * i + 2)
                    link(nc.vector.tensor_tensor(alpha[:], col_max[:], ps[:, 3, 0:SET], ALU.mult))
                    link(nc.vector.reciprocal(alpha[:], alpha[:]))
                    link(nc.vector.tensor_scalar(alpha[:], alpha[:], -1.0, None, ALU.mult))
                    nc.vector.tensor_tensor(inv16[:], minus_back[:],
                                            alpha[:].unsqueeze(2).broadcast_to([P, SET, P]),
                                            ALU.mult).then_inc(s_start, 1)
                    for s, (kind, k) in enumerate(rounds):
                        for g in (1, 3):
                            dve.wait_ge(s_pe, i * (4 * R) + (4 * s + g + 1))
                            if kind == "read" and k == 0 and not first:
                                dve.wait_ge(s_stored, i * 16)
                            for out, src, scale in copies(kind, k, g):
                                last = copy(out, src, scale)
                            last.then_inc(s_vec, 1)
                        if kind == "square" and k - 1 in SPLITS:
                            r = SPLITS.index(k - 1)
                            dve.wait_ge(s_ahi, i * 4 + (r + 1))
                            nc.vector.scalar_tensor_tensor(attn_lo[:, bass.ds(i, 1), r], attn_stage[:, r:r + 1],
                                                           W_SCALE, attn_hi[:, bass.ds(i, 1), r],
                                                           ALU.mult, ALU.subtract).then_inc(s_alo, 1)
                    assert count[0] == LINKS

                one_set(0, True)
                with dve.Fori(1, SETS) as i:
                    one_set(i, False)

            @block.tensor
            def _(pe):
                mm = nc.tensor.matmul
                pe.wait_ge(s_const, 16 * 6)

                def one_set(i, first):
                    pe.wait_ge(s_abs, i + 1)
                    pe.wait_ge(s_norm, i + 1)
                    if not first:
                        pe.wait_ge(s_act, i * (2 * R))
                        pe.wait_ge(s_vec, i * (2 * R))
                    for g in range(CHAINS):
                        mm(bank(g, 0), ones16[:], chain(corr16, g), start=True, stop=True)
                    nc.tensor.transpose(ps[0:SET, 1, 0:P], row_sum[:], eye32[:]).then_inc(s_diag, 1)
                    pe.wait_ge(s_bcast, i + 1)
                    mm(ps[:, 3, 0:SET], ones32[0:SET, :], row_diag[:], start=True, stop=True).then_inc(s_diag, 1)
                    pe.wait_ge(s_start, i + 1)
                    pe.wait_ge(s_neg, i + 1)
                    for s, (kind, k) in enumerate(rounds):
                        for g in range(CHAINS):
                            if s:
                                pe.wait_ge(s_vec if g % 2 else s_act, i * (2 * R) + (2 * (s - 1) + g // 2 + 1))
                            hs = range(CH * g, CH * g + CH)
                            if kind in ("corr16", "corr32"):
                                x, b = (inv16, minus_back16) if kind == "corr16" else (inv32, minus_back)
                                mm(bank(g, 0), eye16[:], two_eye[:], start=True, stop=False)
                                for j, h in enumerate(hs):
                                    last = mm(bank4(g, 0)[:, j], x[:, h], b[:, h], start=False, stop=j == CH - 1)
                            elif kind in ("inv16", "inv32"):
                                x, c = (inv16, corr16) if kind == "inv16" else (inv32, corr32)
                                final = kind == "inv32" and k == EXACT - 1
                                if final:
                                    mm(bank(g, 1), eye16[:], half_eye[:], start=True, stop=False)
                                for j, h in enumerate(hs):
                                    last = mm(bank4(g, 1)[:, j], c[:, h], x[:, h], start=not final, stop=not final or j == CH - 1)
                            elif kind == "transpose":
                                for j, h in enumerate(hs):
                                    last = nc.tensor.transpose(bank4(g, 0)[:, j], power[:, h], eye32[:])
                            elif kind == "seed":
                                b = drive[:, bass.ds(i * SET + CH * g, CH)]
                                mm(bank(g, 1)[:, 0:CH], eye32[:], b, start=True, stop=False)
                                for j, h in enumerate(hs):
                                    last = mm(bank(g, 1)[:, j:j + 1], power_t[:, h],
                                              drive[:, bass.ds(i * SET + h, 1)], start=False, stop=j == CH - 1)
                            elif kind == "square":
                                n = 1 << k
                                for j, h in enumerate(hs):
                                    last = mm(pairs(g, 0, P + n)[:, j // 2, j % 2], power_t[:, h], wide[:, h, 0:P + n],
                                              start=True, stop=True)
                            elif kind == "last_double":
                                n = 1 << k
                                for j, h in enumerate(hs):
                                    last = mm(bank(g, j // 2)[:, (j % 2) * n:(j % 2 + 1) * n], power_t[:, h],
                                              krylov[:, h, 0:n], start=True, stop=True)
                            else:
                                for m in range(2):
                                    h = CH * g + 2 * k + m
                                    last = mm(bank(g, m)[0:CHANNELS], read_t[:, h], krylov[:, h, :], start=True,
                                              stop=True)
                            last.then_inc(s_pe, 1)

                one_set(0, True)
                with pe.Fori(1, SETS) as i:
                    one_set(i, False)


def attention_phase(nc, attn_pair, ffn_w, ffn_pair, biases, consts, tokens, mixed):
    eye32_d, eye_bf_d, causal_d, own_head_d = consts
    IMAGES, S, D = tokens.shape
    HEADS, DK = 16, 32
    QB = 4
    QUADS = IMAGES // QB
    T = QB * S
    KT = D // P
    G = P // DK
    HB = HEADS // 2
    V1 = DK + 1
    EPS = 1e-5

    with ExitStack() as ctx:
        def sb(name, shape, dt):
            return ctx.enter_context(nc.sbuf_tensor(name, shape, dt))

        def sem(name):
            return ctx.enter_context(nc.semaphore(name))

        w_hi, w_lo = attn_pair
        f_hi, f_lo = ffn_pair
        PART = f_hi.shape[1] // QUADS
        stage = sb("b_stage", [P, PART], F32)
        bias = sb("bias", [P, 4, KT], F32)
        eye32 = sb("b_eye32", [P, P], F32)
        own_head = sb("own_head", [P, G], F32)
        eye_bf = sb("b_eye_bf", [S, S], BF16)
        causal = sb("causal", [S, KT * S], BF16)
        rows = sb("b_rows", [S, QB, D], F32)
        normed = sb("b_normed", [S, QB, D], F32)
        stats = sb("b_stats", [S, QB, 6], F32)
        mean = sb("b_mean", [S, QB], F32)
        gap = sb("b_gap", [S, QB], F32)
        spread = sb("b_spread", [S, QB], F32)
        var_eps = sb("b_var_eps", [S, QB], F32)
        rstd = sb("b_rstd", [S, QB], F32)
        minus_half = sb("b_minus_half", [S, QB], F32)
        x_hi = sb("b_x_hi", [P, 2, KT, T], F16)
        x_lo = sb("b_x_lo", [P, 2, KT, T], F16)
        q_t = sb("q_t", [P, 2, KT, T], F32)
        k_t = sb("k_t", [P, 2, KT, T], F32)
        k_diag = sb("k_diag", [P, KT, G, S], F32)
        v_t = sb("v_t", [P, KT, T], F32)
        v_rows = sb("v_rows", [S, 2, QB, HEADS, V1], F32)
        top = sb("top", [S, KT, G], F32)
        probs = sb("probs", [S, KT, G, S], F32)
        probs_t = sb("probs_t", [S, KT, G, S], F32)
        recip = sb("recip", [S, HEADS], F32)
        context = sb("context", [S, QB, HEADS, DK], F32)
        c_hi = sb("c_hi", [P, KT, T], F16)
        c_lo = sb("c_lo", [P, KT, T], F16)
        o_t = sb("o_t", [P, KT, T], F32)
        resid = sb("resid", [S, QB, D], F32)
        ps = ctx.enter_context(nc.psum_tensor("ps_attn", [P, 8, 512], F32))
        SCORES, CTX, WORK = 0, 4, 6

        s_const = sem("b_const")
        s_part = sem("b_ffn_part_loaded")
        s_fhi = sem("b_ffn_high")
        s_flo = sem("b_ffn_low")
        s_diag = sem("b_key_blocks")
        s_rows = sem("b_rows_loaded")
        s_resid = sem("b_resid_loaded")
        s_stored = sem("b_mixed_stored")
        s_stats = sem("b_stats")
        s_var = sem("b_variance")
        s_rstd = sem("b_rstd")
        s_normed = sem("b_normed")
        s_ones = sem("b_ones")
        s_moments = sem("b_moments")
        s_top = sem("b_maxima")
        s_recip = sem("b_recips")
        s_scores = sem("b_scores")
        s_shift = sem("b_shifted")
        s_exp = sem("b_exponentials")
        s_pt = sem("b_probs_turned")
        s_pt_act = sem("b_probs_t_act")
        s_pt_dve = sem("b_probs_t_dve")
        s_ctx = sem("b_contexts")
        s_norm = sem("b_contexts_normed")
        KINDS = {"xt": "AD", "ct": "AD", "q": "A", "k": "A", "v": "A", "vt": "D", "wo": "A", "ot": "D"}
        s_unit = {k: sem(f"b_{k}_products") for k in KINDS}
        s_copy = {(k, e): sem(f"b_{k}_copied_{e}") for k, es in KINDS.items() for e in es}

        def count(n, j, per):
            return n * per + (j + 1)

        def work(kind):
            return ps[:, WORK + (kind not in ("q", "k", "v", "wo")), :]

        HEAVY = ("q", "k", "v", "wo")
        SLOTS = {}
        for b, (heavy, of, light, light_of) in enumerate((("v", 1, "ct", -1), ("wo", -1, "vt", 1),
                                                          ("q", 1, "ot", -1), ("k", 1, "xt", 2))):
            order = [x for j in range(4) for x in ((heavy, of, j), (light, light_of, j))]
            SLOTS[f"A{b}"] = order[0:5]
            SLOTS[f"B{b}"] = [order[5], order[6], order[7]]

        def units(name, q, prev, nxt, nxt2):
            here = {-1: prev, 1: nxt, 2: nxt2}
            return [(kind, q + of, j) for kind, of, j in SLOTS[name] if here[of]]

        START = [("xt", 0), ("v", 0), ("q", 0), ("vt", 0), ("k", 0), ("xt", 1)]
        FINISH = [("ct", QUADS - 1), ("wo", QUADS - 1), ("ot", QUADS - 1)]

        def whole(kinds):
            return [(kind, n, j) for kind, n in kinds for j in range(4)]

        def run_quads(eng, prologue, quad, epilogue):
            prologue()
            quad(0, 0, False, True, True)
            with eng.Fori(0, (QUADS - 4) // 2) as i:
                quad(i * 2 + 1, 1, True, True, True)
                quad(i * 2 + 2, 0, True, True, True)
            quad(QUADS - 3, 1, True, True, True)
            quad(QUADS - 2, 0, True, True, False)
            quad(QUADS - 1, 1, True, False, False)
            epilogue()

        with nc.Block() as block:

            @block.sync
            def _(sp):
                sp.dma_start(rows[:], tokens[0:QB].rearrange("b s d -> s b d")).then_inc(s_rows, 16)
                sp.dma_start(eye32[:], eye32_d).then_inc(s_const, 16)
                sp.dma_start(eye_bf[:], eye_bf_d).then_inc(s_const, 16)
                sp.dma_start(own_head[:], own_head_d).then_inc(s_const, 16)
                sp.dma_start(causal[:], causal_d).then_inc(s_const, 16)
                sp.dma_start(bias[:], biases).then_inc(s_const, 16)
                sp.dma_start(stage[:], ffn_w[:, 0:PART]).then_inc(s_part, 16)

                def load_part(n):
                    sp.wait_ge(s_fhi, n)
                    sp.wait_ge(s_flo, n)
                    sp.dma_start(stage[:], ffn_w[:, bass.ds(n * PART, PART)]).then_inc(s_part, 16)

                def store(n):
                    sp.wait_ge(s_copy["ot", "D"], count(n, 3, 4))
                    sp.dma_start(mixed[bass.ds(n * QB, QB)].rearrange("b s d -> s b d"), resid[:]).then_inc(s_stored, 16)

                def load_resid(n):
                    sp.dma_start(resid[:], tokens[bass.ds(n * QB, QB)].rearrange("b s d -> s b d")).then_inc(s_resid, 16)

                def load_rows(n):
                    sp.wait_ge(s_normed, count(n - 1, 3, 4))
                    sp.dma_start(rows[:], tokens[bass.ds(n * QB, QB)].rearrange("b s d -> s b d")).then_inc(s_rows, 16)

                load_resid(0)
                load_rows(1)
                load_rows(2)
                load_part(1)
                with sp.Fori(0, QUADS - 3) as n:
                    load_rows(n + 3)
                    store(n)
                    sp.wait_ge(s_stored, n * 16 + 16)
                    load_resid(n + 1)
                    load_part(n + 2)
                for n in range(QUADS - 3, QUADS):
                    store(n)
                    sp.wait_ge(s_stored, n * 16 + 16)
                    if n + 1 < QUADS:
                        load_resid(n + 1)
                    if n + 2 < QUADS:
                        load_part(n + 2)

            @block.gpsimd
            def _(pool):
                nc.gpsimd.memset(minus_half[:], -0.5).then_inc(s_ones, 1)
                nc.gpsimd.memset(v_rows[:, :, :, :, DK:V1], 1.0).then_inc(s_ones, 1)
                pool.wait_ge(s_ones, 1)

                pool.wait_ge(s_const, 80)

                def root(n):
                    pool.wait_ge(s_var, n + 1)
                    nc.gpsimd.tensor_tensor(rstd[:], var_eps[:], minus_half[:], ALU.pow).then_inc(s_rstd, 1)

                def quad(q, par, prev, nxt, nxt2):
                    pool.wait_ge(s_copy["k", "A"], count(q, 3, 4))
                    for b in range(QB):
                        if prev or b:
                            pool.wait_ge(s_scores, count(q, b - 1, QB))
                        keys = k_t[:, par, :, b * S:(b + 1) * S].unsqueeze(2).broadcast_to([P, KT, G, S])
                        mine = own_head[:].unsqueeze(1).unsqueeze(3).broadcast_to([P, KT, G, S])
                        nc.gpsimd.tensor_tensor(k_diag[:], keys, mine, ALU.mult).then_inc(s_diag, 1)
                        if nxt2 and b == 1:
                            root(q + 2)

                def prologue():
                    root(0)
                    root(1)

                run_quads(pool, prologue, quad, lambda: None)

            @block.scalar
            def _(act):
                def copy_unit(kind, n, par, j):
                    act.wait_ge(s_unit[kind], count(n, j, 4))
                    src = work(kind)
                    if kind in ("xt", "ct"):
                        dst = x_hi[:, 1 - par] if kind == "xt" else c_hi
                        ins = nc.scalar.activation(dst[:, j], src[:, 0:T], ACT.Copy)
                    elif kind in ("q", "k", "v"):
                        b = bias[:, "qkv".index(kind), j:j + 1]
                        dst = v_t[:, j] if kind == "v" else (q_t if kind == "q" else k_t)[:, par, j]
                        ins = nc.scalar.activation(dst, src[:, 0:T], ACT.Identity, bias=b,
                                                   scale=W_UNSCALE)
                    else:
                        ins = nc.scalar.activation(o_t[:, j], src[:, 0:T], ACT.Identity, bias=bias[:, 3, j:j + 1],
                                                   scale=W_UNSCALE)
                    ins.then_inc(s_copy[kind, "A"], 1)

                def fill(which, par):
                    for kind, n, j in which:
                        if "A" in KINDS[kind]:
                            copy_unit(kind, n, 1 - par, j)

                def prologue():
                    act.wait_ge(s_const, 80)
                    fill(whole(START[:1]), 0)
                    fill(whole(START[1:]), 1)

                def quad(q, par, prev, nxt, nxt2):
                    for b in range(QB):
                        beside = units(f"A{b}", q, prev, nxt, nxt2)
                        fill(beside[:3], par)
                        act.wait_ge(s_shift, count(q, b, QB))
                        nc.scalar.activation(probs[:], probs[:], ACT.Exp, scale=DK ** -0.5).then_inc(s_exp, 1)
                        fill(beside[3:], par)
                        act.wait_ge(s_pt, count(q, b, QB))
                        nc.scalar.activation(probs_t[:, 0:2], ps[0:S, SCORES:SCORES + 2, 0:G * S]
                                             .rearrange("p t (g k) -> p t g k", g=G), ACT.Copy).then_inc(s_pt_act, 1)
                        fill(units(f"B{b}", q, prev, nxt, nxt2), par)
                        if b == 1:
                            act.wait_ge(s_part, q * 16 + 16)
                            nc.scalar.activation(f_hi[:, bass.ds(q * PART, PART)], stage[:], ACT.Copy,
                                                 scale=W_SCALE).then_inc(s_fhi, 1)

                run_quads(act, prologue, quad, lambda: fill(whole(FINISH), 0))

            @block.vector
            def _(dve):
                def copy_unit(kind, n, par, j):
                    dve.wait_ge(s_unit[kind], count(n, j, 4))
                    src = work(kind)
                    if kind in ("xt", "ct"):
                        hi, lo = (x_hi[:, 1 - par], x_lo[:, 1 - par]) if kind == "xt" else (c_hi, c_lo)
                        dve.wait_ge(s_copy[kind, "A"], count(n, j, 4))
                        ins = nc.vector.tensor_tensor(lo[:, j], src[:, 0:T], hi[:, j], ALU.subtract)
                    elif kind == "vt":
                        ins = nc.vector.tensor_copy(v_rows[:, par, j, :, 0:DK],
                                                    src[0:S].rearrange("p (h d) -> p h d", d=DK))
                    else:
                        if j == 0:
                            dve.wait_ge(s_resid, n * 16 + 16)
                        ins = nc.vector.tensor_tensor(resid[:, j], src[0:S], resid[:, j], ALU.add)
                    ins.then_inc(s_copy[kind, "D"], 1)

                def fill(which, par):
                    for kind, n, j in which:
                        if "D" in KINDS[kind]:
                            copy_unit(kind, n, 1 - par, j)

                def ln_stats(n, bs):
                    if bs[0] == 0:
                        dve.wait_ge(s_rows, n * 16 + 16)
                    for b in bs:
                        nc.vector.bn_stats(stats[:, b], rows[:, b]).then_inc(s_stats, 1)
                    if bs[-1] < QB - 1:
                        return
                    dve.wait_ge(s_stats, count(n, 3, 4))
                    tt = nc.vector.tensor_tensor
                    tt(mean[:], stats[:, :, 1], stats[:, :, 4], ALU.add)
                    tt(gap[:], stats[:, :, 1], stats[:, :, 4], ALU.subtract)
                    tt(spread[:], stats[:, :, 2], stats[:, :, 5], ALU.add).then_inc(s_moments, 1)
                    dve.wait_ge(s_moments, n * 2 + 1)
                    nc.vector.tensor_scalar(mean[:], mean[:], 0.5, None, ALU.mult)
                    tt(gap[:], gap[:], gap[:], ALU.mult)
                    nc.vector.tensor_scalar(spread[:], spread[:], 1.0 / D, EPS, ALU.mult,
                                            ALU.add).then_inc(s_moments, 1)
                    dve.wait_ge(s_moments, n * 2 + 2)
                    nc.vector.scalar_tensor_tensor(var_eps[:], gap[:], 0.25, spread[:], ALU.mult,
                                                   ALU.add).then_inc(s_var, 1)

                def ln_rows(n, bs):
                    if bs[0] == 0:
                        dve.wait_ge(s_rstd, n + 1)
                    for b in bs:
                        nc.vector.tensor_scalar(normed[:, b], rows[:, b], mean[:, b:b + 1], rstd[:, b:b + 1],
                                                ALU.subtract, ALU.mult).then_inc(s_normed, 1)

                def prologue():
                    dve.wait_ge(s_ones, 2)
                    for n in range(2):
                        ln_stats(n, (0, 1))
                        ln_stats(n, (2, 3))
                        ln_rows(n, (0, 1, 2, 3))
                        if n == 0:
                            fill(whole(START[:1]), 0)
                    fill(whole(START[1:]), 1)

                def quad(q, par, prev, nxt, nxt2):
                    for b in range(QB):
                        dve.wait_ge(s_scores, count(q, b, QB))
                        scores = ps[0:S, SCORES:SCORES + KT, 0:G * S].rearrange("p t (g k) -> p t g k", g=G)
                        nc.vector.tensor_reduce(top[:], scores, AX.X, ALU.max).then_inc(s_top, 1)
                        dve.wait_ge(s_top, count(q, b, QB))
                        nc.vector.tensor_tensor(probs[:], scores, top[:].unsqueeze(3).broadcast_to([S, KT, G, S]),
                                                ALU.subtract).then_inc(s_shift, 1)
                        fill(units(f"A{b}", q, prev, nxt, nxt2), par)
                        dve.wait_ge(s_pt, count(q, b, QB))
                        nc.vector.tensor_copy(probs_t[:, 2:4], ps[0:S, SCORES + 2:SCORES + 4, 0:G * S]
                                              .rearrange("p t (g k) -> p t g k", g=G)).then_inc(s_pt_dve, 1)
                        fill(units(f"B{b}", q, prev, nxt, nxt2), par)
                        if nxt2 and b == 0:
                            ln_stats(q + 2, (0, 1))
                            ln_stats(q + 2, (2, 3))
                        if nxt2 and b in (1, 2):
                            ln_rows(q + 2, (2 * b - 2, 2 * b - 1))
                        if b == 1:
                            dve.wait_ge(s_fhi, q + 1)
                            nc.vector.scalar_tensor_tensor(f_lo[:, bass.ds(q * PART, PART)], stage[:], W_SCALE,
                                                           f_hi[:, bass.ds(q * PART, PART)], ALU.mult,
                                                           ALU.subtract).then_inc(s_flo, 1)
                        dve.wait_ge(s_ctx, count(q, b, QB))
                        sums = ps[0:S, CTX:CTX + 2, 0:HB * V1].rearrange("p m (h d) -> p m h d", d=V1)
                        nc.vector.reciprocal(recip[:].rearrange("p (m h) -> p m h", m=2),
                                             sums[:, :, :, DK]).then_inc(s_recip, 1)
                        dve.wait_ge(s_recip, count(q, b, QB))
                        nc.vector.tensor_tensor(context[:, b].rearrange("p (m h) d -> p m h d", m=2),
                                                sums[:, :, :, 0:DK],
                                                recip[:].rearrange("p (m h) -> p m h", m=2).unsqueeze(3)
                                                .broadcast_to([S, 2, HB, DK]), ALU.mult).then_inc(s_norm, 1)

                run_quads(dve, prologue, quad, lambda: fill(whole(FINISH), 0))

            @block.tensor
            def _(pe):
                mm = nc.tensor.matmul
                recent = [None, None]

                def unit(kind, n, j, par):
                    w = int(kind not in HEAVY)
                    before = recent[w]
                    if before is not None:
                        for e in KINDS[before[0]]:
                            pe.wait_ge(s_copy[before[0], e], count(before[1], before[2], 4))
                    recent[w] = (kind, n, j)
                    out = work(kind)
                    if kind == "xt":
                        if j == 0:
                            pe.wait_ge(s_normed, count(n, 3, 4))
                        for b in range(QB):
                            last = nc.tensor.transpose(out[:, b * S:(b + 1) * S], normed[:, b, j * P:(j + 1) * P],
                                                       eye32[0:S, 0:S])
                    elif kind == "ct":
                        if j == 0:
                            pe.wait_ge(s_norm, count(n, 3, 4))
                        for b in range(QB):
                            flat = context[:, b].rearrange("p h d -> p (h d)")
                            last = nc.tensor.transpose(out[:, b * S:(b + 1) * S], flat[:, j * P:(j + 1) * P],
                                                       eye32[0:S, 0:S])
                    elif kind in ("q", "k", "v", "wo"):
                        m = ("q", "k", "v", "wo").index(kind)
                        hi, lo = (c_hi, c_lo) if kind == "wo" else (x_hi[:, 1 - par], x_lo[:, 1 - par])
                        src = "ct" if kind == "wo" else "xt"
                        if j == 0 and kind in ("v", "wo"):
                            pe.wait_ge(s_copy[src, "A"], count(n, 3, 4))
                            pe.wait_ge(s_copy[src, "D"], count(n, 3, 4))
                        for k in range(KT):
                            for i, (a, x) in enumerate(((w_hi, hi), (w_hi, lo), (w_lo, hi))):
                                last = mm(out[:, 0:T], a[:, m, k, j * P:(j + 1) * P], x[:, k],
                                          start=k == 0 and i == 0, stop=k == KT - 1 and i == 2)
                    elif kind == "vt":
                        if j == 0:
                            pe.wait_ge(s_copy["v", "A"], count(n, 3, 4))
                        for t in range(KT):
                            last = nc.tensor.transpose(out[0:S, t * P:(t + 1) * P], v_t[:, t, j * S:(j + 1) * S],
                                                       eye32[:])
                    else:
                        if j == 0:
                            pe.wait_ge(s_copy["wo", "A"], count(n, 3, 4))
                        for t in range(KT):
                            last = nc.tensor.transpose(out[0:S, t * P:(t + 1) * P], o_t[:, t, j * S:(j + 1) * S],
                                                       eye32[:])
                    last.then_inc(s_unit[kind], 1)

                def fill(which, par):
                    for kind, n, j in which:
                        unit(kind, n, j, par)

                def prologue():
                    pe.wait_ge(s_const, 80)
                    fill(whole(START), 1)

                def quad(q, par, prev, nxt, nxt2):
                    recent[:] = [("k", q, 3), ("xt", q + 1, 3) if nxt else ("ot", q - 2, 3)]
                    pe.wait_ge(s_copy["q", "A"], count(q, 3, 4))
                    for b in range(QB):
                        if prev or b:
                            pe.wait_ge(s_pt_act, count(q, b - 1, QB))
                            pe.wait_ge(s_pt_dve, count(q, b - 1, QB))
                        for t in range(KT):
                            mm(ps[0:S, SCORES + t, 0:G * S], eye_bf[:], causal[:], start=True, stop=False)
                        pe.wait_ge(s_diag, count(q, b, QB))
                        for t in range(KT):
                            last = mm(ps[0:S, SCORES + t, 0:G * S], q_t[:, par, t, b * S:(b + 1) * S],
                                      k_diag[:, t].rearrange("p g k -> p (g k)"), start=False, stop=True)
                        last.then_inc(s_scores, 1)
                        fill(units(f"A{b}", q, prev, nxt, nxt2), par)
                        pe.wait_ge(s_exp, count(q, b, QB))
                        for t in range(KT):
                            for g in range(G):
                                last = nc.tensor.transpose(ps[0:S, SCORES + t, g * S:(g + 1) * S], probs[:, t, g],
                                                           eye32[0:S, 0:S])
                        last.then_inc(s_pt, 1)
                        fill(units(f"B{b}", q, prev, nxt, nxt2), par)
                        pe.wait_ge(s_pt_act, count(q, b, QB))
                        pe.wait_ge(s_pt_dve, count(q, b, QB))
                        if b == 0:
                            pe.wait_ge(s_copy["vt", "D"], count(q, 3, 4))
                        if prev or b:
                            pe.wait_ge(s_norm, count(q, b - 1, QB))
                        for h in range(HEADS):
                            out = ps[0:S, CTX + h // HB, (h % HB) * V1:(h % HB + 1) * V1]
                            last = mm(out, probs_t[:, h // G, h % G], v_rows[:, par, b, h], start=True, stop=True)
                        last.then_inc(s_ctx, 1)

                run_quads(pe, prologue, quad, lambda: fill(whole(FINISH), 0))


def expert_phase(nc, weights, ready_pair, consts, mixed, out):
    eye32_d, iota_d, select_d = consts
    TOKENS, D = mixed.shape
    E, R = 8, 32
    ER = E * R
    F = 1792
    KT, FT, ET = D // P, F // P, ER // P
    PAIRS = FT // 2
    T = 208
    BLOCKS = TOKENS // T
    TR = 104
    TT = T // TR
    EPS = 1e-5
    BIG = 3e38

    HEAD = 2 * KT * ER + KT * E
    PAIR = 2 * KT * 2 * P + 2 * ET * 2 * P + 2 * ER
    W2_AT = HEAD + PAIRS * PAIR
    B2_AT = W2_AT + FT * D
    WIDTH = B2_AT + ET * D
    PC = PAIR // 4
    READY = ready_pair[0].shape[1]
    READY_PAIRS = (READY - HEAD) // PAIR
    assert READY == HEAD + READY_PAIRS * PAIR
    CHUNKS = [(HEAD + PC * c, PC) for c in range(4 * READY_PAIRS, 4 * PAIRS)] \
        + [(W2_AT + PC * c, PC) for c in range(8)] + [(B2_AT, ET * D)]
    STAGE = max(w for _, w in CHUNKS)
    assert W2_AT + 8 * PC == B2_AT and weights.shape[1] == WIDTH

    with ExitStack() as ctx:
        def sb(name, shape, dt):
            return ctx.enter_context(nc.sbuf_tensor(name, shape, dt))

        def sem(name):
            return ctx.enter_context(nc.semaphore(name))

        ready_hi, ready_lo = ready_pair
        rest_hi = sb("f_rest_hi", [P, WIDTH - READY], F16)
        rest_lo = sb("f_rest_lo", [P, WIDTH - READY], F16)
        stage = sb("f_stage", [P, 2, STAGE], F32)
        eye32 = sb("f_eye32", [P, P], F32)
        iota = sb("f_iota", [TR, TT, E], F32)
        select = sb("f_select", [32, 8, P], F16)
        rows = sb("f_rows", [TR, TT, D], F32)
        resid = sb("f_resid", [TR, TT, D], F32)
        stats = sb("f_stats", [TR, TT, 6], F32)
        mean = sb("f_mean", [TR, TT], F32)
        gap = sb("f_gap", [TR, TT], F32)
        spread = sb("f_spread", [TR, TT], F32)
        var_eps = sb("f_var_eps", [TR, TT], F32)
        rstd = sb("f_rstd", [TR, TT], F32)
        minus_half = sb("f_minus_half", [TR, TT], F32)
        euler = sb("f_euler", [TR, TT], F32)
        logits = sb("f_logits", [TR, TT, E], F32)
        logits2 = sb("f_logits2", [TR, TT, E], F32)
        rank = sb("f_rank", [TR, TT, E], F32)
        best = sb("f_best", [TR, TT], F32)
        best2 = sb("f_best2", [TR, TT], F32)
        first_at = sb("f_first_at", [TR, TT], F32)
        drop = sb("f_drop", [TR, TT], F32)
        odds = sb("f_odds", [TR, TT], F32)
        total = sb("f_total", [TR, TT], F32)
        route = sb("f_route", [TR, TT, 32], F32)
        route_hi = sb("f_route_hi", [32, T], F16)
        route_lo = sb("f_route_lo", [32, T], F16)
        x_hi = sb("f_x_hi", [P, KT, T], F16)
        x_lo = sb("f_x_lo", [P, KT, T], F16)
        a_hi = sb("f_a_hi", [P, ET, T], F16)
        a_lo = sb("f_a_lo", [P, ET, T], F16)
        am_hi = sb("f_am_hi", [P, 2, 2, ET, T], F16)
        am_lo = sb("f_am_lo", [P, 2, 2, ET, T], F16)
        mask = sb("f_mask", [P, 3, ET, T], F16)
        weight = sb("f_weight", [P, 2, T], F32)
        gate = sb("f_gate", [P, 2, T], F32)
        y0 = sb("f_y0", [P, 4, T], F32)
        y1 = sb("f_y1", [P, 2, T], F32)
        y_hi = sb("f_y_hi", [P, 2, 2, 2, T], F16)
        y_lo = sb("f_y_lo", [P, 2, 2, 2, T], F16)
        sum_hi = sb("f_sum_hi", [P, FT, T], F16)
        sum_lo = sb("f_sum_lo", [P, FT, T], F16)
        m_32 = sb("f_m_32", [P, ET, T], F32)
        m_hi = sb("f_m_hi", [P, ET, T], F16)
        m_lo = sb("f_m_lo", [P, ET, T], F16)
        o_t = y0
        ps = ctx.enter_context(nc.psum_tensor("ps_ffn", [P, 8, 512], F32))

        def bank(n):
            return ps[:, n, 0:2 * T].rearrange("p (a t) -> p a t", a=2)

        A2, DOWN = 4, 6

        def w1(m, p, k, j):
            return HEAD + p * PAIR + (m * KT + k) * 2 * P + j * P

        def b1(m, p, k, j):
            return HEAD + p * PAIR + 2 * KT * 2 * P + (m * ET + k) * 2 * P + j * P

        def a2(p, j, t):
            return HEAD + p * PAIR + 2 * (KT + ET) * 2 * P + j * ER + t * P

        def a1(m, k, t):
            return (m * KT + k) * ER + t * P

        names = ("const", "whi", "wlo", "rows", "resid", "stored", "stats", "moments", "var", "rstd", "normed",
                 "ones", "xt", "xhi", "xlo", "logits", "router", "drop", "odds", "route", "rt", "rhi", "rlo",
                 "expand", "exp_act", "low", "ahi", "alo", "am", "first", "second", "silu", "scaled", "y", "yhi",
                 "ylo", "sum", "shi", "slo", "acc0", "acc1", "masked", "mhi", "mlo", "down", "ot", "turned", "added")
        S = {n: sem("f_" + n) for n in names}
        s_wload = [sem(f"f_weights_loaded{n}") for n in range(2)]

        def at(n, per, j):
            return n * per + (j + 1)

        def turn(slot, p):
            if slot == 0:
                return max(2 * p - 1, 0)
            return min(2 * p + 2, 2 * PAIRS - 1)

        def halves(col, width):
            if col < READY:
                return ready_hi[:, col:col + width], ready_lo[:, col:col + width]
            return rest_hi[:, col - READY:col - READY + width], rest_lo[:, col - READY:col - READY + width]

        def chunks_until(p):
            return max(0, 4 * (p + 1 - READY_PAIRS))

        def block_chunks(p):
            per = -(-len(CHUNKS) // (PAIRS - 1))
            return range(len(CHUNKS))[p * per:(p + 1) * per]

        def run_blocks(eng, prologue, body, epilogue):
            prologue()
            body(0, True, True)
            with eng.Fori(1, BLOCKS - 1) as n:
                body(n, False, True)
            body(BLOCKS - 1, False, False)
            epilogue()

        def token_rows(dram, n):
            return dram[bass.ds(n * T, T)].rearrange("(a p) d -> p a d", p=TR)

        with nc.Block() as block:

            @block.sync
            def _(sp):
                sp.dma_start(rows[:], token_rows(mixed, 0)).then_inc(S["rows"], 16)
                for dst, src in ((eye32, eye32_d), (iota, iota_d), (select, select_d)):
                    sp.dma_start(dst[:], src).then_inc(S["const"], 16)
                sp.dma_start(resid[:], token_rows(mixed, 0)).then_inc(S["resid"], 16)
                for c, (start, width) in enumerate(CHUNKS):
                    if c >= 2:
                        sp.wait_ge(S["whi"], c - 1)
                        sp.wait_ge(S["wlo"], c - 1)
                    sp.dma_start(stage[:, c % 2, 0:width], weights[:, start:start + width]).then_inc(s_wload[c % 2], 16)
                    if c == 3:
                        sp.wait_ge(S["xt"], 2)
                        sp.dma_start(rows[:], token_rows(mixed, 1)).then_inc(S["rows"], 16)

                def store(n):
                    sp.wait_ge(S["added"], at(n, 2, 1))
                    sp.dma_start(token_rows(out, n), resid[:]).then_inc(S["stored"], 16)
                    sp.wait_ge(S["stored"], n * 16 + 16)

                with sp.Fori(0, BLOCKS - 2) as n:
                    sp.wait_ge(S["xt"], at(n + 1, 2, 1))
                    sp.dma_start(rows[:], token_rows(mixed, n + 2)).then_inc(S["rows"], 16)
                    store(n)
                    sp.dma_start(resid[:], token_rows(mixed, n + 1)).then_inc(S["resid"], 16)
                store(BLOCKS - 2)
                sp.dma_start(resid[:], token_rows(mixed, BLOCKS - 1)).then_inc(S["resid"], 16)
                store(BLOCKS - 1)

            @block.gpsimd
            def _(pool):
                nc.gpsimd.memset(minus_half[:], -0.5)
                nc.gpsimd.memset(euler[:], 2.718281828459045)
                nc.gpsimd.memset(route[:], 0.0).then_inc(S["ones"], 1)
                pool.wait_ge(S["ones"], 1)

                def one(n):
                    pool.wait_ge(S["var"], n + 1)
                    nc.gpsimd.tensor_tensor(rstd[:], var_eps[:], minus_half[:], ALU.pow).then_inc(S["rstd"], 1)
                    pool.wait_ge(S["drop"], n + 1)
                    nc.gpsimd.tensor_tensor(odds[:], euler[:], drop[:], ALU.pow).then_inc(S["odds"], 1)

                one(0)
                with pool.Fori(1, BLOCKS) as n:
                    one(n)

            @block.scalar
            def _(act):
                cp = nc.scalar.activation

                def split(c):
                    start, width = CHUNKS[c]
                    act.wait_ge(s_wload[c % 2], 16 * (c // 2 + 1))
                    cp(halves(start, width)[0], stage[:, c % 2, 0:width], ACT.Copy,
                       scale=W_SCALE).then_inc(S["whi"], 1)

                def route_copy(n):
                    act.wait_ge(S["rt"], at(n, 1, 0))
                    cp(route_hi[:], ps[0:32, 1, 0:T], ACT.Copy).then_inc(S["rhi"], 1)
                    act.wait_ge(S["expand"], at(n, 4, 1))
                    for m in range(2):
                        last = cp(mask[:, m], bank(m), ACT.Copy)
                    last.then_inc(S["exp_act"], 1)
                    act.wait_ge(S["expand"], at(n, 4, 3))
                    cp(mask[:, 2], bank(4), ACT.Copy)
                    cp(weight[:], bank(5), ACT.Copy).then_inc(S["exp_act"], 1)

                def read_out(slot, n, p, first):
                    par = p % 2
                    k = turn(slot, p)
                    act.wait_ge(S["second" if slot else "first"], at(n, PAIRS, p))
                    cp(gate[:], bank(2 * par), ACT.Silu, scale=W_UNSCALE).then_inc(S["silu"], 1)
                    act.wait_ge(S["y"], at(n, 2 * PAIRS, k))
                    src = y1[:] if slot else y0[:, 2 * par:2 * par + 2]
                    cp(y_hi[:, par, slot], src, ACT.Copy).then_inc(S["yhi"], 1)
                    if slot:
                        act.wait_ge(S["sum"], at(n, PAIRS, p))
                        cp(sum_hi[:, 2 * p:2 * p + 2], y1[:], ACT.Copy).then_inc(S["shi"], 1)

                def prologue():
                    prep_all(0)

                def prep_all(n):
                    for u in range(2):
                        act.wait_ge(S["xt"], at(n, 2, u))
                        cp(x_hi[:, 2 * u:2 * u + 2], bank(2 + u), ACT.Copy).then_inc(S["xhi"], 1)
                    route_copy(n)
                    for m in range(2):
                        act.wait_ge(S["low"], at(n, 2, m))
                        if m:
                            act.wait_ge(S["am"], at(n, 2, 0))
                        cp(a_hi[:], bank(2 + m), ACT.Copy, scale=W_UNSCALE).then_inc(S["ahi"], 1)

                def body(n, first, nxt):
                    read_out(0, n, 0, first)
                    for p in range(PAIRS):
                        if first:
                            for c in block_chunks(p):
                                split(c)
                        if p + 1 < PAIRS:
                            read_out(0, n, p + 1, first)
                        read_out(1, n, p, first)
                    if nxt:
                        for u in range(2):
                            act.wait_ge(S["xt"], at(n + 1, 2, u))
                            cp(x_hi[:, 2 * u:2 * u + 2], bank(2 + u), ACT.Copy).then_inc(S["xhi"], 1)
                    act.wait_ge(S["masked"], at(n, 3, 2))
                    cp(m_hi[:], m_32[:], ACT.Copy).then_inc(S["mhi"], 1)
                    if nxt:
                        route_copy(n + 1)
                        for m in range(2):
                            act.wait_ge(S["low"], at(n + 1, 2, m))
                            if m:
                                act.wait_ge(S["am"], at(n + 1, 2, 0))
                            cp(a_hi[:], bank(2 + m), ACT.Copy, scale=W_UNSCALE).then_inc(S["ahi"], 1)
                    for u in range(2):
                        act.wait_ge(S["down"], at(n, 2, u))
                        cp(o_t[:, 2 * u:2 * u + 2], bank(DOWN + u), ACT.Copy, scale=W_UNSCALE).then_inc(S["ot"], 1)

                run_blocks(act, prologue, body, lambda: None)

            @block.vector
            def _(dve):
                tt, ts, stt = nc.vector.tensor_tensor, nc.vector.tensor_scalar, nc.vector.scalar_tensor_tensor
                ROUTER = 13

                def spread_e(small):
                    return small.unsqueeze(2).broadcast_to([TR, TT, E])

                def split(c):
                    start, width = CHUNKS[c]
                    dve.wait_ge(S["whi"], c + 1)
                    hi, lo = halves(start, width)
                    stt(lo, stage[:, c % 2, 0:width], W_SCALE, hi, ALU.mult, ALU.subtract).then_inc(S["wlo"], 1)

                def ln_stats(n):
                    dve.wait_ge(S["rows"], n * 16 + 16)
                    for b in range(TT):
                        nc.vector.bn_stats(stats[:, b], rows[:, b]).then_inc(S["stats"], 1)
                    dve.wait_ge(S["stats"], at(n, TT, TT - 1))
                    tt(mean[:], stats[:, :, 1], stats[:, :, 4], ALU.add)
                    tt(gap[:], stats[:, :, 1], stats[:, :, 4], ALU.subtract)
                    tt(spread[:], stats[:, :, 2], stats[:, :, 5], ALU.add).then_inc(S["moments"], 1)
                    dve.wait_ge(S["moments"], n * 2 + 1)
                    ts(mean[:], mean[:], 0.5, None, ALU.mult)
                    tt(gap[:], gap[:], gap[:], ALU.mult)
                    ts(spread[:], spread[:], 1.0 / D, EPS, ALU.mult, ALU.add).then_inc(S["moments"], 1)
                    dve.wait_ge(S["moments"], n * 2 + 2)
                    stt(var_eps[:], gap[:], 0.25, spread[:], ALU.mult, ALU.add).then_inc(S["var"], 1)

                def ln_rows(n):
                    dve.wait_ge(S["rstd"], n + 1)
                    for b in range(TT):
                        last = ts(rows[:, b], rows[:, b], mean[:, b:b + 1], rstd[:, b:b + 1],
                                  ALU.subtract, ALU.mult)
                    last.then_inc(S["normed"], 1)

                def x_low(n):
                    for u in range(2):
                        dve.wait_ge(S["xhi"], at(n, 2, u))
                        tt(x_lo[:, 2 * u:2 * u + 2], bank(2 + u), x_hi[:, 2 * u:2 * u + 2],
                           ALU.subtract).then_inc(S["xlo"], 1)

                def router(n):
                    count = [0]

                    def link(ins):
                        count[0] += 1
                        ins.then_inc(S["router"], 1)
                        dve.wait_ge(S["router"], at(n, ROUTER, count[0] - 1))

                    dve.wait_ge(S["logits"], n + 1)
                    link(ts(logits[:], ps[0:TR, 0, 0:TT * E].rearrange("p (a e) -> p a e", e=E), W_UNSCALE, None,
                            ALU.mult))
                    link(nc.vector.tensor_reduce(best[:], logits[:], AX.X, ALU.max))
                    link(tt(rank[:], logits[:], spread_e(best[:]), ALU.is_lt))
                    link(stt(rank[:], rank[:], float(E), iota[:], ALU.mult, ALU.add))
                    link(nc.vector.tensor_reduce(first_at[:], rank[:], AX.X, ALU.min))
                    link(tt(route[:, :, 0:E], iota[:], spread_e(first_at[:]), ALU.is_equal))
                    link(stt(logits2[:], route[:, :, 0:E], -BIG, logits[:], ALU.mult, ALU.add))
                    link(nc.vector.tensor_reduce(best2[:], logits2[:], AX.X, ALU.max))
                    tt(drop[:], best2[:], best[:], ALU.subtract).then_inc(S["drop"], 1)
                    link(tt(rank[:], logits2[:], spread_e(best2[:]), ALU.is_lt))
                    link(stt(rank[:], rank[:], float(E), iota[:], ALU.mult, ALU.add))
                    link(nc.vector.tensor_reduce(first_at[:], rank[:], AX.X, ALU.min))
                    tt(route[:, :, E:2 * E], iota[:], spread_e(first_at[:]), ALU.is_equal)
                    dve.wait_ge(S["odds"], n + 1)
                    link(ts(total[:], odds[:], 1.0, None, ALU.add))
                    link(nc.vector.reciprocal(route[:, :, 2 * E], total[:]))
                    tt(route[:, :, 2 * E + 1], odds[:], route[:, :, 2 * E], ALU.mult).then_inc(S["route"], 1)
                    assert count[0] == ROUTER

                def route_low(n):
                    dve.wait_ge(S["rhi"], n + 1)
                    tt(route_lo[:], ps[0:32, 1, 0:T], route_hi[:], ALU.subtract).then_inc(S["rlo"], 1)

                def mask_low_rank(n):
                    dve.wait_ge(S["exp_act"], at(n, 2, 1))
                    for m in range(2):
                        dve.wait_ge(S["ahi"], at(n, 2, m))
                        stt(a_lo[:], bank(2 + m), W_UNSCALE, a_hi[:], ALU.mult, ALU.subtract).then_inc(S["alo"], 1)
                        dve.wait_ge(S["alo"], at(n, 2, m))
                        for slot in range(2):
                            tt(am_hi[:, slot, m], a_hi[:], mask[:, 2 * slot], ALU.mult)
                            last = tt(am_lo[:, slot, m], a_lo[:], mask[:, 2 * slot], ALU.mult)
                        last.then_inc(S["am"], 1)

                def read_out(slot, n, p, first):
                    par = p % 2
                    k = turn(slot, p)
                    dve.wait_ge(S["silu"], at(n, 2 * PAIRS, k))
                    tt(gate[:], gate[:], weight[:, slot].unsqueeze(1).broadcast_to([P, 2, T]),
                       ALU.mult).then_inc(S["scaled"], 1)
                    dve.wait_ge(S["scaled"], at(n, 2 * PAIRS, k))
                    dst = y1[:] if slot else y0[:, 2 * par:2 * par + 2]
                    if slot == 0 and p < 2 and not first:
                        dve.wait_ge(S["turned"], at(n - 1, 2, 1))
                    stt(dst, bank(2 * par + 1), W_UNSCALE, gate[:], ALU.mult, ALU.mult).then_inc(S["y"], 1)
                    dve.wait_ge(S["yhi"], at(n, 2 * PAIRS, k))
                    tt(y_lo[:, par, slot], dst, y_hi[:, par, slot], ALU.subtract).then_inc(S["ylo"], 1)
                    if slot:
                        tt(y1[:], y1[:], y0[:, 2 * par:2 * par + 2], ALU.add).then_inc(S["sum"], 1)
                        dve.wait_ge(S["shi"], at(n, PAIRS, p))
                        tt(sum_lo[:, 2 * p:2 * p + 2], y1[:], sum_hi[:, 2 * p:2 * p + 2],
                           ALU.subtract).then_inc(S["slo"], 1)

                def masked(n):
                    dve.wait_ge(S["acc1"], n + 1)
                    stt(m_32[:], bank(A2), W_UNSCALE, mask[:, 0], ALU.mult, ALU.mult)
                    stt(gate[:], bank(A2 + 1), W_UNSCALE, mask[:, 1], ALU.mult, ALU.mult).then_inc(S["masked"], 2)
                    dve.wait_ge(S["masked"], at(n, 3, 1))
                    tt(m_32[:], m_32[:], gate[:], ALU.add).then_inc(S["masked"], 1)
                    dve.wait_ge(S["mhi"], n + 1)
                    tt(m_lo[:], m_32[:], m_hi[:], ALU.subtract).then_inc(S["mlo"], 1)

                def add_rows(n):
                    dve.wait_ge(S["resid"], n * 16 + 16)
                    for u in range(TT):
                        dve.wait_ge(S["turned"], at(n, 2, u))
                        tt(resid[:, u], ps[0:TR, DOWN + u, :], resid[:, u], ALU.add).then_inc(S["added"], 1)

                def prologue():
                    dve.wait_ge(S["const"], 48)
                    dve.wait_ge(S["ones"], 1)
                    ln_stats(0)
                    ln_rows(0)
                    x_low(0)
                    router(0)
                    route_low(0)
                    mask_low_rank(0)

                def body(n, first, nxt):
                    read_out(0, n, 0, first)
                    if not first:
                        add_rows(n - 1)
                    for p in range(PAIRS):
                        if first:
                            for c in block_chunks(p):
                                split(c)
                        if p + 1 < PAIRS:
                            read_out(0, n, p + 1, first)
                        read_out(1, n, p, first)
                        if nxt and p == 1:
                            ln_stats(n + 1)
                        if nxt and p == 3:
                            ln_rows(n + 1)
                    if nxt:
                        x_low(n + 1)
                    masked(n)
                    if nxt:
                        router(n + 1)
                        route_low(n + 1)
                        mask_low_rank(n + 1)

                run_blocks(dve, prologue, body, lambda: add_rows(BLOCKS - 1))

            @block.tensor
            def _(pe):
                mm = nc.tensor.matmul

                def triple(out_ap, col, x, xl, start, stop, skip=False):
                    hi, lo = halves(col, P)
                    mm(out_ap, hi, x, start=start, stop=False, skip_group_check=skip)
                    mm(out_ap, hi, xl, start=False, stop=False, skip_group_check=skip)
                    return mm(out_ap, lo, x, start=False, stop=stop, skip_group_check=skip)

                def base(n, p, first):
                    par = p % 2
                    if first and chunks_until(p):
                        pe.wait_ge(S["wlo"], chunks_until(p))
                    if p >= 2:
                        pe.wait_ge(S["y"], at(n, 2 * PAIRS, turn(1, p - 2)))
                    for m in range(2):
                        for j in range(2):
                            for k in range(KT):
                                last = triple(bank(2 * par + m)[:, j], w1(m, p, k, j), x_hi[:, k], x_lo[:, k],
                                              j == 0 and k == 0, False)
                            for k in range(ET):
                                last = triple(bank(2 * par + m)[:, j], b1(m, p, k, j), am_hi[:, 0, m, k],
                                              am_lo[:, 0, m, k], False, j == 1 and k == ET - 1)
                    last.then_inc(S["first"], 1)

                def delta(n, p):
                    par = p % 2
                    pe.wait_ge(S["y"], at(n, 2 * PAIRS, turn(0, p)))
                    for m in range(2):
                        for j in range(2):
                            for k in range(ET):
                                last = triple(bank(2 * par + m)[:, j], b1(m, p, k, j), am_hi[:, 1, m, k],
                                              am_lo[:, 1, m, k], False, False, skip=True)
                    last.then_inc(S["second"], 1)

                def down_low(n, p, slot):
                    par = p % 2
                    pe.wait_ge(S["ylo"], at(n, 2 * PAIRS, turn(slot, p)))
                    for t in range(ET):
                        for j in range(2):
                            last = triple(bank(A2 + slot)[:, t], a2(p, j, t), y_hi[:, par, slot, j],
                                          y_lo[:, par, slot, j], p == 0 and t == 0 and j == 0,
                                          p == PAIRS - 1 and t == ET - 1 and j == 1)
                    if p == PAIRS - 1:
                        last.then_inc(S[f"acc{slot}"], 1)

                def down(h, fs):
                    for f in fs:
                        triple(bank(DOWN + h // 2)[:, h % 2], W2_AT + f * D + h * P, sum_hi[:, f], sum_lo[:, f],
                               f == 0 and h % 2 == 0, False)

                def turn_rows(n):
                    pe.wait_ge(S["normed"], n + 1)
                    for u in range(2):
                        for k in (2 * u, 2 * u + 1):
                            for b in range(TT):
                                last = nc.tensor.transpose(bank(2 + u)[:, k % 2, b * TR:(b + 1) * TR],
                                                           rows[:, b, k * P:(k + 1) * P], eye32[0:TR, 0:TR])
                        last.then_inc(S["xt"], 1)

                def logit(n):
                    pe.wait_ge(S["xlo"], at(n, 2, 1))
                    for b in range(TT):
                        for k in range(KT):
                            hi, lo = halves(2 * KT * ER + k * E, E)
                            xs = slice(b * TR, (b + 1) * TR)
                            o = ps[0:TR, 0, b * E:(b + 1) * E]
                            mm(o, x_hi[:, k, xs], hi, start=k == 0, stop=False)
                            mm(o, x_hi[:, k, xs], lo, start=False, stop=False)
                            last = mm(o, x_lo[:, k, xs], hi, start=False, stop=k == KT - 1)
                    last.then_inc(S["logits"], 1)

                def low_rank(n):
                    for m in range(2):
                        for t in range(ET):
                            for k in range(KT):
                                last = triple(bank(2 + m)[:, t], a1(m, k, t), x_hi[:, k], x_lo[:, k],
                                              t == 0 and k == 0, t == ET - 1 and k == KT - 1)
                        last.then_inc(S["low"], 1)

                def turn_route(n):
                    pe.wait_ge(S["route"], n + 1)
                    for b in range(TT):
                        last = nc.tensor.transpose(ps[0:32, 1, b * TR:(b + 1) * TR], route[:, b],
                                                   eye32[0:TR, 0:TR])
                    last.then_inc(S["rt"], 1)

                def expand(n):
                    pe.wait_ge(S["rlo"], n + 1)
                    for m, b in enumerate((0, 1, 4, 5)):
                        for t in range(2):
                            o = bank(b)[:, t]
                            s = select[:, 2 * m + t]
                            if m < 3:
                                last = mm(o, s, route_hi[:], start=t == 0, stop=t == 1)
                            else:
                                mm(o, s, route_hi[:], start=t == 0, stop=False)
                                last = mm(o, s, route_lo[:], start=False, stop=t == 1)
                        last.then_inc(S["expand"], 1)

                def turn_out(n):
                    for u in range(TT):
                        pe.wait_ge(S["ot"], at(n, 2, 1))
                        for k in range(KT):
                            last = nc.tensor.transpose(ps[0:TR, DOWN + u, k * P:(k + 1) * P],
                                                       o_t[:, k, u * TR:(u + 1) * TR], eye32[:])
                        last.then_inc(S["turned"], 1)

                def prologue():
                    pe.wait_ge(S["const"], 48)
                    turn_rows(0)
                    logit(0)
                    low_rank(0)
                    turn_route(0)
                    expand(0)

                def body(n, first, nxt):
                    pe.wait_ge(S["am"], at(n, 2, 1))
                    base(n, 0, first)
                    if not first:
                        turn_out(n - 1)
                    for p in range(PAIRS):
                        if p + 1 < PAIRS:
                            base(n, p + 1, first)
                        delta(n, p)
                        down_low(n, p, 0)
                        if p:
                            down_low(n, p - 1, 1)
                    if nxt:
                        pe.wait_ge(S["y"], at(n, 2 * PAIRS, turn(1, PAIRS - 2)))
                        turn_rows(n + 1)
                    if first:
                        pe.wait_ge(S["wlo"], len(CHUNKS))
                    if not first:
                        pe.wait_ge(S["added"], at(n - 1, 2, 1))
                    pe.wait_ge(S["slo"], at(n, PAIRS, PAIRS - 2))
                    down(0, range(0, FT - 2))
                    down(1, range(0, FT - 2))
                    pe.wait_ge(S["ylo"], at(n, 2 * PAIRS, turn(1, PAIRS - 1)))
                    down_low(n, PAIRS - 1, 1)
                    pe.wait_ge(S["slo"], at(n, PAIRS, PAIRS - 1))
                    if nxt:
                        logit(n + 1)
                        low_rank(n + 1)
                    down(0, range(FT - 2, FT))
                    down(1, range(FT - 2, FT))
                    down(2, range(0, FT // 2))
                    if nxt:
                        turn_route(n + 1)
                    down(2, range(FT // 2, FT))
                    if nxt:
                        expand(n + 1)
                    down(3, range(0, FT))
                    pe.wait_ge(S["mlo"], n + 1)
                    for h in range(KT):
                        for t in range(ET):
                            last = triple(bank(DOWN + h // 2)[:, h % 2], B2_AT + t * D + h * P, m_hi[:, t], m_lo[:, t],
                                          False, h % 2 == 1 and t == ET - 1)
                        if h % 2:
                            last.then_inc(S["down"], 1)

                run_blocks(pe, prologue, body, lambda: turn_out(BLOCKS - 1))


def build(nc, spectra, kry_b, readout, log_dt, cls_rows, eye32, eye16, two_eye, half_eye, ones16, ones32,
          w_attn, b_attn, eye_bf, causal, own_head,
          w_ffn, iota, select, out):
    tokens = nc.dram_tensor("tokens", (64, 65, 512), F32, kind="Internal").ap()
    mixed = nc.dram_tensor("mixed", (64, 65, 512), F32, kind="Internal").ap()
    READY = 2080 + 4 * 3584
    with nc.sbuf_tensor("arena", [P, READY], F32) as arena_t:
        arena = arena_t[:]
        ffn_pair = (arena[:, 0:READY // 2].bitcast(F16), arena[:, READY // 2:READY].bitcast(F16))
        with nc.sbuf_tensor("attn_hi", [P, 4, 4, 512], F16) as hi, nc.sbuf_tensor("attn_lo", [P, 4, 4, 512], F16) as lo:
            attn_pair = (hi[:], lo[:])
            tokenizer_phase(nc, arena, w_attn, attn_pair, spectra, kry_b, readout, log_dt, cls_rows,
                            (eye32, eye16, two_eye, half_eye, ones16, ones32), tokens)
            attention_phase(nc, attn_pair, w_ffn, ffn_pair, b_attn, (eye32, eye_bf, causal, own_head), tokens, mixed)
        expert_phase(nc, w_ffn, ffn_pair, (eye32, iota, select), mixed.rearrange("b s d -> (b s) d"),
                     out.rearrange("b s d -> (b s) d"))


def kernel(**inputs):
    import ml_dtypes
    import numpy as np
    import concourse.bacc as bacc
    from concourse.bass_utils import run_bass_kernel_spmd as run
    a = {k: np.asarray(v) for k, v in inputs.items()}
    A = a["L0_tok_A"]
    re, im = A[..., 0].transpose(2, 0, 1), A[..., 1].transpose(2, 0, 1)
    at = [a["L0_attn_W" + n] for n in "qkvo"]
    ab = [a["L0_attn_b" + n] for n in "qkvo"]
    mask = np.where(np.arange(65)[None, :] > np.arange(65)[:, None], -1e30, 0.0).astype(ml_dtypes.bfloat16)

    def tiles(w):
        return w.reshape(-1, 128, w.shape[1]).transpose(1, 0, 2)

    f = {n: a["L0_ffn_" + n] for n in ("Wg", "W1", "W2", "W3", "A1", "A2", "A3", "B1", "B2", "B3")}
    low = {n: tiles(f[n].reshape(256, -1).T) for n in ("A1", "A2", "A3")}
    high = {n: tiles(f[n].transpose(0, 2, 1).reshape(256, -1)) for n in ("B1", "B2", "B3")}
    up = {n: tiles(f[n].T) for n in ("W1", "W2", "W3", "Wg")}
    cols = [low["A1"], low["A3"], up["Wg"]]
    for p in range(7):
        part = slice(256 * p, 256 * p + 256)
        cols += [up["W1"][:, :, part], up["W3"][:, :, part], high["B1"][:, :, part], high["B3"][:, :, part],
                 low["A2"][:, 2 * p:2 * p + 2]]
    cols += [up["W2"], high["B2"]]
    select = np.zeros((32, 8, 128), np.float16)
    for t in range(2):
        for p in range(128):
            e = 4 * t + p // 32
            select[e, t, p] = 1
            select[8 + e, 2 + t, p] = 1
            select[8 + e, 4 + t, p] = 1
            select[e, 4 + t, p] = -1
            select[16 + t, 6 + t, p] = 1
    arrays = {
        "spectra": np.concatenate([np.concatenate([re, im], 2), np.concatenate([im, re], 2)], 0),
        "kry_b": a["L0_tok_B"].transpose(2, 1, 0).reshape(128, 64),
        "readout": a["x"].transpose(3, 2, 1, 0).reshape(128, 64, 64),
        "log_dt": np.broadcast_to(a["L0_tok_log_dt"].reshape(1, 64), (128, 64)),
        "cls_rows": np.broadcast_to(a["cls_tok"].reshape(1, 512), (64, 512)),
        "eye32": np.eye(128, dtype=np.float32),
        "eye16": np.eye(128, dtype=np.float16),
        "two_eye": np.tile(2 * np.eye(128, dtype=np.float16), (1, 4)),
        "half_eye": np.tile(-0.5 * np.eye(128, dtype=np.float16), (1, 4)),
        "ones16": np.ones((128, 128), np.float16),
        "ones32": np.ones((128, 128), np.float32),
        "w_attn": np.stack([w.T.reshape(4, 128, 512).transpose(1, 0, 2) for w in at]),
        "b_attn": np.stack([b.reshape(4, 128).T for b in ab], 1),
        "eye_bf": np.eye(65).astype(ml_dtypes.bfloat16),
        "causal": np.tile(mask, (1, 4)),
        "own_head": np.kron(np.eye(4, dtype=np.float32), np.ones((32, 1), np.float32)),
        "w_ffn": np.concatenate([c.reshape(128, -1) for c in cols], 1),
        "iota": np.broadcast_to(np.arange(8, dtype=np.float32), (104, 2, 8)),
        "select": select,
    }
    nc = bacc.Bacc("TRN2", target_bir_lowering=False, num_devices=1)
    feeds, aps = {}, []
    for name, v in arrays.items():
        v = np.ascontiguousarray(v)
        feeds["in_" + name] = v
        aps.append(nc.dram_tensor("in_" + name, v.shape, mybir.dt.from_np(v.dtype), kind="ExternalInput").ap())
    aps.append(nc.dram_tensor("out", (64, 65, 512), F32, kind="ExternalOutput").ap())
    build(nc, *aps)
    return run(nc, [feeds], core_ids=[0]).results[0]["out"]
```

```python
from contextlib import ExitStack

import concourse.bass as bass
from concourse import mybir

F32 = mybir.dt.float32
F16 = mybir.dt.float16
BF16 = mybir.dt.bfloat16
ACT = mybir.ActivationFunctionType
ALU = mybir.AluOpType
AX = mybir.AxisListType
P = 128
W_SCALE = 64.0
W_UNSCALE = 1.0 / W_SCALE


def tokenizer_phase(nc, arena, attn_w, attn_pair, spectra, kry_b, readout, log_dt, cls_rows, consts, tokens):
    eye32_d, eye16_d, two_eye_d, half_eye_d, ones16_d, ones32_d = consts
    H = spectra.shape[1]
    CHANNELS = readout.shape[2]
    L = tokens.shape[2]
    CHAINS, CH = 4, 4
    SET = CHAINS * CH
    SETS = H // SET
    COARSE = 5
    EXACT = 2
    LEVELS = L.bit_length() - 1

    with ExitStack() as ctx:
        def sb(name, shape, dt):
            return ctx.enter_context(nc.sbuf_tensor(name, shape, dt))

        def sem(name):
            return ctx.enter_context(nc.semaphore(name))

        raw = sb("raw", [P, SET, P], F32)
        minus_back = sb("minus_back", [P, SET, P], F32)
        minus_back16 = sb("minus_back16", [P, SET, P], F16)
        inv16 = sb("inv16", [P, SET, P], F16)
        corr16 = sb("corr16", [P, SET, P], F16)
        inv32 = sb("inv32", [P, SET, P], F32)
        corr32 = sb("corr32", [P, SET, P], F32)
        wide = sb("wide", [P, SET, P + L], F32)
        power, krylov = wide[:, :, 0:P], wide[:, :, P:P + L]
        power_t = arena[:, 0:SET * P].rearrange("p (h m) -> p h m", m=P)
        read_t = sb("read_t", [P, SET, CHANNELS], F32)
        rows = arena[0:CHANNELS, SET * P:SET * (P + L)].rearrange("p (h l) -> p h l", l=L)
        attn_stage = sb("attn_stage", [P, 4, 512], F32)
        attn_hi, attn_lo = attn_pair
        half_dt = sb("half_dt", [P, H], F32)
        signed_dt = sb("signed_dt", [P, H], F32)
        drive = sb("drive", [P, H], F32)
        row_sum = sb("row_sum", [P, SET], F32)
        col_max = sb("col_max", [P, SET], F32)
        row_max = sb("row_max", [SET, 1], F32)
        row_diag = sb("row_diag", [SET, SET], F32)
        row_norm = sb("row_norm", [P, SET], F32)
        alpha = sb("alpha", [P, SET], F32)
        eye32 = sb("eye32", [P, P], F32)
        eye16 = sb("eye16", [P, P], F16)
        two_eye = sb("two_eye", [P, CH * P], F16)
        half_eye = sb("half_eye", [P, CH * P], F16)
        ones16 = sb("ones16", [P, P], F16)
        ones32 = sb("ones32", [P, P], F32)
        ps = ctx.enter_context(nc.psum_tensor("ps_tok", [P, 8, 512], F32))

        s_const = sem("a_const")
        s_dt = sem("a_dt")
        s_raw = sem("a_raw_loaded")
        s_read = sem("a_readout_loaded")
        s_stored = sem("a_rows_stored")
        s_cls = sem("a_cls_stored")
        s_dve = sem("a_dve_chain")
        s_rawfree = sem("a_raw_consumed")
        s_back = sem("a_back_ready")
        s_abs = sem("a_abs_ready")
        s_norm = sem("a_norms")
        s_diag = sem("a_diag")
        s_bcast = sem("a_bcast")
        s_rnorm = sem("a_row_norms")
        s_cmax = sem("a_column_norms")
        s_start = sem("a_start_ready")
        s_neg = sem("a_readout_signed")
        s_pe = sem("a_products")
        s_act = sem("a_act_copied")
        s_vec = sem("a_dve_copied")
        s_attn = sem("a_attn_weight_loaded")
        s_ahi = sem("a_attn_high")
        s_alo = sem("a_attn_low")

        rounds = []
        for n in range(COARSE):
            rounds += [("corr16", n), ("inv16", n)]
        for n in range(EXACT):
            rounds += [("corr32", n), ("inv32", n)]
        rounds += [("transpose", -1), ("seed", 0)]
        for k in range(LEVELS - 1):
            rounds += [("square", k), ("transpose", k)]
        rounds += [("last_double", LEVELS - 1), ("read", 0), ("read", 1)]
        R = len(rounds)
        SPLITS = (3, 4, 5, 6)
        SUMS, FORMS = (2, 3, 4, 5), (3, 4, 5, 6)
        TURN_ROWS, SPREAD_ROWS, SUM_COLUMNS = LEVELS - 4, LEVELS - 3, LEVELS - 2
        BACK_READ = rounds.index(("corr32", EXACT - 1))
        NORM_BANK = 2 * CHAINS - 1
        NORM_STEPS = 2 + CHAINS

        def run_sets(eng, one_set):
            one_set(0, True, True)
            with eng.Fori(1, SETS - 1) as i:
                one_set(i, False, True)
            one_set(SETS - 1, False, False)

        def build_back(engine, wait, n):
            tt = engine.tensor_tensor
            wait(s_raw, n * 16 + 16)
            half = P // 2
            for lo, dt in ((0, signed_dt), (half, half_dt)):
                last = tt(minus_back[:, :, lo:lo + half], raw[:, :, lo:lo + half],
                          dt[:, bass.ds(n * SET, SET)].unsqueeze(2).broadcast_to([P, SET, half]), ALU.mult)
            last.then_inc(s_rawfree, 1)
            wait(s_rawfree, n + 1)
            tt(minus_back[:], minus_back[:], eye32[:].unsqueeze(1).broadcast_to([P, SET, P]),
               ALU.subtract).then_inc(s_back, 1)

        def bank(g, n):
            return ps[:, 2 * g + n, :]

        def bank4(g, n, m=P):
            return ps[:, 2 * g + n, 0:CH * m].rearrange("p (h m) -> p h m", m=m)

        def pairs(g, lo, hi):
            return ps[:, 2 * g:2 * g + 2, :].rearrange("p b (h m) -> p b h m", h=2)[:, :, :, lo:hi]

        def chain2(t, g):
            return chain(t, g).rearrange("p (b h) m -> p b h m", b=2)

        def chain(t, g):
            return t[:, CH * g:CH * g + CH, :]

        def copies(kind, k, g):
            if kind == "corr16":
                return [(chain(corr16, g), bank4(g, 0), 1.0)]
            if kind == "inv16":
                return [(chain(inv32 if k == COARSE - 1 else inv16, g), bank4(g, 1), 1.0)]
            if kind == "corr32":
                return [(chain(corr32, g), bank4(g, 0), 1.0)]
            if kind == "inv32":
                if k == EXACT - 1:
                    return [(chain(power, g), bank4(g, 1), 2.0)]
                return [(chain(inv32, g), bank4(g, 1), 1.0)]
            if kind == "transpose":
                return [(chain(power_t, g), bank4(g, 0), 1.0)]
            if kind == "seed":
                return [(krylov[:, CH * g:CH * g + CH, 0:1], bank4(g, 1, 1), 1.0)]
            if kind == "square":
                n = 1 << k
                return [(chain2(power, g), pairs(g, 0, P), 1.0),
                        (chain2(krylov[:, :, n:2 * n], g), pairs(g, P, P + n), 1.0)]
            if kind == "last_double":
                n = 1 << k
                return [(krylov[:, CH * g + 2 * m:CH * g + 2 * m + 2, n:2 * n],
                         bank(g, m).rearrange("p (h l) -> p h l", h=2), 1.0) for m in range(2)]
            return [(rows[:, CH * g + 2 * k + m, :], bank(g, m)[0:CHANNELS], 1.0) for m in range(2)]

        with nc.Block() as block:

            @block.sync
            def _(sp):
                sp.dma_start(half_dt[:], log_dt).then_inc(s_dt, 16)
                sp.dma_start(drive[:], kry_b).then_inc(s_dt, 16)
                sp.dma_start(raw[:], spectra[:, 0:SET, :]).then_inc(s_raw, 16)
                for dst, src in ((eye32, eye32_d), (eye16, eye16_d), (two_eye, two_eye_d),
                                 (half_eye, half_eye_d), (ones16, ones16_d), (ones32, ones32_d)):
                    sp.dma_start(dst[:], src).then_inc(s_const, 16)
                sp.dma_start(read_t[:], readout[:, 0:SET, :]).then_inc(s_read, 16)
                sp.dma_start(tokens[:, 0, :], cls_rows).then_inc(s_cls, 16)

                sp.dma_start(attn_stage[:], attn_w[0]).then_inc(s_attn, 16)

                def store(i):
                    for k in range(2):
                        sp.wait_ge(s_act, i * (2 * R) + 2 * (R - 1 + k))
                        sp.wait_ge(s_vec, i * (2 * R) + 2 * (R - 1 + k))
                        for m in range(2):
                            sp.dma_start(tokens[:, bass.ds(i * SET + 1, SET), :]
                                         .rearrange("c (g h) l -> c g h l", h=CH)[:, :, 2 * k + m],
                                         rows.rearrange("c (g h) l -> c g h l", h=CH)[:, :, 2 * k + m]).then_inc(s_stored, 16)

                with sp.Fori(0, SETS - 1) as i:
                    sp.wait_ge(s_rawfree, i + 1)
                    sp.dma_start(raw[:], spectra[:, bass.ds((i + 1) * SET, SET), :]).then_inc(s_raw, 16)
                    sp.wait_ge(s_ahi, i * 4 + 4)
                    sp.wait_ge(s_alo, i * 4 + 4)
                    sp.dma_start(attn_stage[:], attn_w[bass.ds(i + 1, 1)].rearrange("a p k d -> p (a k) d")).then_inc(s_attn, 16)
                    store(i)
                    sp.dma_start(read_t[:], readout[:, bass.ds((i + 1) * SET, SET), :]).then_inc(s_read, 16)
                store(SETS - 1)
                sp.wait_ge(s_stored, 64 * SETS)
                sp.wait_ge(s_cls, 16)

            @block.gpsimd
            def _(pool):
                pool.wait_ge(s_const, 16 * 6)
                pool.wait_ge(s_dve, 3)

                def ahead(i):
                    pool.wait_ge(s_pe, i * (4 * R) + (4 * BACK_READ + CHAINS))
                    build_back(nc.gpsimd, pool.wait_ge, i + 1)

                ahead(0)
                with pool.Fori(1, SETS - 1) as i:
                    ahead(i)

            @block.scalar
            def _(act):
                def copy(out, src, scale):
                    return nc.scalar.activation(out, src, ACT.Copy, scale=scale)

                act.wait_ge(s_dt, 32)
                nc.scalar.activation(half_dt[:], half_dt[:], ACT.Exp).then_inc(s_dt, 1)

                def forms(n, g):
                    act.wait_ge(s_back, n + 1)
                    nc.scalar.activation(chain(corr16, g), chain(minus_back, g), ACT.Abs)
                    nc.scalar.activation(chain(minus_back16, g), chain(minus_back, g), ACT.Copy).then_inc(s_abs, 1)

                def one_set(i, first, nxt):
                    for s, (kind, k) in enumerate(rounds):
                        for g in (0, 2):
                            act.wait_ge(s_pe, i * (4 * R) + (4 * s + g + 1))
                            if kind == "read" and k == 0 and not first:
                                act.wait_ge(s_stored, i * 64)
                            for out, src, scale in copies(kind, k, g):
                                last = copy(out, src, scale)
                            last.then_inc(s_act, 1)
                            if nxt and kind == "square" and k in FORMS and g == 0:
                                forms(i + 1, FORMS.index(k))
                        if kind == "square" and k in SPLITS:
                            r = SPLITS.index(k)
                            if r == 0:
                                act.wait_ge(s_attn, i * 16 + 16)
                            nc.scalar.activation(attn_hi[:, bass.ds(i, 1), r], attn_stage[:, r:r + 1], ACT.Copy,
                                                 scale=W_SCALE).then_inc(s_ahi, 1)

                for g in range(CHAINS):
                    forms(0, g)
                run_sets(act, one_set)

            @block.vector
            def _(dve):
                two_eyes = two_eye[:].rearrange("p (h m) -> p h m", m=P)

                def copy(kind, out, src, scale):
                    if kind in ("corr16", "corr32"):
                        return nc.vector.tensor_tensor(out, src, two_eyes, ALU.add)
                    if scale == 1.0:
                        return nc.vector.tensor_copy(out, src)
                    return nc.vector.tensor_scalar(out, src, scale, None, ALU.mult)

                dve.wait_ge(s_dt, 33)
                nc.vector.tensor_scalar(half_dt[:], half_dt[:], 0.5, None, ALU.mult).then_inc(s_dve, 1)
                dve.wait_ge(s_dve, 1)
                nc.vector.tensor_tensor(drive[:], drive[:], half_dt[:], ALU.mult).then_inc(s_dve, 1)
                half = P // 2
                nc.vector.tensor_copy(signed_dt[0:half], half_dt[0:half])
                nc.vector.tensor_scalar(signed_dt[half:P], half_dt[half:P], -1.0, None, ALU.mult).then_inc(s_dve, 1)
                dve.wait_ge(s_dve, 3)
                BEFORE, LINKS = 3, 4

                def link(ins, n, j):
                    ins.then_inc(s_dve, 1)
                    dve.wait_ge(s_dve, n * LINKS + (BEFORE + j))

                def row_sums(n, g):
                    dve.wait_ge(s_back, n + 1)
                    nc.vector.tensor_reduce(row_sum[:, CH * g:CH * g + CH], chain(minus_back, g), AX.X, ALU.add,
                                            apply_absolute_value=True).then_inc(s_norm, 1)

                def row_maxima(n):
                    dve.wait_ge(s_diag, n * NORM_STEPS + 1)
                    link(nc.vector.tensor_reduce(row_max[:], ps[0:SET, NORM_BANK, 0:P], AX.X, ALU.max), n, 1)
                    nc.vector.tensor_scalar(row_diag[:], eye32[0:SET, 0:SET], row_max[:, 0:1], None,
                                            ALU.mult).then_inc(s_bcast, 1)

                def row_norms(n):
                    dve.wait_ge(s_diag, n * NORM_STEPS + 2)
                    nc.vector.tensor_copy(row_norm[:], ps[:, NORM_BANK, 0:SET]).then_inc(s_rnorm, 1)

                def column_norms(n, chains):
                    for g in chains:
                        dve.wait_ge(s_diag, n * NORM_STEPS + (3 + g))
                        nc.vector.tensor_reduce(col_max[:, CH * g:CH * g + CH], bank4(g, 1), AX.X,
                                                ALU.max).then_inc(s_cmax, 1)

                def newton_start(n):
                    dve.wait_ge(s_rnorm, n + 1)
                    dve.wait_ge(s_cmax, n * CHAINS + CHAINS)
                    link(nc.vector.tensor_tensor(alpha[:], col_max[:], row_norm[:], ALU.mult), n, 2)
                    link(nc.vector.reciprocal(alpha[:], alpha[:]), n, 3)
                    link(nc.vector.tensor_scalar(alpha[:], alpha[:], -1.0, None, ALU.mult), n, 4)
                    nc.vector.tensor_tensor(inv16[:], minus_back[:],
                                            alpha[:].unsqueeze(2).broadcast_to([P, SET, P]),
                                            ALU.mult).then_inc(s_start, 1)

                def one_set(i, first, nxt):
                    for s, (kind, k) in enumerate(rounds):
                        for g in (1, 3):
                            dve.wait_ge(s_pe, i * (4 * R) + (4 * s + g + 1))
                            if kind == "read" and k == 0 and not first:
                                dve.wait_ge(s_stored, i * 64)
                            for out, src, scale in copies(kind, k, g):
                                last = copy(kind, out, src, scale)
                            last.then_inc(s_vec, 1)
                            if kind == "square" and k - 1 in SPLITS and g == 1:
                                r = SPLITS.index(k - 1)
                                dve.wait_ge(s_ahi, i * 4 + (r + 1))
                                nc.vector.scalar_tensor_tensor(attn_lo[:, bass.ds(i, 1), r], attn_stage[:, r:r + 1],
                                                               W_SCALE, attn_hi[:, bass.ds(i, 1), r],
                                                               ALU.mult, ALU.subtract).then_inc(s_alo, 1)
                            if nxt and (kind, k) == ("transpose", SUM_COLUMNS):
                                column_norms(i + 1, (g - 1, g))
                        if s == BACK_READ:
                            dve.wait_ge(s_read, i * 16 + 16)
                            nc.vector.tensor_scalar(read_t[64:P], read_t[64:P], -1.0, None, ALU.mult).then_inc(s_neg, 1)
                        if not nxt:
                            continue
                        if kind == "square" and k in SUMS:
                            row_sums(i + 1, SUMS.index(k))
                        if (kind, k) == ("transpose", TURN_ROWS):
                            row_maxima(i + 1)
                        if (kind, k) == ("transpose", SPREAD_ROWS):
                            row_norms(i + 1)
                        if kind == "last_double":
                            newton_start(i + 1)

                dve.wait_ge(s_raw, 16)
                dve.wait_ge(s_const, 16 * 6)
                build_back(nc.vector, dve.wait_ge, 0)
                for g in range(CHAINS):
                    row_sums(0, g)
                row_maxima(0)
                row_norms(0)
                column_norms(0, range(CHAINS))
                newton_start(0)
                run_sets(dve, one_set)

            @block.tensor
            def _(pe):
                mm = nc.tensor.matmul
                pe.wait_ge(s_const, 16 * 6)

                def turn_rows(n):
                    pe.wait_ge(s_norm, n * CHAINS + CHAINS)
                    nc.tensor.transpose(ps[0:SET, NORM_BANK, 0:P], row_sum[:], eye32[:]).then_inc(s_diag, 1)

                def spread_rows(n):
                    pe.wait_ge(s_bcast, n + 1)
                    mm(ps[:, NORM_BANK, 0:SET], ones32[0:SET, :], row_diag[:], start=True, stop=True).then_inc(s_diag, 1)

                def sum_columns(n, g):
                    if g == 0:
                        pe.wait_ge(s_abs, n * CHAINS + CHAINS)
                        pe.wait_ge(s_rnorm, n + 1)
                    mm(bank(g, 1), ones16[:], chain(corr16, g), start=True, stop=True).then_inc(s_diag, 1)

                def one_set(i, first, nxt):
                    pe.wait_ge(s_start, i + 1)
                    for s, (kind, k) in enumerate(rounds):
                        if (kind, k) == ("read", 0):
                            pe.wait_ge(s_neg, i + 1)
                        for g in range(CHAINS):
                            if s:
                                pe.wait_ge(s_vec if g % 2 else s_act, i * (2 * R) + (2 * (s - 1) + g // 2 + 1))
                            elif not first:
                                pe.wait_ge(s_vec if g % 2 else s_act, i * (2 * R) + (g // 2 - 1))
                            if nxt and (kind, k, g) == ("square", TURN_ROWS + 1, CHAINS - 1):
                                pe.wait_ge(s_bcast, i + 2)
                            if nxt and (kind, k, g) == ("square", SPREAD_ROWS + 1, CHAINS - 1):
                                pe.wait_ge(s_rnorm, i + 2)
                            if nxt and kind == "last_double":
                                pe.wait_ge(s_cmax, i * CHAINS + (CHAINS + g + 1))
                            hs = range(CH * g, CH * g + CH)
                            if kind in ("corr16", "corr32"):
                                x, b = (inv16, minus_back16) if kind == "corr16" else (inv32, minus_back)
                                add = g % 2 == 0
                                if add:
                                    mm(bank(g, 0), eye16[:], two_eye[:], start=True, stop=False)
                                for j, h in enumerate(hs):
                                    last = mm(bank4(g, 0)[:, j], x[:, h], b[:, h], start=not add,
                                              stop=not add or j == CH - 1)
                            elif kind in ("inv16", "inv32"):
                                x, c = (inv16, corr16) if kind == "inv16" else (inv32, corr32)
                                final = kind == "inv32" and k == EXACT - 1
                                if final:
                                    mm(bank(g, 1), eye16[:], half_eye[:], start=True, stop=False)
                                for j, h in enumerate(hs):
                                    last = mm(bank4(g, 1)[:, j], c[:, h], x[:, h], start=not final, stop=not final or j == CH - 1)
                            elif kind == "transpose":
                                for j, h in enumerate(hs):
                                    last = nc.tensor.transpose(bank4(g, 0)[:, j], power[:, h], eye32[:])
                            elif kind == "seed":
                                b = drive[:, bass.ds(i * SET + CH * g, CH)]
                                mm(bank(g, 1)[:, 0:CH], eye32[:], b, start=True, stop=False)
                                for j, h in enumerate(hs):
                                    last = mm(bank(g, 1)[:, j:j + 1], power_t[:, h],
                                              drive[:, bass.ds(i * SET + h, 1)], start=False, stop=j == CH - 1)
                            elif kind == "square":
                                n = 1 << k
                                for j, h in enumerate(hs):
                                    last = mm(pairs(g, 0, P + n)[:, j // 2, j % 2], power_t[:, h], wide[:, h, 0:P + n],
                                              start=True, stop=True)
                            elif kind == "last_double":
                                n = 1 << k
                                for j, h in enumerate(hs):
                                    last = mm(bank(g, j // 2)[:, (j % 2) * n:(j % 2 + 1) * n], power_t[:, h],
                                              krylov[:, h, 0:n], start=True, stop=True)
                            else:
                                for m in range(2):
                                    h = CH * g + 2 * k + m
                                    last = mm(bank(g, m)[0:CHANNELS], read_t[:, h], krylov[:, h, :], start=True,
                                              stop=True)
                            last.then_inc(s_pe, 1)
                            if nxt and (kind, k) == ("transpose", SUM_COLUMNS):
                                sum_columns(i + 1, g)
                        if nxt and (kind, k) == ("transpose", TURN_ROWS):
                            turn_rows(i + 1)
                        if nxt and (kind, k) == ("transpose", SPREAD_ROWS):
                            spread_rows(i + 1)

                turn_rows(0)
                spread_rows(0)
                for g in range(CHAINS):
                    sum_columns(0, g)
                run_sets(pe, one_set)


def attention_phase(nc, attn_pair, ffn_w, ffn_pair, biases, consts, tokens, mixed):
    eye32_d, eye_bf_d, causal_d, own_head_d = consts
    IMAGES, S, D = tokens.shape
    HEADS, DK = 16, 32
    QB = 4
    QUADS = IMAGES // QB
    T = QB * S
    KT = D // P
    G = P // DK
    EPS = 1e-5

    with ExitStack() as ctx:
        def sb(name, shape, dt):
            return ctx.enter_context(nc.sbuf_tensor(name, shape, dt))

        def sem(name):
            return ctx.enter_context(nc.semaphore(name))

        w_hi, w_lo = attn_pair
        f_hi, f_lo = ffn_pair
        PART = f_hi.shape[1] // QUADS
        stage = sb("b_stage", [P, PART], F32)
        bias = sb("bias", [P, 4, KT], F32)
        eye32 = sb("b_eye32", [P, P], F32)
        own_head = sb("own_head", [P, G], F32)
        eye_bf = sb("b_eye_bf", [S, S], BF16)
        causal = sb("causal", [S, KT * S], BF16)
        rows = sb("b_rows", [S, QB, D], F32)
        normed = sb("b_normed", [S, QB, D], F32)
        stats = sb("b_stats", [S, QB, 6], F32)
        mean = sb("b_mean", [S, QB], F32)
        gap = sb("b_gap", [S, QB], F32)
        spread = sb("b_spread", [S, QB], F32)
        var_eps = sb("b_var_eps", [S, QB], F32)
        rstd = sb("b_rstd", [S, QB], F32)
        minus_half = sb("b_minus_half", [S, QB], F32)
        x_hi = sb("b_x_hi", [P, 2, KT, T], F16)
        x_lo = sb("b_x_lo", [P, 2, KT, T], F16)
        q_t = sb("q_t", [P, 2, KT, T], F32)
        k_t = sb("k_t", [P, 2, KT, T], F32)
        k_diag = sb("k_diag", [P, KT, G, S], F32)
        v_t = sb("v_t", [P, KT, T], F32)
        v_rows = sb("v_rows", [S, 2, QB, HEADS, DK], F32)
        top = sb("top", [S, KT, G], F32)
        probs = sb("probs", [S, KT, G, S], F32)
        probs_t = sb("probs_t", [S, KT, G, S], F32)
        sums = sb("sums", [S, KT, G], F32)
        recip = sb("recip", [S, HEADS], F32)
        context = sb("context", [S, QB, HEADS, DK], F32)
        c_hi = sb("c_hi", [P, KT, T], F16)
        c_lo = sb("c_lo", [P, KT, T], F16)
        o_t = sb("o_t", [P, KT, T], F32)
        resid = sb("resid", [S, QB, D], F32)
        ps = ctx.enter_context(nc.psum_tensor("ps_attn", [P, 8, 512], F32))
        SCORES, CTX, WORK = 0, 4, 5

        s_const = sem("b_const")
        s_part = sem("b_ffn_part_loaded")
        s_fhi = sem("b_ffn_high")
        s_flo = sem("b_ffn_low")
        s_diag = sem("b_key_blocks")
        s_rows = sem("b_rows_loaded")
        s_resid = sem("b_resid_loaded")
        s_stored = sem("b_mixed_stored")
        s_stats = sem("b_stats")
        s_var = sem("b_variance")
        s_rstd = sem("b_rstd")
        s_normed = sem("b_normed")
        s_ones = sem("b_ones")
        s_moments = sem("b_moments")
        s_top = sem("b_maxima")
        s_sums = sem("b_softmax_sums")
        s_recip = sem("b_recips")
        s_scores = sem("b_scores")
        s_shift = sem("b_shifted")
        s_exp = sem("b_exponentials")
        s_pt = sem("b_probs_turned")
        s_pt_act = sem("b_probs_t_act")
        s_pt_dve = sem("b_probs_t_dve")
        s_ctx = sem("b_contexts")
        s_norm = sem("b_contexts_normed")
        KINDS = {"xt": "AD", "ct": "AD", "q": "A", "k": "A", "v": "A", "vt": "D", "wo": "A", "ot": "D"}
        s_unit = {k: sem(f"b_{k}_products") for k in KINDS}
        s_copy = {(k, e): sem(f"b_{k}_copied_{e}") for k, es in KINDS.items() for e in es}

        def count(n, j, per):
            return n * per + (j + 1)

        HEAVY = ("q", "k", "v", "wo")
        SLOTS = {}
        SOURCE = {"v": "xt", "vt": "v", "wo": "ct", "ot": "wo"}
        BANK = {}
        resting = [WORK, WORK + 1, WORK + 2]
        for b, (heavy, of, light, light_of) in enumerate((("v", 1, "ct", -1), ("wo", -1, "vt", 1),
                                                          ("k", 1, "ot", -1), ("q", 1, "xt", 2))):
            order = [x for j in range(4) for x in ((heavy, of, j), (light, light_of, j))]
            for kind, _, j in order:
                BANK[kind, j] = BANK[kind, j - 1] if (b % 2, kind, j) == (1, light, 3) else resting[0]
                resting.remove(BANK[kind, j])
                resting.append(BANK[kind, j])
            SLOTS[f"A{b}"] = order[0:5]
            SLOTS[f"B{b}"] = [order[5], order[6], order[7]]

        def units(name, q, prev, nxt, nxt2):
            here = {-1: prev, 1: nxt, 2: nxt2}
            return [(kind, q + of, j) for kind, of, j in SLOTS[name] if here[of]]

        assert resting == [WORK, WORK + 1, WORK + 2]

        def bank_of(kind, j, alone):
            if not alone:
                return BANK[kind, j]
            return WORK + j % 2 if kind in HEAVY else SCORES + j

        def last_units(q, prev, nxt, nxt2):
            last = {}
            for b in range(QB):
                for name in (f"A{b}", f"B{b}"):
                    for kind, n, j in units(name, q, prev, nxt, nxt2):
                        last[BANK[kind, j]] = (kind, n, j)
            return last

        START = [("xt", 0), ("v", 0), ("k", 0), ("vt", 0), ("q", 0), ("xt", 1)]
        FINISH = [("ct", QUADS - 1), ("wo", QUADS - 1), ("ot", QUADS - 1)]

        def whole(kinds):
            return [(kind, n, j) for kind, n in kinds for j in range(4)]

        def run_quads(eng, prologue, quad, epilogue):
            prologue()
            quad(0, 0, False, True, True)
            with eng.Fori(0, (QUADS - 4) // 2) as i:
                quad(i * 2 + 1, 1, True, True, True)
                quad(i * 2 + 2, 0, True, True, True)
            quad(QUADS - 3, 1, True, True, True)
            quad(QUADS - 2, 0, True, True, False)
            quad(QUADS - 1, 1, True, False, False)
            epilogue()

        with nc.Block() as block:

            @block.sync
            def _(sp):
                sp.dma_start(rows[:], tokens[0:QB].rearrange("b s d -> s b d")).then_inc(s_rows, 16)
                sp.dma_start(eye32[:], eye32_d).then_inc(s_const, 16)
                sp.dma_start(eye_bf[:], eye_bf_d).then_inc(s_const, 16)
                sp.dma_start(own_head[:], own_head_d).then_inc(s_const, 16)
                sp.dma_start(causal[:], causal_d).then_inc(s_const, 16)
                sp.dma_start(bias[:], biases).then_inc(s_const, 16)
                sp.dma_start(stage[:], ffn_w[:, 0:PART]).then_inc(s_part, 16)

                def load_part(n):
                    sp.wait_ge(s_fhi, n)
                    sp.wait_ge(s_flo, n)
                    sp.dma_start(stage[:], ffn_w[:, bass.ds(n * PART, PART)]).then_inc(s_part, 16)

                def store(n):
                    sp.wait_ge(s_copy["ot", "D"], count(n, 3, 4))
                    sp.dma_start(mixed[bass.ds(n * QB, QB)].rearrange("b s d -> s b d"), resid[:]).then_inc(s_stored, 16)

                def load_resid(n):
                    sp.dma_start(resid[:], tokens[bass.ds(n * QB, QB)].rearrange("b s d -> s b d")).then_inc(s_resid, 16)

                def load_rows(n):
                    sp.wait_ge(s_normed, count(n - 1, 3, 4))
                    sp.dma_start(rows[:], tokens[bass.ds(n * QB, QB)].rearrange("b s d -> s b d")).then_inc(s_rows, 16)

                load_resid(0)
                load_rows(1)
                load_rows(2)
                load_part(1)
                with sp.Fori(0, QUADS - 3) as n:
                    load_rows(n + 3)
                    store(n)
                    sp.wait_ge(s_stored, n * 16 + 16)
                    load_resid(n + 1)
                    load_part(n + 2)
                for n in range(QUADS - 3, QUADS):
                    store(n)
                    sp.wait_ge(s_stored, n * 16 + 16)
                    if n + 1 < QUADS:
                        load_resid(n + 1)
                    if n + 2 < QUADS:
                        load_part(n + 2)

            @block.gpsimd
            def _(pool):
                nc.gpsimd.memset(minus_half[:], -0.5).then_inc(s_ones, 1)
                pool.wait_ge(s_ones, 1)

                pool.wait_ge(s_const, 80)

                def root(n):
                    pool.wait_ge(s_var, n + 1)
                    nc.gpsimd.tensor_tensor(rstd[:], var_eps[:], minus_half[:], ALU.pow).then_inc(s_rstd, 1)

                def quad(q, par, prev, nxt, nxt2):
                    pool.wait_ge(s_copy["k", "A"], count(q, 3, 4))
                    for b in range(QB):
                        if prev or b:
                            pool.wait_ge(s_scores, count(q, b - 1, QB))
                        keys = k_t[:, par, :, b * S:(b + 1) * S].unsqueeze(2).broadcast_to([P, KT, G, S])
                        mine = own_head[:].unsqueeze(1).unsqueeze(3).broadcast_to([P, KT, G, S])
                        nc.gpsimd.tensor_tensor(k_diag[:], keys, mine, ALU.mult).then_inc(s_diag, 1)
                        if nxt2 and b == 2:
                            root(q + 2)

                def prologue():
                    root(0)
                    root(1)

                run_quads(pool, prologue, quad, lambda: None)

            @block.scalar
            def _(act):
                def copy_unit(kind, n, par, j, alone):
                    act.wait_ge(s_unit[kind], count(n, j, 4))
                    src = ps[:, bank_of(kind, j, alone)]
                    if kind in ("xt", "ct"):
                        dst = x_hi[:, 1 - par] if kind == "xt" else c_hi
                        ins = nc.scalar.activation(dst[:, j], src[:, 0:T], ACT.Copy)
                    elif kind in ("q", "k", "v"):
                        b = bias[:, "qkv".index(kind), j:j + 1]
                        dst = v_t[:, j] if kind == "v" else (q_t if kind == "q" else k_t)[:, par, j]
                        ins = nc.scalar.activation(dst, src[:, 0:T], ACT.Identity, bias=b,
                                                   scale=W_UNSCALE)
                    else:
                        ins = nc.scalar.activation(o_t[:, j], src[:, 0:T], ACT.Identity, bias=bias[:, 3, j:j + 1],
                                                   scale=W_UNSCALE)
                    ins.then_inc(s_copy[kind, "A"], 1)

                def fill(which, par, alone=False):
                    for kind, n, j in which:
                        if "A" in KINDS[kind]:
                            copy_unit(kind, n, 1 - par, j, alone)

                def prologue():
                    act.wait_ge(s_const, 80)
                    fill(whole(START[:1]), 0, True)
                    fill(whole(START[1:]), 1, True)

                def quad(q, par, prev, nxt, nxt2):
                    for b in range(QB):
                        beside = units(f"A{b}", q, prev, nxt, nxt2)
                        fill(beside[:3], par)
                        act.wait_ge(s_shift, count(q, b, QB))
                        nc.scalar.activation(probs[:], probs[:], ACT.Exp, scale=DK ** -0.5).then_inc(s_exp, 1)
                        fill(beside[3:], par)
                        act.wait_ge(s_pt, count(q, b, QB))
                        nc.scalar.activation(probs_t[:, 0:2], ps[0:S, SCORES:SCORES + 2, 0:G * S]
                                             .rearrange("p t (g k) -> p t g k", g=G), ACT.Copy).then_inc(s_pt_act, 1)
                        fill(units(f"B{b}", q, prev, nxt, nxt2), par)
                        if b == 2:
                            act.wait_ge(s_part, q * 16 + 16)
                            nc.scalar.activation(f_hi[:, bass.ds(q * PART, PART)], stage[:], ACT.Copy,
                                                 scale=W_SCALE).then_inc(s_fhi, 1)

                run_quads(act, prologue, quad, lambda: fill(whole(FINISH), 0, True))

            @block.vector
            def _(dve):
                def copy_unit(kind, n, par, j, alone):
                    dve.wait_ge(s_unit[kind], count(n, j, 4))
                    src = ps[:, bank_of(kind, j, alone)]
                    if kind in ("xt", "ct"):
                        hi, lo = (x_hi[:, 1 - par], x_lo[:, 1 - par]) if kind == "xt" else (c_hi, c_lo)
                        dve.wait_ge(s_copy[kind, "A"], count(n, j, 4))
                        ins = nc.vector.tensor_tensor(lo[:, j], src[:, 0:T], hi[:, j], ALU.subtract)
                    elif kind == "vt":
                        ins = nc.vector.tensor_copy(v_rows[:, par, j, :, 0:DK],
                                                    src[0:S].rearrange("p (h d) -> p h d", d=DK))
                    else:
                        if j == 0:
                            dve.wait_ge(s_resid, n * 16 + 16)
                        ins = nc.vector.tensor_tensor(resid[:, j], src[0:S], resid[:, j], ALU.add)
                    ins.then_inc(s_copy[kind, "D"], 1)

                def fill(which, par, alone=False):
                    for kind, n, j in which:
                        if "D" in KINDS[kind]:
                            copy_unit(kind, n, 1 - par, j, alone)

                def ln_stats(n, bs):
                    if bs[0] == 0:
                        dve.wait_ge(s_rows, n * 16 + 16)
                    for b in bs:
                        nc.vector.bn_stats(stats[:, b], rows[:, b]).then_inc(s_stats, 1)
                    if bs[-1] < QB - 1:
                        return
                    dve.wait_ge(s_stats, count(n, 3, 4))
                    tt = nc.vector.tensor_tensor
                    tt(mean[:], stats[:, :, 1], stats[:, :, 4], ALU.add)
                    tt(gap[:], stats[:, :, 1], stats[:, :, 4], ALU.subtract)
                    tt(spread[:], stats[:, :, 2], stats[:, :, 5], ALU.add).then_inc(s_moments, 1)
                    dve.wait_ge(s_moments, n * 2 + 1)
                    nc.vector.tensor_scalar(mean[:], mean[:], 0.5, None, ALU.mult)
                    tt(gap[:], gap[:], gap[:], ALU.mult)
                    nc.vector.tensor_scalar(spread[:], spread[:], 1.0 / D, EPS, ALU.mult,
                                            ALU.add).then_inc(s_moments, 1)
                    dve.wait_ge(s_moments, n * 2 + 2)
                    nc.vector.scalar_tensor_tensor(var_eps[:], gap[:], 0.25, spread[:], ALU.mult,
                                                   ALU.add).then_inc(s_var, 1)

                def ln_rows(n, bs):
                    if bs[0] == 0:
                        dve.wait_ge(s_rstd, n + 1)
                    for b in bs:
                        nc.vector.tensor_scalar(normed[:, b], rows[:, b], mean[:, b:b + 1], rstd[:, b:b + 1],
                                                ALU.subtract, ALU.mult).then_inc(s_normed, 1)

                def prologue():
                    for n in range(2):
                        ln_stats(n, (0, 1))
                        ln_stats(n, (2, 3))
                        ln_rows(n, (0, 1, 2, 3))
                        if n == 0:
                            fill(whole(START[:1]), 0, True)
                    fill(whole(START[1:]), 1, True)

                def quad(q, par, prev, nxt, nxt2):
                    for b in range(QB):
                        dve.wait_ge(s_scores, count(q, b, QB))
                        scores = ps[0:S, SCORES:SCORES + KT, 0:G * S].rearrange("p t (g k) -> p t g k", g=G)
                        nc.vector.tensor_reduce(top[:], scores, AX.X, ALU.max).then_inc(s_top, 1)
                        dve.wait_ge(s_top, count(q, b, QB))
                        nc.vector.tensor_tensor(probs[:], scores, top[:].unsqueeze(3).broadcast_to([S, KT, G, S]),
                                                ALU.subtract).then_inc(s_shift, 1)
                        fill(units(f"A{b}", q, prev, nxt, nxt2), par)
                        dve.wait_ge(s_exp, count(q, b, QB))
                        nc.vector.tensor_reduce(sums[:], probs[:], AX.X, ALU.add).then_inc(s_sums, 1)
                        dve.wait_ge(s_pt, count(q, b, QB))
                        nc.vector.tensor_copy(probs_t[:, 2:4], ps[0:S, SCORES + 2:SCORES + 4, 0:G * S]
                                              .rearrange("p t (g k) -> p t g k", g=G)).then_inc(s_pt_dve, 1)
                        fill(units(f"B{b}", q, prev, nxt, nxt2), par)
                        if nxt2 and b < 2:
                            ln_stats(q + 2, (2 * b, 2 * b + 1))
                        if nxt2 and b == 2:
                            ln_rows(q + 2, (0, 1, 2, 3))
                        if b == 3:
                            dve.wait_ge(s_fhi, q + 1)
                            nc.vector.scalar_tensor_tensor(f_lo[:, bass.ds(q * PART, PART)], stage[:], W_SCALE,
                                                           f_hi[:, bass.ds(q * PART, PART)], ALU.mult,
                                                           ALU.subtract).then_inc(s_flo, 1)
                        dve.wait_ge(s_sums, count(q, b, QB))
                        nc.vector.reciprocal(recip[:].rearrange("p (t g) -> p t g", g=G),
                                             sums[:]).then_inc(s_recip, 1)
                        dve.wait_ge(s_recip, count(q, b, QB))
                        dve.wait_ge(s_ctx, count(q, b, QB))
                        nc.vector.tensor_tensor(context[:, b],
                                                ps[0:S, CTX].rearrange("p (h d) -> p h d", d=DK),
                                                recip[:].unsqueeze(2).broadcast_to([S, HEADS, DK]),
                                                ALU.mult).then_inc(s_norm, 1)

                run_quads(dve, prologue, quad, lambda: fill(whole(FINISH), 0, True))

            @block.tensor
            def _(pe):
                mm = nc.tensor.matmul
                recent = {}

                def unit(kind, n, j, par, alone):
                    w = bank_of(kind, j, alone)
                    before = recent.get(w)
                    if before is not None and not (j == 0 and SOURCE.get(kind) == before[0]):
                        for e in KINDS[before[0]]:
                            pe.wait_ge(s_copy[before[0], e], count(before[1], before[2], 4))
                    recent[w] = (kind, n, j)
                    out = ps[:, w]
                    if kind == "xt":
                        if j == 0:
                            pe.wait_ge(s_normed, count(n, 3, 4))
                        for b in range(QB):
                            last = nc.tensor.transpose(out[:, b * S:(b + 1) * S], normed[:, b, j * P:(j + 1) * P],
                                                       eye32[0:S, 0:S])
                    elif kind == "ct":
                        if j == 0:
                            pe.wait_ge(s_norm, count(n, 3, 4))
                        for b in range(QB):
                            flat = context[:, b].rearrange("p h d -> p (h d)")
                            last = nc.tensor.transpose(out[:, b * S:(b + 1) * S], flat[:, j * P:(j + 1) * P],
                                                       eye32[0:S, 0:S])
                    elif kind in ("q", "k", "v", "wo"):
                        m = ("q", "k", "v", "wo").index(kind)
                        hi, lo = (c_hi, c_lo) if kind == "wo" else (x_hi[:, 1 - par], x_lo[:, 1 - par])
                        src = "ct" if kind == "wo" else "xt"
                        if j == 0 and kind in ("v", "wo"):
                            pe.wait_ge(s_copy[src, "A"], count(n, 3, 4))
                            pe.wait_ge(s_copy[src, "D"], count(n, 3, 4))
                        for k in range(KT):
                            for i, (a, x) in enumerate(((w_hi, hi), (w_hi, lo), (w_lo, hi))):
                                last = mm(out[:, 0:T], a[:, m, k, j * P:(j + 1) * P], x[:, k],
                                          start=k == 0 and i == 0, stop=k == KT - 1 and i == 2)
                    elif kind == "vt":
                        if j == 0:
                            pe.wait_ge(s_copy["v", "A"], count(n, 3, 4))
                        for t in range(KT):
                            last = nc.tensor.transpose(out[0:S, t * P:(t + 1) * P], v_t[:, t, j * S:(j + 1) * S],
                                                       eye32[:])
                    else:
                        if j == 0:
                            pe.wait_ge(s_copy["wo", "A"], count(n, 3, 4))
                        for t in range(KT):
                            last = nc.tensor.transpose(out[0:S, t * P:(t + 1) * P], o_t[:, t, j * S:(j + 1) * S],
                                                       eye32[:])
                    last.then_inc(s_unit[kind], 1)

                def fill(which, par, alone=False):
                    for kind, n, j in which:
                        unit(kind, n, j, par, alone)

                def prologue():
                    pe.wait_ge(s_const, 80)
                    fill(whole(START), 1, True)

                def quad(q, par, prev, nxt, nxt2):
                    recent.clear()
                    if prev:
                        recent.update(last_units(q - 1, False, True, nxt))
                    else:
                        recent.update({WORK: ("q", q, 2), WORK + 1: ("q", q, 3)})
                        pe.wait_ge(s_copy["xt", "D"], count(q + 1, 3, 4))
                    pe.wait_ge(s_copy["q", "A"], count(q, 3, 4))
                    for b in range(QB):
                        if prev or b:
                            pe.wait_ge(s_pt_act, count(q, b - 1, QB))
                            pe.wait_ge(s_pt_dve, count(q, b - 1, QB))
                        for t in range(KT):
                            mm(ps[0:S, SCORES + t, 0:G * S], eye_bf[:], causal[:], start=True, stop=False)
                        pe.wait_ge(s_diag, count(q, b, QB))
                        for t in range(KT):
                            last = mm(ps[0:S, SCORES + t, 0:G * S], q_t[:, par, t, b * S:(b + 1) * S],
                                      k_diag[:, t].rearrange("p g k -> p (g k)"), start=False, stop=True)
                        last.then_inc(s_scores, 1)
                        fill(units(f"A{b}", q, prev, nxt, nxt2), par)
                        pe.wait_ge(s_exp, count(q, b, QB))
                        for t in range(KT):
                            for g in range(G):
                                last = nc.tensor.transpose(ps[0:S, SCORES + t, g * S:(g + 1) * S], probs[:, t, g],
                                                           eye32[0:S, 0:S])
                        last.then_inc(s_pt, 1)
                        fill(units(f"B{b}", q, prev, nxt, nxt2), par)
                        pe.wait_ge(s_pt_act, count(q, b, QB))
                        pe.wait_ge(s_pt_dve, count(q, b, QB))
                        if b == 0:
                            pe.wait_ge(s_copy["vt", "D"], count(q, 3, 4))
                        if prev or b:
                            pe.wait_ge(s_norm, count(q, b - 1, QB))
                        for h in range(HEADS):
                            last = mm(ps[0:S, CTX, h * DK:(h + 1) * DK], probs_t[:, h // G, h % G], v_rows[:, par, b, h], start=True, stop=True)
                        last.then_inc(s_ctx, 1)

                run_quads(pe, prologue, quad, lambda: fill(whole(FINISH), 0, True))


def expert_phase(nc, weights, ready_pair, consts, mixed, out):
    eye32_d, iota_d, select_d = consts
    TOKENS, D = mixed.shape
    E, R = 8, 32
    ER = E * R
    F = 1792
    KT, FT, ET = D // P, F // P, ER // P
    PAIRS = FT // 2
    T = 208
    BLOCKS = TOKENS // T
    TR = 104
    TT = T // TR
    EPS = 1e-5
    BIG = 3e38

    HEAD = 2 * KT * ER + KT * E
    PAIR = 2 * KT * 2 * P + 2 * ET * 2 * P + 2 * ER
    W2_AT = HEAD + PAIRS * PAIR
    B2_AT = W2_AT + FT * D
    WIDTH = B2_AT + ET * D
    PC = PAIR // 4
    READY = ready_pair[0].shape[1]
    READY_PAIRS = (READY - HEAD) // PAIR
    assert READY == HEAD + READY_PAIRS * PAIR
    CHUNKS = [(HEAD + PC * c, PC) for c in range(4 * READY_PAIRS, 4 * PAIRS)] \
        + [(W2_AT + PC * c, PC) for c in range(8)] + [(B2_AT + D * t, D) for t in range(ET)]
    STAGE = max(w for _, w in CHUNKS)
    STAGES = 4
    assert W2_AT + 8 * PC == B2_AT and weights.shape[1] == WIDTH

    with ExitStack() as ctx:
        def sb(name, shape, dt):
            return ctx.enter_context(nc.sbuf_tensor(name, shape, dt))

        def sem(name):
            return ctx.enter_context(nc.semaphore(name))

        ready_hi, ready_lo = ready_pair
        rest_hi = sb("f_rest_hi", [P, WIDTH - READY], F16)
        rest_lo = sb("f_rest_lo", [P, WIDTH - READY], F16)
        stage = sb("f_stage", [P, STAGES, STAGE], F32)
        eye32 = sb("f_eye32", [P, P], F32)
        iota = sb("f_iota", [TR, TT, E], F32)
        select = sb("f_select", [32, 8, P], F16)
        rows = sb("f_rows", [TR, TT, D], F32)
        resid = sb("f_resid", [TR, TT, D], F32)
        stats = sb("f_stats", [TR, TT, 6], F32)
        mean = sb("f_mean", [TR, TT], F32)
        gap = sb("f_gap", [TR, TT], F32)
        spread = sb("f_spread", [TR, TT], F32)
        var_eps = sb("f_var_eps", [TR, TT], F32)
        rstd = sb("f_rstd", [TR, TT], F32)
        minus_half = sb("f_minus_half", [TR, TT], F32)
        euler = sb("f_euler", [TR, TT], F32)
        logits = sb("f_logits", [TR, TT, E], F32)
        logits2 = sb("f_logits2", [TR, TT, E], F32)
        rank = sb("f_rank", [TR, TT, E], F32)
        best = sb("f_best", [TR, TT], F32)
        best2 = sb("f_best2", [TR, TT], F32)
        first_at = sb("f_first_at", [TR, TT], F32)
        drop = sb("f_drop", [TR, TT], F32)
        odds = sb("f_odds", [TR, TT], F32)
        total = sb("f_total", [TR, TT], F32)
        route = sb("f_route", [TR, TT, 32], F32)
        route_hi = sb("f_route_hi", [32, T], F16)
        route_lo = sb("f_route_lo", [32, T], F16)
        x_hi = sb("f_x_hi", [P, KT, T], F16)
        x_lo = sb("f_x_lo", [P, KT, T], F16)
        a_hi = sb("f_a_hi", [P, ET, T], F16)
        a_lo = sb("f_a_lo", [P, ET, T], F16)
        am_hi = sb("f_am_hi", [P, 2, 2, ET, T], F16)
        am_lo = sb("f_am_lo", [P, 2, 2, ET, T], F16)
        mask = sb("f_mask", [P, 3, ET, T], F16)
        weight = sb("f_weight", [P, 2, T], F32)
        gate = sb("f_gate", [P, 2, T], F32)
        y0 = sb("f_y0", [P, 4, T], F32)
        y1 = sb("f_y1", [P, 2, T], F32)
        y_hi = sb("f_y_hi", [P, 2, 2, 2, T], F16)
        y_lo = sb("f_y_lo", [P, 2, 2, 2, T], F16)
        sum_hi = sb("f_sum_hi", [P, FT, T], F16)
        sum_lo = sb("f_sum_lo", [P, FT, T], F16)
        m_32 = sb("f_m_32", [P, ET, T], F32)
        m_hi = sb("f_m_hi", [P, ET, T], F16)
        m_lo = sb("f_m_lo", [P, ET, T], F16)
        o_t = y0
        ps = ctx.enter_context(nc.psum_tensor("ps_ffn", [P, 8, 512], F32))

        def bank(n):
            return ps[:, n, 0:2 * T].rearrange("p (a t) -> p a t", a=2)

        A2, DOWN = 4, 6

        def w1(m, p, k, j):
            return HEAD + p * PAIR + (m * KT + k) * 2 * P + j * P

        def b1(m, p, k, j):
            return HEAD + p * PAIR + 2 * KT * 2 * P + (m * ET + k) * 2 * P + j * P

        def a2(p, j, t):
            return HEAD + p * PAIR + 2 * (KT + ET) * 2 * P + j * ER + t * P

        def a1(m, k, t):
            return (m * KT + k) * ER + t * P

        names = ("const", "whi", "wlo", "rows", "resid", "stored", "stats", "moments", "var", "rstd", "normed",
                 "ones", "xt", "xhi", "xlo", "logits", "router", "drop", "odds", "route", "rt", "rhi", "rlo",
                 "expand", "exp_act", "low", "ahi", "alo", "am", "first", "second", "silu", "scaled", "y", "yhi",
                 "ylo", "sum", "shi", "slo", "acc0", "acc1", "masked", "mhi", "mlo", "down", "ot", "turned", "added")
        S = {n: sem("f_" + n) for n in names}
        s_wload = [sem(f"f_weights_loaded{n}") for n in range(STAGES)]

        def at(n, per, j):
            return n * per + (j + 1)

        def turn(slot, p):
            if slot == 0:
                return max(2 * p - 1, 0)
            return min(2 * p + 2, 2 * PAIRS - 1)

        def halves(col, width):
            if col < READY:
                return ready_hi[:, col:col + width], ready_lo[:, col:col + width]
            return rest_hi[:, col - READY:col - READY + width], rest_lo[:, col - READY:col - READY + width]

        def chunks_until(p):
            return max(0, 4 * (p + 1 - READY_PAIRS))

        def block_chunks(p):
            per = -(-len(CHUNKS) // (PAIRS - 1))
            return range(len(CHUNKS))[p * per:(p + 1) * per]

        def run_blocks(eng, prologue, body, epilogue):
            prologue()
            body(0, True, True)
            with eng.Fori(1, BLOCKS - 1) as n:
                body(n, False, True)
            body(BLOCKS - 1, False, False)
            epilogue()

        def token_rows(dram, n):
            return dram[bass.ds(n * T, T)].rearrange("(a p) d -> p a d", p=TR)

        with nc.Block() as block:

            @block.sync
            def _(sp):
                sp.dma_start(rows[:], token_rows(mixed, 0)).then_inc(S["rows"], 16)
                for dst, src in ((eye32, eye32_d), (iota, iota_d), (select, select_d)):
                    sp.dma_start(dst[:], src).then_inc(S["const"], 16)
                sp.dma_start(resid[:], token_rows(mixed, 0)).then_inc(S["resid"], 16)
                for c, (start, width) in enumerate(CHUNKS):
                    if c >= STAGES:
                        sp.wait_ge(S["whi"], c - STAGES + 1)
                        sp.wait_ge(S["wlo"], c - STAGES + 1)
                    sp.dma_start(stage[:, c % STAGES, 0:width],
                                 weights[:, start:start + width]).then_inc(s_wload[c % STAGES], 16)
                    if c == 3:
                        sp.wait_ge(S["xt"], 2)
                        sp.dma_start(rows[:], token_rows(mixed, 1)).then_inc(S["rows"], 16)

                def store(n):
                    sp.wait_ge(S["added"], at(n, 2, 1))
                    sp.dma_start(token_rows(out, n), resid[:]).then_inc(S["stored"], 16)
                    sp.wait_ge(S["stored"], n * 16 + 16)

                with sp.Fori(0, BLOCKS - 2) as n:
                    sp.wait_ge(S["xt"], at(n + 1, 2, 1))
                    sp.dma_start(rows[:], token_rows(mixed, n + 2)).then_inc(S["rows"], 16)
                    store(n)
                    sp.dma_start(resid[:], token_rows(mixed, n + 1)).then_inc(S["resid"], 16)
                store(BLOCKS - 2)
                sp.dma_start(resid[:], token_rows(mixed, BLOCKS - 1)).then_inc(S["resid"], 16)
                store(BLOCKS - 1)

            @block.gpsimd
            def _(pool):
                nc.gpsimd.memset(minus_half[:], -0.5)
                nc.gpsimd.memset(euler[:], 2.718281828459045)
                nc.gpsimd.memset(route[:], 0.0).then_inc(S["ones"], 1)
                pool.wait_ge(S["ones"], 1)

                def one(n):
                    pool.wait_ge(S["var"], n + 1)
                    nc.gpsimd.tensor_tensor(rstd[:], var_eps[:], minus_half[:], ALU.pow).then_inc(S["rstd"], 1)
                    pool.wait_ge(S["drop"], n + 1)
                    nc.gpsimd.tensor_tensor(odds[:], euler[:], drop[:], ALU.pow).then_inc(S["odds"], 1)

                one(0)
                with pool.Fori(1, BLOCKS) as n:
                    one(n)

            @block.scalar
            def _(act):
                cp = nc.scalar.activation

                def split(c):
                    start, width = CHUNKS[c]
                    act.wait_ge(s_wload[c % STAGES], 16 * (c // STAGES + 1))
                    cp(halves(start, width)[0], stage[:, c % STAGES, 0:width], ACT.Copy,
                       scale=W_SCALE).then_inc(S["whi"], 1)

                def route_copy(n):
                    act.wait_ge(S["rt"], at(n, 1, 0))
                    cp(route_hi[:], ps[0:32, 1, 0:T], ACT.Copy).then_inc(S["rhi"], 1)
                    act.wait_ge(S["expand"], at(n, 4, 1))
                    for m in range(2):
                        last = cp(mask[:, m], bank(m), ACT.Copy)
                    last.then_inc(S["exp_act"], 1)
                    act.wait_ge(S["expand"], at(n, 4, 3))
                    cp(mask[:, 2], bank(4), ACT.Copy)
                    cp(weight[:], bank(5), ACT.Copy).then_inc(S["exp_act"], 1)

                def read_out(slot, n, p, first):
                    par = p % 2
                    k = turn(slot, p)
                    act.wait_ge(S["second" if slot else "first"], at(n, 2 * PAIRS, 2 * p))
                    cp(gate[:], bank(2 * par), ACT.Silu, scale=W_UNSCALE).then_inc(S["silu"], 1)
                    act.wait_ge(S["y"], at(n, 2 * PAIRS, k))
                    src = y1[:] if slot else y0[:, 2 * par:2 * par + 2]
                    cp(y_hi[:, par, slot], src, ACT.Copy).then_inc(S["yhi"], 1)
                    if slot:
                        act.wait_ge(S["sum"], at(n, PAIRS, p))
                        cp(sum_hi[:, 2 * p:2 * p + 2], y1[:], ACT.Copy).then_inc(S["shi"], 1)

                def prologue():
                    prep_all(0)

                def prep_all(n):
                    for u in range(2):
                        act.wait_ge(S["xt"], at(n, 2, u))
                        cp(x_hi[:, 2 * u:2 * u + 2], bank(2 + u), ACT.Copy).then_inc(S["xhi"], 1)
                    route_copy(n)
                    for m in range(2):
                        act.wait_ge(S["low"], at(n, 2, m))
                        if m:
                            act.wait_ge(S["am"], at(n, 2, 0))
                        cp(a_hi[:], bank(2 + m), ACT.Copy, scale=W_UNSCALE).then_inc(S["ahi"], 1)

                def body(n, first, nxt):
                    read_out(0, n, 0, first)
                    for p in range(PAIRS):
                        if first:
                            for c in block_chunks(p):
                                split(c)
                        if p + 1 < PAIRS:
                            read_out(0, n, p + 1, first)
                        read_out(1, n, p, first)
                    if nxt:
                        for u in range(2):
                            act.wait_ge(S["xt"], at(n + 1, 2, u))
                            cp(x_hi[:, 2 * u:2 * u + 2], bank(2 + u), ACT.Copy).then_inc(S["xhi"], 1)
                    act.wait_ge(S["masked"], at(n, 3, 2))
                    cp(m_hi[:], m_32[:], ACT.Copy).then_inc(S["mhi"], 1)
                    if nxt:
                        route_copy(n + 1)
                        for m in range(2):
                            act.wait_ge(S["low"], at(n + 1, 2, m))
                            if m:
                                act.wait_ge(S["am"], at(n + 1, 2, 0))
                            cp(a_hi[:], bank(2 + m), ACT.Copy, scale=W_UNSCALE).then_inc(S["ahi"], 1)
                    for u in range(2):
                        act.wait_ge(S["down"], at(n, 2, u))
                        cp(o_t[:, 2 * u:2 * u + 2], bank(DOWN + u), ACT.Copy, scale=W_UNSCALE).then_inc(S["ot"], 1)

                run_blocks(act, prologue, body, lambda: None)

            @block.vector
            def _(dve):
                tt, ts, stt = nc.vector.tensor_tensor, nc.vector.tensor_scalar, nc.vector.scalar_tensor_tensor
                ROUTER = 13

                def spread_e(small):
                    return small.unsqueeze(2).broadcast_to([TR, TT, E])

                def split(c):
                    start, width = CHUNKS[c]
                    dve.wait_ge(S["whi"], c + 1)
                    hi, lo = halves(start, width)
                    stt(lo, stage[:, c % STAGES, 0:width], W_SCALE, hi, ALU.mult, ALU.subtract).then_inc(S["wlo"], 1)

                def ln_stats(n):
                    dve.wait_ge(S["rows"], n * 16 + 16)
                    for b in range(TT):
                        nc.vector.bn_stats(stats[:, b], rows[:, b]).then_inc(S["stats"], 1)
                    dve.wait_ge(S["stats"], at(n, TT, TT - 1))
                    tt(mean[:], stats[:, :, 1], stats[:, :, 4], ALU.add)
                    tt(gap[:], stats[:, :, 1], stats[:, :, 4], ALU.subtract)
                    tt(spread[:], stats[:, :, 2], stats[:, :, 5], ALU.add).then_inc(S["moments"], 1)
                    dve.wait_ge(S["moments"], n * 2 + 1)
                    ts(mean[:], mean[:], 0.5, None, ALU.mult)
                    tt(gap[:], gap[:], gap[:], ALU.mult)
                    ts(spread[:], spread[:], 1.0 / D, EPS, ALU.mult, ALU.add).then_inc(S["moments"], 1)
                    dve.wait_ge(S["moments"], n * 2 + 2)
                    stt(var_eps[:], gap[:], 0.25, spread[:], ALU.mult, ALU.add).then_inc(S["var"], 1)

                def ln_rows(n):
                    dve.wait_ge(S["rstd"], n + 1)
                    for b in range(TT):
                        last = ts(rows[:, b], rows[:, b], mean[:, b:b + 1], rstd[:, b:b + 1],
                                  ALU.subtract, ALU.mult)
                    last.then_inc(S["normed"], 1)

                def x_low(n):
                    for u in range(2):
                        dve.wait_ge(S["xhi"], at(n, 2, u))
                        tt(x_lo[:, 2 * u:2 * u + 2], bank(2 + u), x_hi[:, 2 * u:2 * u + 2],
                           ALU.subtract).then_inc(S["xlo"], 1)

                def router(n):
                    count = [0]

                    def link(ins):
                        count[0] += 1
                        ins.then_inc(S["router"], 1)
                        dve.wait_ge(S["router"], at(n, ROUTER, count[0] - 1))

                    dve.wait_ge(S["logits"], n + 1)
                    link(ts(logits[:], ps[0:TR, 0, 0:TT * E].rearrange("p (a e) -> p a e", e=E), W_UNSCALE, None,
                            ALU.mult))
                    link(nc.vector.tensor_reduce(best[:], logits[:], AX.X, ALU.max))
                    link(tt(rank[:], logits[:], spread_e(best[:]), ALU.is_lt))
                    link(stt(rank[:], rank[:], float(E), iota[:], ALU.mult, ALU.add))
                    link(nc.vector.tensor_reduce(first_at[:], rank[:], AX.X, ALU.min))
                    link(tt(route[:, :, 0:E], iota[:], spread_e(first_at[:]), ALU.is_equal))
                    link(stt(logits2[:], route[:, :, 0:E], -BIG, logits[:], ALU.mult, ALU.add))
                    link(nc.vector.tensor_reduce(best2[:], logits2[:], AX.X, ALU.max))
                    tt(drop[:], best2[:], best[:], ALU.subtract).then_inc(S["drop"], 1)
                    link(tt(rank[:], logits2[:], spread_e(best2[:]), ALU.is_lt))
                    link(stt(rank[:], rank[:], float(E), iota[:], ALU.mult, ALU.add))
                    link(nc.vector.tensor_reduce(first_at[:], rank[:], AX.X, ALU.min))
                    tt(route[:, :, E:2 * E], iota[:], spread_e(first_at[:]), ALU.is_equal)
                    dve.wait_ge(S["odds"], n + 1)
                    link(ts(total[:], odds[:], 1.0, None, ALU.add))
                    link(nc.vector.reciprocal(route[:, :, 2 * E], total[:]))
                    tt(route[:, :, 2 * E + 1], odds[:], route[:, :, 2 * E], ALU.mult).then_inc(S["route"], 1)
                    assert count[0] == ROUTER

                def route_low(n):
                    dve.wait_ge(S["rhi"], n + 1)
                    tt(route_lo[:], ps[0:32, 1, 0:T], route_hi[:], ALU.subtract).then_inc(S["rlo"], 1)

                def mask_low_rank(n):
                    dve.wait_ge(S["exp_act"], at(n, 2, 1))
                    for m in range(2):
                        dve.wait_ge(S["ahi"], at(n, 2, m))
                        stt(a_lo[:], bank(2 + m), W_UNSCALE, a_hi[:], ALU.mult, ALU.subtract).then_inc(S["alo"], 1)
                        dve.wait_ge(S["alo"], at(n, 2, m))
                        for slot in range(2):
                            tt(am_hi[:, slot, m], a_hi[:], mask[:, 2 * slot], ALU.mult)
                            last = tt(am_lo[:, slot, m], a_lo[:], mask[:, 2 * slot], ALU.mult)
                        last.then_inc(S["am"], 1)

                def read_out(slot, n, p, first):
                    par = p % 2
                    k = turn(slot, p)
                    dve.wait_ge(S["silu"], at(n, 2 * PAIRS, k))
                    tt(gate[:], gate[:], weight[:, slot].unsqueeze(1).broadcast_to([P, 2, T]),
                       ALU.mult).then_inc(S["scaled"], 1)
                    dve.wait_ge(S["scaled"], at(n, 2 * PAIRS, k))
                    dst = y1[:] if slot else y0[:, 2 * par:2 * par + 2]
                    if slot == 0 and p < 2 and not first:
                        dve.wait_ge(S["turned"], at(n - 1, 2, 1))
                    dve.wait_ge(S["second" if slot else "first"], at(n, 2 * PAIRS, 2 * p + 1))
                    stt(dst, bank(2 * par + 1), W_UNSCALE, gate[:], ALU.mult, ALU.mult).then_inc(S["y"], 1)
                    dve.wait_ge(S["yhi"], at(n, 2 * PAIRS, k))
                    tt(y_lo[:, par, slot], dst, y_hi[:, par, slot], ALU.subtract).then_inc(S["ylo"], 1)
                    if slot:
                        tt(y1[:], y1[:], y0[:, 2 * par:2 * par + 2], ALU.add).then_inc(S["sum"], 1)
                        dve.wait_ge(S["shi"], at(n, PAIRS, p))
                        tt(sum_lo[:, 2 * p:2 * p + 2], y1[:], sum_hi[:, 2 * p:2 * p + 2],
                           ALU.subtract).then_inc(S["slo"], 1)

                def masked(n):
                    dve.wait_ge(S["acc1"], n + 1)
                    stt(m_32[:], bank(A2), W_UNSCALE, mask[:, 0], ALU.mult, ALU.mult)
                    stt(gate[:], bank(A2 + 1), W_UNSCALE, mask[:, 1], ALU.mult, ALU.mult).then_inc(S["masked"], 2)
                    dve.wait_ge(S["masked"], at(n, 3, 1))
                    tt(m_32[:], m_32[:], gate[:], ALU.add).then_inc(S["masked"], 1)
                    dve.wait_ge(S["mhi"], n + 1)
                    tt(m_lo[:], m_32[:], m_hi[:], ALU.subtract).then_inc(S["mlo"], 1)

                def add_rows(n):
                    dve.wait_ge(S["resid"], n * 16 + 16)
                    for u in range(TT):
                        dve.wait_ge(S["turned"], at(n, 2, u))
                        tt(resid[:, u], ps[0:TR, DOWN + u, :], resid[:, u], ALU.add).then_inc(S["added"], 1)

                def prologue():
                    dve.wait_ge(S["const"], 48)
                    dve.wait_ge(S["ones"], 1)
                    ln_stats(0)
                    ln_rows(0)
                    x_low(0)
                    router(0)
                    route_low(0)
                    mask_low_rank(0)

                def body(n, first, nxt):
                    read_out(0, n, 0, first)
                    if not first:
                        add_rows(n - 1)
                    for p in range(PAIRS):
                        if first:
                            for c in block_chunks(p):
                                split(c)
                        if p + 1 < PAIRS:
                            read_out(0, n, p + 1, first)
                        read_out(1, n, p, first)
                        if nxt and p == 1:
                            ln_stats(n + 1)
                        if nxt and p == 3:
                            ln_rows(n + 1)
                    if nxt:
                        x_low(n + 1)
                    masked(n)
                    if nxt:
                        router(n + 1)
                        route_low(n + 1)
                        mask_low_rank(n + 1)

                run_blocks(dve, prologue, body, lambda: add_rows(BLOCKS - 1))

            @block.tensor
            def _(pe):
                mm = nc.tensor.matmul

                def triple(out_ap, col, x, xl, start, stop, skip=False):
                    hi, lo = halves(col, P)
                    mm(out_ap, hi, x, start=start, stop=False, skip_group_check=skip)
                    mm(out_ap, hi, xl, start=False, stop=False, skip_group_check=skip)
                    return mm(out_ap, lo, x, start=False, stop=stop, skip_group_check=skip)

                def base(n, p, first):
                    par = p % 2
                    if first and chunks_until(p):
                        pe.wait_ge(S["wlo"], chunks_until(p))
                    for m in range(2):
                        if p >= 2:
                            pe.wait_ge(S["y" if m else "silu"], at(n, 2 * PAIRS, turn(1, p - 2)))
                        for j in range(2):
                            for k in range(KT):
                                triple(bank(2 * par + m)[:, j], w1(m, p, k, j), x_hi[:, k], x_lo[:, k],
                                       j == 0 and k == 0, False)
                        if p == 0:
                            pe.wait_ge(S["am"], at(n, 2, m))
                        for j in range(2):
                            for k in range(ET):
                                last = triple(bank(2 * par + m)[:, j], b1(m, p, k, j), am_hi[:, 0, m, k],
                                              am_lo[:, 0, m, k], False, j == 1 and k == ET - 1)
                        last.then_inc(S["first"], 1)

                def delta(n, p):
                    par = p % 2
                    for m in range(2):
                        pe.wait_ge(S["y" if m else "silu"], at(n, 2 * PAIRS, turn(0, p)))
                        for j in range(2):
                            for k in range(ET):
                                last = triple(bank(2 * par + m)[:, j], b1(m, p, k, j), am_hi[:, 1, m, k],
                                              am_lo[:, 1, m, k], False, False, skip=True)
                        last.then_inc(S["second"], 1)

                def down_low(n, p, slot):
                    par = p % 2
                    pe.wait_ge(S["ylo"], at(n, 2 * PAIRS, turn(slot, p)))
                    for t in range(ET):
                        for j in range(2):
                            last = triple(bank(A2 + slot)[:, t], a2(p, j, t), y_hi[:, par, slot, j],
                                          y_lo[:, par, slot, j], p == 0 and t == 0 and j == 0,
                                          p == PAIRS - 1 and t == ET - 1 and j == 1)
                    if p == PAIRS - 1:
                        last.then_inc(S[f"acc{slot}"], 1)

                def down(h, fs):
                    for f in fs:
                        triple(bank(DOWN + h // 2)[:, h % 2], W2_AT + f * D + h * P, sum_hi[:, f], sum_lo[:, f],
                               f == 0 and h % 2 == 0, False)

                def turn_rows(n):
                    pe.wait_ge(S["normed"], n + 1)
                    for u in range(2):
                        for k in (2 * u, 2 * u + 1):
                            for b in range(TT):
                                last = nc.tensor.transpose(bank(2 + u)[:, k % 2, b * TR:(b + 1) * TR],
                                                           rows[:, b, k * P:(k + 1) * P], eye32[0:TR, 0:TR])
                        last.then_inc(S["xt"], 1)

                def logit(n):
                    pe.wait_ge(S["xlo"], at(n, 2, 1))
                    for b in range(TT):
                        for k in range(KT):
                            hi, lo = halves(2 * KT * ER + k * E, E)
                            xs = slice(b * TR, (b + 1) * TR)
                            o = ps[0:TR, 0, b * E:(b + 1) * E]
                            mm(o, x_hi[:, k, xs], hi, start=k == 0, stop=False)
                            mm(o, x_hi[:, k, xs], lo, start=False, stop=False)
                            last = mm(o, x_lo[:, k, xs], hi, start=False, stop=k == KT - 1)
                    last.then_inc(S["logits"], 1)

                def low_rank(n):
                    for m in range(2):
                        for t in range(ET):
                            for k in range(KT):
                                last = triple(bank(2 + m)[:, t], a1(m, k, t), x_hi[:, k], x_lo[:, k],
                                              t == 0 and k == 0, t == ET - 1 and k == KT - 1)
                        last.then_inc(S["low"], 1)

                def turn_route(n):
                    pe.wait_ge(S["route"], n + 1)
                    for b in range(TT):
                        last = nc.tensor.transpose(ps[0:32, 1, b * TR:(b + 1) * TR], route[:, b],
                                                   eye32[0:TR, 0:TR])
                    last.then_inc(S["rt"], 1)

                def expand(n):
                    pe.wait_ge(S["rlo"], n + 1)
                    for m, b in enumerate((0, 1, 4, 5)):
                        for t in range(2):
                            o = bank(b)[:, t]
                            s = select[:, 2 * m + t]
                            if m < 3:
                                last = mm(o, s, route_hi[:], start=t == 0, stop=t == 1)
                            else:
                                mm(o, s, route_hi[:], start=t == 0, stop=False)
                                last = mm(o, s, route_lo[:], start=False, stop=t == 1)
                        last.then_inc(S["expand"], 1)

                def turn_out(n):
                    for u in range(TT):
                        pe.wait_ge(S["ot"], at(n, 2, 1))
                        for k in range(KT):
                            last = nc.tensor.transpose(ps[0:TR, DOWN + u, k * P:(k + 1) * P],
                                                       o_t[:, k, u * TR:(u + 1) * TR], eye32[:])
                        last.then_inc(S["turned"], 1)

                def prologue():
                    pe.wait_ge(S["const"], 48)
                    turn_rows(0)
                    logit(0)
                    low_rank(0)
                    turn_route(0)
                    expand(0)

                def body(n, first, nxt):
                    pe.wait_ge(S["exp_act"], at(n, 2, 0))
                    base(n, 0, first)
                    if not first:
                        turn_out(n - 1)
                    for p in range(PAIRS):
                        if p + 1 < PAIRS:
                            base(n, p + 1, first)
                        delta(n, p)
                        down_low(n, p, 0)
                        if p:
                            down_low(n, p - 1, 1)
                    if nxt:
                        pe.wait_ge(S["y"], at(n, 2 * PAIRS, turn(1, PAIRS - 2)))
                        turn_rows(n + 1)
                    if first:
                        pe.wait_ge(S["wlo"], len(CHUNKS))
                    if not first:
                        pe.wait_ge(S["added"], at(n - 1, 2, 1))
                    pe.wait_ge(S["slo"], at(n, PAIRS, PAIRS - 2))
                    down(0, range(0, FT - 2))
                    down(1, range(0, FT - 2))
                    pe.wait_ge(S["ylo"], at(n, 2 * PAIRS, turn(1, PAIRS - 1)))
                    down_low(n, PAIRS - 1, 1)
                    pe.wait_ge(S["slo"], at(n, PAIRS, PAIRS - 1))
                    if nxt:
                        logit(n + 1)
                        low_rank(n + 1)
                    down(0, range(FT - 2, FT))
                    down(1, range(FT - 2, FT))
                    down(2, range(0, FT // 2))
                    if nxt:
                        turn_route(n + 1)
                    down(2, range(FT // 2, FT))
                    if nxt:
                        expand(n + 1)
                    down(3, range(0, FT))
                    pe.wait_ge(S["mlo"], n + 1)
                    for h in range(KT):
                        for t in range(ET):
                            last = triple(bank(DOWN + h // 2)[:, h % 2], B2_AT + t * D + h * P, m_hi[:, t], m_lo[:, t],
                                          False, h % 2 == 1 and t == ET - 1)
                        if h % 2:
                            last.then_inc(S["down"], 1)

                run_blocks(pe, prologue, body, lambda: turn_out(BLOCKS - 1))


def build(nc, spectra, kry_b, readout, log_dt, cls_rows, eye32, eye16, two_eye, half_eye, ones16, ones32,
          w_attn, b_attn, eye_bf, causal, own_head,
          w_ffn, iota, select, out):
    tokens = nc.dram_tensor("tokens", (64, 65, 512), F32, kind="Internal").ap()
    mixed = nc.dram_tensor("mixed", (64, 65, 512), F32, kind="Internal").ap()
    READY = 2080 + 4 * 3584
    with nc.sbuf_tensor("arena", [P, READY], F32) as arena_t:
        arena = arena_t[:]
        ffn_pair = (arena[:, 0:READY // 2].bitcast(F16), arena[:, READY // 2:READY].bitcast(F16))
        with nc.sbuf_tensor("attn_hi", [P, 4, 4, 512], F16) as hi, nc.sbuf_tensor("attn_lo", [P, 4, 4, 512], F16) as lo:
            attn_pair = (hi[:], lo[:])
            tokenizer_phase(nc, arena, w_attn, attn_pair, spectra, kry_b, readout, log_dt, cls_rows,
                            (eye32, eye16, two_eye, half_eye, ones16, ones32), tokens)
            attention_phase(nc, attn_pair, w_ffn, ffn_pair, b_attn, (eye32, eye_bf, causal, own_head), tokens, mixed)
        expert_phase(nc, w_ffn, ffn_pair, (eye32, iota, select), mixed.rearrange("b s d -> (b s) d"),
                     out.rearrange("b s d -> (b s) d"))


def kernel(**inputs):
    import ml_dtypes
    import numpy as np
    import concourse.bacc as bacc
    from concourse.bass_utils import run_bass_kernel_spmd as run
    a = {k: np.asarray(v) for k, v in inputs.items()}
    A = a["L0_tok_A"]
    re, im = A[..., 0].transpose(2, 0, 1), A[..., 1].transpose(2, 0, 1)
    at = [a["L0_attn_W" + n] for n in "qkvo"]
    ab = [a["L0_attn_b" + n] for n in "qkvo"]
    mask = np.where(np.arange(65)[None, :] > np.arange(65)[:, None], -1e30, 0.0).astype(ml_dtypes.bfloat16)

    def tiles(w):
        return w.reshape(-1, 128, w.shape[1]).transpose(1, 0, 2)

    f = {n: a["L0_ffn_" + n] for n in ("Wg", "W1", "W2", "W3", "A1", "A2", "A3", "B1", "B2", "B3")}
    low = {n: tiles(f[n].reshape(256, -1).T) for n in ("A1", "A2", "A3")}
    high = {n: tiles(f[n].transpose(0, 2, 1).reshape(256, -1)) for n in ("B1", "B2", "B3")}
    up = {n: tiles(f[n].T) for n in ("W1", "W2", "W3", "Wg")}
    cols = [low["A1"], low["A3"], up["Wg"]]
    for p in range(7):
        part = slice(256 * p, 256 * p + 256)
        cols += [up["W1"][:, :, part], up["W3"][:, :, part], high["B1"][:, :, part], high["B3"][:, :, part],
                 low["A2"][:, 2 * p:2 * p + 2]]
    cols += [up["W2"], high["B2"]]
    select = np.zeros((32, 8, 128), np.float16)
    for t in range(2):
        for p in range(128):
            e = 4 * t + p // 32
            select[e, t, p] = 1
            select[8 + e, 2 + t, p] = 1
            select[8 + e, 4 + t, p] = 1
            select[e, 4 + t, p] = -1
            select[16 + t, 6 + t, p] = 1
    arrays = {
        "spectra": np.concatenate([np.concatenate([re, im], 2), np.concatenate([im, re], 2)], 0),
        "kry_b": a["L0_tok_B"].transpose(2, 1, 0).reshape(128, 64),
        "readout": a["x"].transpose(3, 2, 1, 0).reshape(128, 64, 64),
        "log_dt": np.broadcast_to(a["L0_tok_log_dt"].reshape(1, 64), (128, 64)),
        "cls_rows": np.broadcast_to(a["cls_tok"].reshape(1, 512), (64, 512)),
        "eye32": np.eye(128, dtype=np.float32),
        "eye16": np.eye(128, dtype=np.float16),
        "two_eye": np.tile(2 * np.eye(128, dtype=np.float16), (1, 4)),
        "half_eye": np.tile(-0.5 * np.eye(128, dtype=np.float16), (1, 4)),
        "ones16": np.ones((128, 128), np.float16),
        "ones32": np.ones((128, 128), np.float32),
        "w_attn": np.stack([w.T.reshape(4, 128, 512).transpose(1, 0, 2) for w in at]),
        "b_attn": np.stack([b.reshape(4, 128).T for b in ab], 1),
        "eye_bf": np.eye(65).astype(ml_dtypes.bfloat16),
        "causal": np.tile(mask, (1, 4)),
        "own_head": np.kron(np.eye(4, dtype=np.float32), np.ones((32, 1), np.float32)),
        "w_ffn": np.concatenate([c.reshape(128, -1) for c in cols], 1),
        "iota": np.broadcast_to(np.arange(8, dtype=np.float32), (104, 2, 8)),
        "select": select,
    }
    nc = bacc.Bacc("TRN2", target_bir_lowering=False, num_devices=1)
    feeds, aps = {}, []
    for name, v in arrays.items():
        v = np.ascontiguousarray(v)
        feeds["in_" + name] = v
        aps.append(nc.dram_tensor("in_" + name, v.shape, mybir.dt.from_np(v.dtype), kind="ExternalInput").ap())
    aps.append(nc.dram_tensor("out", (64, 65, 512), F32, kind="ExternalOutput").ap())
    build(nc, *aps)
    return run(nc, [feeds], core_ids=[0]).results[0]["out"]
```
